# Optimizing a Trainium2 kernel written in Bass

```python
import numpy as np
import jax
import jax.numpy as jnp

def _softmax(x, axis=-1):
    return jax.nn.softmax(x, axis=axis)

def _gelu(x):
    return jax.nn.gelu(x, approximate=True)

def _silu(x):
    return jax.nn.silu(x)

def _sigmoid(x):
    return jax.nn.sigmoid(x)

def _layernorm(x, axis=-1, eps=1e-05):
    m = jnp.mean(x, axis=axis, keepdims=True)
    v = jnp.var(x, axis=axis, keepdims=True)
    return (x - m) / jnp.sqrt(v + eps)

def _scatter_add(tgt, idx, src, axis=0):
    return tgt.at[idx].add(src)

def _segment_sum(src, seg, n):
    return jax.ops.segment_sum(src, seg, n)
kernel_name = 'mk_sandwich_d1_jaxref_r4_b49a8e'

def setup_inputs(seed: int=0):
    np.random.seed(seed)
    _w = jnp.asarray

    def _L0_attn_setup():
        import jax, jax.numpy as jnp
        import numpy as np
        DIM = 256
        STATE = 64
        HEADS = 8
        EXPAND = 2
        INNER = DIM * EXPAND
        HEAD_DIM = INNER // HEADS
        KERNEL = 4
        B, L = (2, 512)
        EPS = 1e-05

        def _causal_conv(x, conv_w, conv_b):
            x_pad = jnp.pad(x, ((0, 0), (KERNEL - 1, 0), (0, 0)))
            w = conv_w[:, 0, :]
            y = sum((x_pad[:, k:k + x.shape[1], :] * w[:, k] for k in range(KERNEL)))
            return y + conv_b

        def _ssd_scan(x, b, c, dt, a):
            state0 = jnp.zeros((x.shape[0], HEADS, STATE, HEAD_DIM), x.dtype)

            def step(state, inp):
                x_t, b_t, c_t, dt_t = inp
                decay = jnp.exp(dt_t * a)[..., None, None]
                b_bar = dt_t[..., None] * b_t
                state = decay * state + b_bar[..., None] * x_t[:, :, None, :]
                y_t = jnp.einsum('bhn,bhnp->bhp', c_t, state)
                return (state, y_t)
            xs = (x.transpose(1, 0, 2, 3), b.transpose(1, 0, 2, 3), c.transpose(1, 0, 2, 3), dt.transpose(1, 0, 2))
            _, ys = jax.lax.scan(step, state0, xs)
            return ys.transpose(1, 0, 2, 3)
        key = jax.random.key(seed)
        ks = jax.random.split(key, 12)
        s = 0.02
        return {'input_tensor': jax.random.normal(ks[0], (B, L, DIM), jnp.float32), 'Wx': jax.random.normal(ks[1], (INNER, DIM), jnp.float32) * s, 'Wz': jax.random.normal(ks[2], (INNER, DIM), jnp.float32) * s, 'conv_w': jax.random.normal(ks[3], (INNER, 1, KERNEL), jnp.float32) * s, 'conv_b': jnp.zeros((INNER,), jnp.float32), 'Wb': jax.random.normal(ks[4], (HEADS * STATE, INNER), jnp.float32) * s, 'Wc': jax.random.normal(ks[5], (HEADS * STATE, INNER), jnp.float32) * s, 'Wdt': jax.random.normal(ks[6], (HEADS, INNER), jnp.float32) * s, 'b_dt': jnp.zeros((HEADS,), jnp.float32), 'log_a': jnp.log(jnp.full((HEADS,), 0.5, jnp.float32)), 'd_param': jnp.ones((HEADS,), jnp.float32), 'gn_w': jnp.ones((INNER,), jnp.float32), 'gn_b': jnp.zeros((INNER,), jnp.float32), 'Wout': jax.random.normal(ks[7], (DIM, INNER), jnp.float32) * s}
    _L0_attn_in = _L0_attn_setup()

    def _L0_ffn_setup():
        import jax, jax.numpy as jnp
        import numpy as np

        def _binarize(w):
            alpha = jax.lax.stop_gradient(jnp.mean(jnp.abs(w), axis=1, keepdims=True))
            bw = alpha * jnp.sign(w)
            return w + jax.lax.stop_gradient(bw - w)
        key = jax.random.key(seed)
        k1, k2, k3, k4, k5 = jax.random.split(key, 5)
        D, H = (256, 1024)
        x = jax.random.normal(k1, (64, 196, D), dtype=jnp.float32)
        w1 = jax.random.normal(k2, (H, D), dtype=jnp.float32) * 0.02
        b1 = jax.random.normal(k3, (H,), dtype=jnp.float32) * 0.02
        w2 = jax.random.normal(k4, (D, H), dtype=jnp.float32) * 0.02
        b2 = jax.random.normal(k5, (D,), dtype=jnp.float32) * 0.02
        return {'x': x, 'w1': w1, 'b1': b1, 'w2': w2, 'b2': b2}
    _L0_ffn_in = _L0_ffn_setup()
    _d = {'L0_attn_input_tensor': _L0_attn_in['input_tensor'], 'L0_attn_Wx': _L0_attn_in['Wx'], 'L0_attn_Wz': _L0_attn_in['Wz'], 'L0_attn_conv_w': _L0_attn_in['conv_w'], 'L0_attn_conv_b': _L0_attn_in['conv_b'], 'L0_attn_Wb': _L0_attn_in['Wb'], 'L0_attn_Wc': _L0_attn_in['Wc'], 'L0_attn_Wdt': _L0_attn_in['Wdt'], 'L0_attn_b_dt': _L0_attn_in['b_dt'], 'L0_attn_log_a': _L0_attn_in['log_a'], 'L0_attn_d_param': _L0_attn_in['d_param'], 'L0_attn_gn_w': _L0_attn_in['gn_w'], 'L0_attn_gn_b': _L0_attn_in['gn_b'], 'L0_attn_Wout': _L0_attn_in['Wout'], 'L0_ffn_w1': _L0_ffn_in['w1'], 'L0_ffn_b1': _L0_ffn_in['b1'], 'L0_ffn_w2': _L0_ffn_in['w2'], 'L0_ffn_b2': _L0_ffn_in['b2']}
    _x0 = _d['L0_attn_input_tensor']
    _d['L0_attn_input_tensor'] = jax.random.normal(jax.random.fold_in(jax.random.key(seed), 1), (8, 1024, 256), dtype=_x0.dtype)
    del _x0
    return _d

def reference(L0_attn_input_tensor, L0_attn_Wx, L0_attn_Wz, L0_attn_conv_w, L0_attn_conv_b, L0_attn_Wb, L0_attn_Wc, L0_attn_Wdt, L0_attn_b_dt, L0_attn_log_a, L0_attn_d_param, L0_attn_gn_w, L0_attn_gn_b, L0_attn_Wout, L0_ffn_w1, L0_ffn_b1, L0_ffn_w2, L0_ffn_b2):

    def _L0_attn_ref(input_tensor, Wx, Wz, conv_w, conv_b, Wb, Wc, Wdt, b_dt, log_a, d_param, gn_w, gn_b, Wout):
        import jax, jax.numpy as jnp
        import numpy as np
        DIM = 256
        STATE = 64
        HEADS = 8
        EXPAND = 2
        INNER = DIM * EXPAND
        HEAD_DIM = INNER // HEADS
        KERNEL = 4
        B, L = (2, 512)
        EPS = 1e-05

        def _causal_conv(x, conv_w, conv_b):
            x_pad = jnp.pad(x, ((0, 0), (KERNEL - 1, 0), (0, 0)))
            w = conv_w[:, 0, :]
            y = sum((x_pad[:, k:k + x.shape[1], :] * w[:, k] for k in range(KERNEL)))
            return y + conv_b

        def _ssd_scan(x, b, c, dt, a):
            state0 = jnp.zeros((x.shape[0], HEADS, STATE, HEAD_DIM), x.dtype)

            def step(state, inp):
                x_t, b_t, c_t, dt_t = inp
                decay = jnp.exp(dt_t * a)[..., None, None]
                b_bar = dt_t[..., None] * b_t
                state = decay * state + b_bar[..., None] * x_t[:, :, None, :]
                y_t = jnp.einsum('bhn,bhnp->bhp', c_t, state)
                return (state, y_t)
            xs = (x.transpose(1, 0, 2, 3), b.transpose(1, 0, 2, 3), c.transpose(1, 0, 2, 3), dt.transpose(1, 0, 2))
            _, ys = jax.lax.scan(step, state0, xs)
            return ys.transpose(1, 0, 2, 3)
        bsz, seq, _ = input_tensor.shape
        x = input_tensor @ Wx.T
        z = input_tensor @ Wz.T
        x = _causal_conv(x, conv_w, conv_b)
        x = jax.nn.silu(x)
        b = (x @ Wb.T).reshape(bsz, seq, HEADS, STATE)
        c = (x @ Wc.T).reshape(bsz, seq, HEADS, STATE)
        dt = jax.nn.softplus(x @ Wdt.T + b_dt)
        xh = x.reshape(bsz, seq, HEADS, HEAD_DIM)
        a = -jnp.exp(log_a)
        y = _ssd_scan(xh, b, c, dt, a)
        y = y + d_param[None, None, :, None] * xh
        yg = y
        mean = yg.mean(axis=(1, 3), keepdims=True)
        var = yg.var(axis=(1, 3), keepdims=True)
        yn = (yg - mean) / jnp.sqrt(var + EPS)
        yn = yn * gn_w.reshape(1, 1, HEADS, HEAD_DIM) + gn_b.reshape(1, 1, HEADS, HEAD_DIM)
        yn = yn.reshape(bsz, seq, INNER)
        out = yn * jax.nn.silu(z)
        return out @ Wout.T

    def _L0_ffn_ref(x, w1, b1, w2, b2):
        import jax, jax.numpy as jnp
        import numpy as np

        def _binarize(w):
            alpha = jax.lax.stop_gradient(jnp.mean(jnp.abs(w), axis=1, keepdims=True))
            bw = alpha * jnp.sign(w)
            return w + jax.lax.stop_gradient(bw - w)
        bw1 = _binarize(w1)
        h = jnp.einsum('bsd,hd->bsh', x, bw1) + b1
        h = jax.nn.gelu(h, approximate=False)
        bw2 = _binarize(w2)
        out = jnp.einsum('bsh,dh->bsd', h, bw2) + b2
        return out
    x = L0_attn_input_tensor
    x = x + _layernorm(_L0_attn_ref(_layernorm(x, axis=-1), L0_attn_Wx, L0_attn_Wz, L0_attn_conv_w, L0_attn_conv_b, L0_attn_Wb, L0_attn_Wc, L0_attn_Wdt, L0_attn_b_dt, L0_attn_log_a, L0_attn_d_param, L0_attn_gn_w, L0_attn_gn_b, L0_attn_Wout), axis=-1)
    x = x + _layernorm(_L0_ffn_ref(_layernorm(x, axis=-1), L0_ffn_w1, L0_ffn_b1, L0_ffn_w2, L0_ffn_b2), axis=-1)
    return x

_drawn_inputs = setup_inputs


def setup_inputs(seed=0):
    import zlib

    import numpy as np

    out = dict(_drawn_inputs(seed))
    spreads = {'L0_attn_conv_b': (0.0, 0.1),
     'L0_attn_b_dt': (0.0, 0.8),
     'L0_attn_log_a': (-0.6931471824645996, 0.6),
     'L0_attn_d_param': (1.0, 0.6),
     'L0_attn_gn_w': (1.0, 0.2),
     'L0_attn_gn_b': (0.0, 0.1)}
    factors = {'L0_attn_Wb': 8.0, 'L0_attn_Wc': 8.0, 'L0_attn_Wdt': 64.0}
    for name, (base, spread) in spreads.items():
        noise = np.random.default_rng([zlib.crc32(name.encode()), seed]).standard_normal(out[name].shape)
        drawn = base * np.exp(spread * noise) if base else spread * noise
        out[name] = jnp.asarray(drawn.astype(out[name].dtype))
    for name, factor in factors.items():
        out[name] = (out[name] * factor).astype(out[name].dtype)
    return out
```

```python
from contextlib import ExitStack

import concourse.bass as bass
from concourse import mybir

F32 = mybir.dt.float32
F16 = mybir.dt.float16
ALU = mybir.AluOpType
ACT = mybir.ActivationFunctionType
AX_X = mybir.AxisListType.X

P = 128
NB, T, D = 8, 1024, 256
INNER, HEADS, HD, NS = 512, 8, 64, 64
TAPS = 4
FF = 1024
EPS = 1e-5

BLK = 512
NJ = T // BLK
NQ = BLK // P
KD = D // P
KI = INNER // P
HP = P // HD
KF = FF // P
HALO = TAPS - 1

SW = 256.0
SX = 256.0
SG = 64.0
MASKED = -30000.0
DECAY_FLOOR = -10000.0


class Signal:

    def __init__(self, sem, each, once=0, step=1):
        self.sem, self.each, self.once, self.step = sem, each, once, step

    def count(self, b, n):
        return self.sem, b * (self.each * self.step) + (self.once + self.each + n) * self.step

    def prime(self, eng):
        eng.sem_inc(self.sem, self.each * self.step)


class Banks:

    N = 8

    def __init__(self, sem, before, turn):
        self.before, self.turn = before, turn
        self.place = {}
        self.once, self.each = [0] * self.N, [0] * self.N
        for keys, counts in ((before, self.once), (turn, self.each)):
            for n, key in enumerate(keys):
                self.place[key] = n % self.N, counts[n % self.N]
                counts[n % self.N] += 1
        self.full_sems = [sem(f"bank_full{k}") for k in range(self.N)]
        self.read = {}

    def index(self, key):
        return self.place[key][0]

    def full_sem(self, key):
        return self.full_sems[self.index(key)]

    def full(self, b, key, turns_ago=0):
        k, m = self.place[key]
        if b is None:
            return self.full_sems[k], m + 1
        return self.full_sems[k], b * self.each[k] + (self.once[k] + self.each[k] * (1 - turns_ago) + m + 1)

    def empty(self, b, key):
        k, m = self.place[key]
        if b is None:
            signal, n = self.read[[x for x in self.before if self.place[x] == (k, m - 1)][0]]
            return signal, n
        of = [x for x in self.turn if self.place[x] == (k, (m - 1) % self.each[k])][0]
        signal, n = self.read[of]
        return signal.count(b, n - signal.each if m == 0 else n)

    def prime(self, pe):
        for k in range(self.N):
            pe.sem_inc(self.full_sems[k], self.each[k])


def scan_steps():
    steps = []
    for q in range(NQ + 2):
        if q < NQ:
            steps.append(("front", q))
        if 1 <= q <= NQ:
            steps.append(("back", q - 1))
        if q >= 2:
            steps.append(("turn", q - 2))
    return steps


def mamba_sandwich_kernel(nc, x, Wx, Wz, conv_w, conv_b, Wb, Wc, Wdt, b_dt, log_a, d_param, gn_w, gn_b,
                          Wout, w1, b1, w2, b2, out):
    ctx = ExitStack()
    with ctx:
        def sb(name, shape, dt=F32):
            return ctx.enter_context(nc.sbuf_tensor(name, shape, dt))

        def sem(name):
            return ctx.enter_context(nc.semaphore(name))

        ident = sb("ident", [P, P])
        ident_h = sb("ident_h", [P, P], F16)
        upto = sb("upto", [P, P])
        upto_h = sb("upto_h", [P, P], F16)
        after = sb("after", [P, P])
        after_h = sb("after_h", [P, P], F16)
        ones = sb("ones", [P, P])
        future_h = sb("future_h", [P, P], F16)
        head_mean = sb("head_mean", [P, P])
        power = sb("power", [P, 4])

        WxT = [sb(f"WxT{i}", [P, KD, INNER], F16) for i in range(2)]
        WzT = [sb(f"WzT{i}", [P, KD, INNER], F16) for i in range(2)]
        WbT = [sb(f"WbT{i}", [P, KI, HEADS * NS], F16) for i in range(2)]
        WcT = [sb(f"WcT{i}", [P, KI, HEADS * NS], F16) for i in range(2)]
        WdtT = [sb(f"WdtT{i}", [P, KI, HEADS], F16) for i in range(2)]
        WoutT = sb("WoutT", [P, KI, D])
        sign1T = sb("sign1T", [P, KD, FF], F16)
        sign2T = sb("sign2T", [P, KF, D], F16)
        alpha1 = sb("alpha1", [P, KF])
        alpha2 = sb("alpha2", [P, KD])
        alpha2_row = sb("alpha2_row", [P, D])
        b1_col = sb("b1_col", [P, KF])
        b2_row = sb("b2_row", [P, D])
        taps = sb("taps", [P, KI, TAPS])
        last_tap = sb("last_tap", [P, KI])
        conv_bias = sb("conv_bias", [P, KI])
        gnw = sb("gnw", [P, KI])
        gnb = sb("gnb", [P, KI])
        skip = sb("skip", [P, KI])
        bdt_row = sb("bdt_row", [P, HEADS])
        a_row = sb("a_row", [P, HEADS])
        Wdt_in = sb("Wdt_in", [HEADS, INNER])

        xt = [sb(f"xt{j}", [P, NQ, D]) for j in range(NJ)]
        xn = sb("xn", [P, NQ, D])
        xh = [sb(f"xh{i}", [P, KD, BLK], F16) for i in range(2)]
        xi = [sb(f"xi{j}", [P, KI, HALO + BLK]) for j in range(NJ)]
        xs = sb("xs", [P, KI, BLK])
        sh = [sb(f"sh{i}", [P, KI, BLK], F16) for i in range(2)]
        zs = sb("zs", [P, KI, T])
        yT = sb("yT", [P, KI, T])
        BT = sb("BT", [P, KI, BLK])
        CT = sb("CT", [P, KI, BLK])

        def small(name, dt=F32):
            return sb(name, [P, NQ, HEADS], dt)
        v_dt, abs_v, exp_v, one_e, e_back, e_rest, log_u = (small(n) for n in (
            "v_dt", "abs_v", "exp_v", "one_e", "e_back", "e_rest", "log_u"))
        dt_raw = small("dt_raw")
        dt_t = small("dt_t")
        da_raw = small("da_raw")
        da = small("da")
        da_hi, da_lo = small("da_hi", F16), small("da_lo", F16)
        decays = sb("decays", [P, 3, NQ, HEADS])

        seg = [[sb(f"seg{i}{r}", [P, HP, KI, P], F16) for r in range(2)] for i in range(2)]
        mt = [sb(f"mt{r}", [P, HP, KI, P]) for r in range(2)]
        xdt = [sb(f"xdt{r}", [P, HEADS, HD]) for r in range(2)]
        bw = [sb(f"bw{r}", [P, HEADS, NS]) for r in range(2)]
        yk = [sb(f"yk{r}", [P, HEADS, HD]) for r in range(2)]
        state = sb("state", [P, KI, P])

        stats = sb("stats", [P, NQ, 6])
        moments = sb("moments", [P, NQ, 2])
        var_eps = sb("var_eps", [P, NQ])
        rstd = sb("rstd", [P, NQ])
        gn_stats = sb("gn_stats", [P, KI, NJ, 6])
        gn_mom = sb("gn_mom", [P, KI, 2])
        gn_sq = sb("gn_sq", [P, KI])
        gn_head = sb("gn_head", [P, KI, 2])
        gn_msq = sb("gn_msq", [P, KI])
        gn_var = sb("gn_var", [P, KI])
        gn_rstd = sb("gn_rstd", [P, KI])
        gn_scale = sb("gn_scale", [P, KI])
        gn_ms = sb("gn_ms", [P, KI])
        gn_shift = sb("gn_shift", [P, KI])

        u = [sb(f"u{j}", [P, NQ, D]) for j in range(NJ)]
        un = xn
        hf = [sb(f"hf{r}", [P, BLK]) for r in range(2)]
        hh = [sb(f"hh{i}", [P, KF, BLK], F16) for i in range(2)]
        y2 = sb("y2", [P, NQ, D])

        Wb_in, Wc_in = zs[:, :, 0:INNER], zs[:, :, INNER:2 * INNER]
        w1_in = yT[:, 0:2, :].rearrange("p a (b d) -> p (a b) d", d=D)
        w2_in = yT[:, 2:4, :]
        Wx_in = BT[:, :, :].rearrange("p a n -> p (a n)")[:, 0:KI * D].rearrange("p (a d) -> p a d", d=D)
        Wz_in = BT[:, :, :].rearrange("p a n -> p (a n)")[:, KI * D:2 * KI * D].rearrange("p (a d) -> p a d", d=D)
        Wout_in = CT[:, 0:2, :]
        alpha2_wide = [CT[:, 2, k * P:(k + 1) * P] for k in range(KD)]

        before = [("Wx", k) for k in range(KD)] + [("Wz", k) for k in range(KD)]
        before += [("Wb", k) for k in range(KI)] + [("Wc", k) for k in range(KI)] + [("Wdt", 0)]
        before += [("Wout", k) for k in range(KI // 2)]
        before += [("w1", k, m) for k in range(KD) for m in range(2)] + [("w2", f) for f in range(KF // 2)]
        before += [("alpha2", 0)]
        turn = []
        for j in range(NJ):
            turn += [("xT", j, k) for k in range(KD)] + [("xi", j, c) for c in range(KI)]
            turn += [("z", j, c) for c in range(KI)] + [("dt", j)]
            turn += [("B", j, c) for c in range(KI)] + [("C", j, c) for c in range(KI)] + [("sums", j)]
            for kind, q in scan_steps():
                if kind == "front":
                    turn += [("seg", j, q, g) for g in range(HP)] + [("X", j, q), ("Bt", j, q)]
                    turn += [("S", j, q, g) for g in range(HP)]
                elif kind == "back":
                    turn += [("YI", j, q), ("St", j, q), ("Y", j, q)]
                else:
                    turn += [("YT", j, q)]
        turn += [("gn",)]
        turn += [("Wo", j, m) for j in range(NJ) for m in range(NQ // 2)]
        turn += [("uT", 0, k) for k in range(KD)] + [("H", 0, f) for f in range(KF)]
        turn += [("uT", 1, k) for k in range(KD)] + [("O", 0, m) for m in range(NQ // 2)]
        turn += [("H", 1, f) for f in range(KF)] + [("O", 1, m) for m in range(NQ // 2)]
        banks = Banks(sem, before, turn)
        psum = [ctx.enter_context(nc.psum_tensor(f"bank{k}", [P, 512], F32)) for k in range(Banks.N)]

        def bank(*key):
            return psum[banks.index(key)]

        LNS = [("in", 0), ("in", 1), ("mid", 0), ("ff", 0), ("mid", 1), ("ff", 1), ("end", 0), ("end", 1)]
        NLN = len(LNS)
        masks_zero = sem("masks_zero")
        masks_made = sem("masks_made")
        loaded = sem("loaded")
        w_split = sem("w_split")
        act_set = sem("act_set")
        dve_set = sem("dve_set")
        low_set = sem("low_set")
        wide_set = sem("wide_set")
        a_exp = sem("a_exp")
        stats_seen = sem("stats_seen")
        x_in = [Signal(sem(f"x_in{j}"), 1, step=16) for j in range(NJ)]
        stored = [Signal(sem(f"stored{j}"), 1, step=16) for j in range(NJ)]
        ln_stats = Signal(sem("ln_stats"), NLN * NQ)
        ln_moments = Signal(sem("ln_moments"), NLN * NQ)
        ln_eps = Signal(sem("ln_eps"), NLN)
        ln_rstd = Signal(sem("ln_rstd"), NLN)
        xn_made = Signal(sem("xn_made"), NJ * NQ)
        xh_hi = Signal(sem("xh_hi"), NJ * KD)
        xh_lo = Signal(sem("xh_lo"), NJ * KD)
        xi_out = Signal(sem("xi_out"), NJ * KI)
        halo = Signal(sem("halo"), 1)
        tap_out = Signal(sem("tap_out"), NJ * KI * TAPS)
        taps_in = Signal(sem("taps_in"), NJ * KI)
        conv_out = Signal(sem("conv_out"), NJ * KI * (TAPS - 1))
        xs_out = Signal(sem("xs_out"), NJ * KI)
        zs_out = Signal(sem("zs_out"), NJ * KI)
        sh_hi = Signal(sem("sh_hi"), NJ * KI)
        sh_lo = Signal(sem("sh_lo"), NJ * KI)
        B_out = Signal(sem("B_out"), NJ * KI)
        C_out = Signal(sem("C_out"), NJ * KI)
        dt_step = Signal(sem("dt_step"), NJ * 10)
        dt_act = Signal(sem("dt_act"), NJ * 2)
        da_seen = Signal(sem("da_seen"), NJ)
        decays_out = Signal(sem("decays_out"), NJ)
        NCH = NJ * NQ
        seg_hi = Signal(sem("seg_hi"), NCH)
        seg_lo = Signal(sem("seg_lo"), NCH)
        seg_exp = Signal(sem("seg_exp"), NCH * HP)
        mt_out = Signal(sem("mt_out"), NCH * HP)
        xdt_out = Signal(sem("xdt_out"), NCH)
        bw_out = Signal(sem("bw_out"), NCH)
        yk_part = Signal(sem("yk_part"), NCH)
        yk_out = Signal(sem("yk_out"), NCH)
        st_zero = Signal(sem("st_zero"), 1)
        st_scaled = Signal(sem("st_scaled"), NCH)
        st_out = Signal(sem("st_out"), NCH * HP)
        yT_out = Signal(sem("yT_out"), NCH * KI)
        gn_st = Signal(sem("gn_st"), NJ * KI)
        gn_mo = Signal(sem("gn_mo"), KI)
        gn_step = Signal(sem("gn_step"), 8)
        gn_rs = Signal(sem("gn_rs"), 1)
        yn_out = Signal(sem("yn_out"), NJ * KI)
        g_out = Signal(sem("g_out"), NJ * KI)
        mid_out = Signal(sem("mid_out"), NJ * NQ)
        u_out = Signal(sem("u_out"), NJ * NQ)
        un_out = Signal(sem("un_out"), NJ * NQ)
        hf_out = Signal(sem("hf_out"), NJ * KF)
        hh_hi = Signal(sem("hh_hi"), NJ * KF)
        hh_lo = Signal(sem("hh_lo"), NJ * KF)
        y2_scaled = Signal(sem("y2_scaled"), NJ * NQ // 2)
        y2_out = Signal(sem("y2_out"), NJ * NQ // 2)
        y2_norm = Signal(sem("y2_norm"), NJ * NQ)
        o_out = Signal(sem("o_out"), NJ * NQ)
        uh_hi = Signal(sem("uh_hi"), NJ * KD)
        uh_lo = Signal(sem("uh_lo"), NJ * KD)
        uh = xh

        x_v = x.rearrange("b (j q p) d -> b j p q d", j=NJ, p=P)
        out_v = out.rearrange("b (j q p) d -> b j p q d", j=NJ, p=P)
        NLOADS = 16 + HP
        DVE_SETUP, ACT_SETUP = 6, KI // 2 + 2 * KD + KF // 2

        def ch(j, q):
            return j * NQ + q

        lows = [("Wx", k) for k in range(KD)] + [("Wz", k) for k in range(KD)]
        lows += [("Wb", k) for k in range(KI)] + [("Wc", k) for k in range(KI)] + [("Wdt", 0)]
        banks.read.update({key: (low_set, n + 1) for n, key in enumerate(lows)})
        banks.read.update({key: (act_set, n + 1) for n, key in enumerate(before[len(lows):-1])})
        banks.read[("gn",)] = gn_step, 3
        for j in range(NJ):
            for k in range(KD):
                banks.read[("xT", j, k)] = xh_lo, j * KD + k + 1
                banks.read[("uT", j, k)] = uh_lo, j * KD + k + 1
            for c in range(KI):
                for name, signal in (("xi", taps_in), ("z", zs_out), ("B", B_out), ("C", C_out)):
                    banks.read[(name, j, c)] = signal, j * KI + c + 1
            banks.read[("dt", j)] = dt_step, j * 10 + 1
            banks.read[("sums", j)] = decays_out, j + 1
            for q in range(NQ):
                n = ch(j, q)
                for name, signal in (("X", xdt_out), ("Bt", bw_out), ("YI", yk_part), ("Y", yk_out)):
                    banks.read[(name, j, q)] = signal, n + 1
                banks.read[("St", j, q)] = st_out, (n + 1) * HP
                banks.read[("YT", j, q)] = yT_out, (n + 1) * KI
                for g in range(HP):
                    banks.read[("seg", j, q, g)] = seg_exp, n * HP + g + 1
                    banks.read[("S", j, q, g)] = mt_out, n * HP + g + 1
            for f in range(KF):
                banks.read[("H", j, f)] = hf_out, j * KF + f + 1
            for m in range(NQ // 2):
                banks.read[("Wo", j, m)] = mid_out, j * NQ + 2 * m + 2
                banks.read[("O", j, m)] = y2_scaled, j * NQ // 2 + m + 1

        block = ctx.enter_context(nc.Block())

        @block.sync
        def _(sp):
            def load(dst, src):
                sp.dma_start(dst, src).then_inc(loaded, 16)

            with nc.allow_non_contiguous_dma(reason="vectors, once"):
                load(Wx_in, Wx.rearrange("(m p) d -> p m d", p=P))
                load(Wz_in, Wz.rearrange("(m p) d -> p m d", p=P))
                load(Wb_in, Wb.rearrange("(m p) d -> p m d", p=P))
                load(Wc_in, Wc.rearrange("(m p) d -> p m d", p=P))
                load(Wdt_in[:, :], Wdt)
                load(Wout_in, Wout.rearrange("(m p) d -> p m d", p=P))
                load(w1_in, w1.rearrange("(m p) d -> p m d", p=P))
                load(w2_in, w2.rearrange("(m p) d -> p m d", p=P))
                load(taps[:, :, :], conv_w.rearrange("(c p) o k -> p c (o k)", p=P))
                load(conv_bias[:, :], conv_b.rearrange("(c p) -> p c", p=P))
                load(gnw[:, :], gn_w.rearrange("(c p) -> p c", p=P))
                load(gnb[:, :], gn_b.rearrange("(c p) -> p c", p=P))
                load(b1_col[:, :], b1.rearrange("(c p) -> p c", p=P))
                load(b2_row[:, :], b2.partition_broadcast(P))
                load(bdt_row[:, :], b_dt.partition_broadcast(P))
                load(a_row[:, :], log_a.partition_broadcast(P))
                for g in range(HP):
                    load(skip[g * HD:(g + 1) * HD, :],
                         d_param.rearrange("(c g) -> g c", g=HP)[g].partition_broadcast(HD))
            for j in range(NJ):
                x_in[j].prime(sp)
                stored[j].prime(sp)
            with sp.Fori(0, NB) as b:
                for j in range(NJ):
                    sp.wait_ge(*u_out.count(b, (j + 1) * NQ - NJ * NQ))
                    sp.dma_start(xt[j][:, :, :], x_v[bass.ds(b, 1), j].rearrange("a p q d -> p (a q) d"))\
                        .then_inc(x_in[j].sem, 16)
                for j in range(NJ):
                    sp.wait_ge(*o_out.count(b, (j + 1) * NQ))
                    sp.dma_start(out_v[bass.ds(b, 1), j].rearrange("a p q d -> p (a q) d"), u[j][:, :, :])\
                        .then_inc(stored[j].sem, 16)
            for j in range(NJ):
                sp.wait_ge(*stored[j].count(NB - 1, 1))

        @block.gpsimd
        def _(pool):
            for n, (t, v) in enumerate(((ident, 0.0), (ident_h, 0.0), (upto, 1.0), (upto_h, 1.0), (after, 1.0),
                                        (after_h, 1.0), (future_h, 0.0), (ones, 1.0), (head_mean, 0.0),
                                        (power, -0.5))):
                pool.memset(t[:, :], v).then_inc(masks_zero, 1)
            pool.memset(xi[0][:, :, 0:HALO], 0.0).then_inc(masks_zero, 1)
            pool.wait_ge(masks_zero, 11)
            for g in range(HP):
                pool.memset(head_mean[g * HD:(g + 1) * HD, g * HD:(g + 1) * HD], 1.0 / HD).then_inc(masks_made, 1)
                pool.wait_ge(masks_made, g + 1)
            for t in (ident, ident_h):
                pool.affine_select(out=t[:, :], in_=t[:, :], compare_op=ALU.not_equal, fill=1.0, base=0,
                                   pattern=[[-1, P]], channel_multiplier=1).then_inc(masks_made, 1)
            for t in (upto, upto_h):
                pool.affine_select(out=t[:, :], in_=t[:, :], compare_op=ALU.is_ge, fill=0.0, base=0,
                                   pattern=[[1, P]], channel_multiplier=-1).then_inc(masks_made, 1)
            for t in (after, after_h):
                pool.affine_select(out=t[:, :], in_=t[:, :], compare_op=ALU.is_ge, fill=0.0, base=-1,
                                   pattern=[[-1, P]], channel_multiplier=1).then_inc(masks_made, 1)
            pool.affine_select(out=future_h[:, :], in_=future_h[:, :], compare_op=ALU.is_ge, fill=MASKED, base=0,
                               pattern=[[1, P]], channel_multiplier=-1).then_inc(masks_made, 1)
            pool.wait_ge(masks_made, 9)
            for s in (ln_rstd, seg_hi, seg_lo, gn_rs, u_out, o_out):
                s.prime(pool)

            def inverse_root(b, which):
                n = LNS.index(which)
                pool.wait_ge(*ln_eps.count(b, n + 1))
                pool.tensor_tensor(rstd[:, :], var_eps[:, :], power[:, 0:NQ], ALU.pow).then_inc(ln_rstd.sem, 1)

            def segments(b, j, q):
                n = ch(j, q)
                for i, (part, sig) in enumerate(((da_hi, seg_hi), (da_lo, seg_lo))):
                    pool.wait_ge(*banks.full(b, *last_seg(n)))
                    if q == 0:
                        pool.wait_ge(*dt_step.count(b, j * 10 + 9 + i))
                    pool.tensor_tensor(seg[i][n % 2][:, :, :, :],
                                       upto_h[:, None, None, :].to_broadcast([P, HP, KI, P]),
                                       part[:, q, :].rearrange("p (c g) -> p g c", g=HP)[:, :, :, None]
                                       .to_broadcast([P, HP, KI, P]), ALU.mult).then_inc(sig.sem, 1)

            def last_seg(n):
                m = (n - 2) % NCH
                return ("seg", m // NQ, m % NQ, HP - 1), int(n < 2)

            with pool.Fori(0, NB) as b:
                for j in range(NJ):
                    inverse_root(b, ("in", j))
                    for q in range(NQ):
                        segments(b, j, q)
                pool.wait_ge(*gn_step.count(b, 5))
                pool.tensor_tensor(gn_rstd[:, :], gn_var[:, :], power[:, 0:KI], ALU.pow).then_inc(gn_rs.sem, 1)

                def add_input(j):
                    for i in range(NQ):
                        pool.wait_ge(*mid_out.count(b, j * NQ + i + 1))
                        pool.tensor_tensor(u[j][:, i, :], u[j][:, i, :], xt[j][:, i, :], ALU.add)\
                            .then_inc(u_out.sem, 1)

                def add_middle(j):
                    for i in range(NQ):
                        pool.wait_ge(*y2_norm.count(b, j * NQ + i + 1))
                        pool.tensor_tensor(u[j][:, i, :], u[j][:, i, :], y2[:, i, :], ALU.add)\
                            .then_inc(o_out.sem, 1)

                for j in range(NJ):
                    inverse_root(b, ("mid", j))
                    add_input(j)
                    inverse_root(b, ("ff", j))
                for j in range(NJ):
                    inverse_root(b, ("end", j))
                    add_middle(j)

        @block.scalar
        def _(act):

            def high_half(dst, key):
                act.wait_ge(*banks.full(None, key))
                nc.scalar.activation(dst, psum[banks.index(key)][:, :], ACT.Copy, scale=SW).then_inc(w_split, 1)

            for k in range(KD):
                high_half(WxT[0][:, k, :], ("Wx", k))
            for k in range(KD):
                high_half(WzT[0][:, k, :], ("Wz", k))
            for k in range(KI):
                high_half(WbT[0][:, k, :], ("Wb", k))
            for k in range(KI):
                high_half(WcT[0][:, k, :], ("Wc", k))
            act.wait_ge(*banks.full(None, ("Wdt", 0)))
            nc.scalar.activation(WdtT[0][:, :, :], bank("Wdt", 0)[:, 0:KI * HEADS].rearrange("p (k h) -> p k h", k=KI),
                                 ACT.Copy, scale=SW).then_inc(w_split, 1)
            for k in range(KI // 2):
                act.wait_ge(*banks.full(None, ("Wout", k)))
                nc.scalar.activation(WoutT[:, 2 * k:2 * k + 2, :], bank("Wout", k)[:, :].rearrange("p (k n) -> p k n", k=2),
                                     ACT.Copy).then_inc(act_set, 1)
            for k in range(KD):
                for m in range(2):
                    act.wait_ge(*banks.full(None, ("w1", k, m)))
                    nc.scalar.activation(sign1T[:, k, m * 512:(m + 1) * 512], bank("w1", k, m)[:, :],
                                         ACT.Sign).then_inc(act_set, 1)
            for f in range(KF // 2):
                act.wait_ge(*banks.full(None, ("w2", f)))
                nc.scalar.activation(sign2T[:, 2 * f:2 * f + 2, :], bank("w2", f)[:, :].rearrange("p (k n) -> p k n", k=2),
                                     ACT.Sign).then_inc(act_set, 1)
            act.wait_ge(loaded, 16 * NLOADS)
            nc.scalar.activation(a_row[:, :], a_row[:, :], ACT.Exp).then_inc(a_exp, 1)
            act.wait_ge(masks_zero, 11)
            act.wait_ge(dve_set, DVE_SETUP)
            for s in (xh_hi, xi_out, taps_in, xs_out, zs_out, sh_hi, C_out, dt_act, decays_out, seg_exp, yn_out,
                      hf_out, uh_hi, halo):
                s.prime(act)

            def project(b, j):
                for k in range(KD):
                    act.wait_ge(*banks.full(b, ("xT", j, k)))
                    if k == 0:
                        act.wait_ge(*banks.full(b, ("H", 1, KF - 1), 1) if j == 0 else banks.full(b, ("z", 0, KI - 1)))
                    nc.scalar.activation(xh[0][:, k, :], bank("xT", j, k)[:, :], ACT.Copy).then_inc(xh_hi.sem, 1)
                if j == 1:
                    act.wait_ge(*xi_out.count(b, KI))
                    act.wait_ge(*conv_out.count(b, 0))
                    nc.scalar.activation(xi[1][:, :, 0:HALO], xi[0][:, :, BLK:BLK + HALO], ACT.Copy)\
                        .then_inc(halo.sem, 1)
                for c in range(KI):
                    act.wait_ge(*banks.full(b, ("xi", j, c)))
                    if j == 0 and c == 0:
                        act.wait_ge(*halo.count(b, 0))
                    act.wait_ge(*conv_out.count(b, (j * KI + c + 1 - NJ * KI) * (TAPS - 1)))
                    nc.scalar.activation(xi[j][:, c, HALO:HALO + BLK], bank("xi", j, c)[:, :], ACT.Copy,
                                         scale=1.0 / SW).then_inc(xi_out.sem, 1)
                    act.wait_ge(*yT_out.count(b, (j - 1) * NQ * KI + NQ * KI))
                    nc.scalar.activation(xs[:, c, :], bank("xi", j, c)[:, :], ACT.Identity, bias=conv_bias[:, c:c + 1],
                                         scale=last_tap[:, c:c + 1]).then_inc(taps_in.sem, 1)
                for c in range(KI):
                    if c == 0:
                        act.wait_ge(*g_out.count(b, (j + 1 - NJ) * KI))
                    act.wait_ge(*banks.full(b, ("z", j, c)))
                    nc.scalar.activation(zs[:, c, j * BLK:(j + 1) * BLK], bank("z", j, c)[:, :], ACT.Silu,
                                         scale=1.0 / SW).then_inc(zs_out.sem, 1)
                    act.wait_ge(*conv_out.count(b, (j * KI + c + 1) * (TAPS - 1)))
                    nc.scalar.activation(xs[:, c, :], xs[:, c, :], ACT.Silu).then_inc(xs_out.sem, 1)
                for c in range(KI):
                    act.wait_ge(*xs_out.count(b, j * KI + c + 1))
                    if c == 0:
                        act.wait_ge(*banks.full(b, ("C", 1 - j, KI - 1), int(j == 0)))
                    nc.scalar.activation(sh[0][:, c, :], xs[:, c, :], ACT.Copy, scale=SX).then_inc(sh_hi.sem, 1)
                act.wait_ge(*dt_step.count(b, j * 10 + 2))
                nc.scalar.activation(exp_v[:, :, :], abs_v[:, :, :], ACT.Exp, scale=-1.0).then_inc(dt_act.sem, 1)
                act.wait_ge(*dt_step.count(b, j * 10 + 3))
                nc.scalar.activation(log_u[:, :, :], one_e[:, :, :], ACT.Ln).then_inc(dt_act.sem, 1)
                for c in range(KI):
                    act.wait_ge(*banks.full(b, ("C", j, c)))
                    if c == 0:
                        act.wait_ge(*banks.full(b, ("YI", 1 - j, NQ - 1), int(j == 0)))
                    nc.scalar.activation(CT[:, c, :], bank("C", j, c)[:, :], ACT.Copy,
                                         scale=1.0 / (SW * SX)).then_inc(C_out.sem, 1)
                act.wait_ge(*banks.full(b, ("sums", j)))
                act.wait_ge(*st_scaled.count(b, j * NQ))
                nc.scalar.activation(decays[:, :, :, :].rearrange("p a q h -> p (a q h)"),
                                     bank("sums", j)[:, 0:3 * NQ * HEADS], ACT.Exp).then_inc(decays_out.sem, 1)

            def scan(b, j):
                for q in range(NQ):
                    n = ch(j, q)
                    for g in range(HP):
                        act.wait_ge(*banks.full(b, ("seg", j, q, g)))
                        m = (n - 2) % NCH
                        act.wait_ge(*banks.full(b, ("Y", m // NQ, m % NQ), int(n < 2)))
                        nc.scalar.activation(mt[n % 2][:, g].rearrange("p c t -> p (c t)"), bank("seg", j, q, g)[:, :],
                                             ACT.Exp).then_inc(seg_exp.sem, 1)

            with act.Fori(0, NB) as b:
                for j in range(NJ):
                    project(b, j)
                    scan(b, j)
                act.wait_ge(*gn_step.count(b, 8))
                for j in range(NJ):
                    for c in range(KI):
                        v = yT[:, c, j * BLK:(j + 1) * BLK]
                        nc.scalar.activation(v, v, ACT.Identity, bias=gn_shift[:, c:c + 1],
                                             scale=gn_scale[:, c:c + 1]).then_inc(yn_out.sem, 1)
                for j in range(NJ):
                    for k in range(KD):
                        act.wait_ge(*banks.full(b, ("uT", j, k)))
                        if k == 0:
                            act.wait_ge(*banks.full(b, ("z", 1, KI - 1) if j == 0 else ("H", 0, KF - 1)))
                        nc.scalar.activation(uh[0][:, k, :], bank("uT", j, k)[:, :], ACT.Copy).then_inc(uh_hi.sem, 1)
                    for f in range(KF):
                        n = j * KF + f
                        act.wait_ge(*banks.full(b, ("H", j, f)))
                        act.wait_ge(*hh_lo.count(b, n - 1))
                        nc.scalar.activation(hf[f % 2][:, :], bank("H", j, f)[:, :], ACT.Gelu, bias=b1_col[:, f:f + 1],
                                             scale=alpha1[:, f:f + 1]).then_inc(hf_out.sem, 1)

        @block.vector
        def _(dve):
            halves = {"Wx": WxT, "Wz": WzT, "Wb": WbT, "Wc": WcT}
            for n, key in enumerate(lows[:-1]):
                w, k = halves[key[0]], key[1]
                dve.wait_ge(w_split, n + 1)
                nc.vector.scalar_tensor_tensor(out=w[1][:, k, :], in0=psum[banks.index(key)][:, :], scalar=SW,
                                               in1=w[0][:, k, :], op0=ALU.mult, op1=ALU.subtract)\
                    .then_inc(low_set, 1)
            dve.wait_ge(w_split, len(lows))
            nc.vector.scalar_tensor_tensor(out=WdtT[1][:, :, :], in0=bank("Wdt", 0)[:, 0:KI * HEADS]
                                           .rearrange("p (k h) -> p k h", k=KI), scalar=SW, in1=WdtT[0][:, :, :],
                                           op0=ALU.mult, op1=ALU.subtract).then_inc(low_set, 1)
            dve.wait_ge(loaded, 16 * NLOADS)
            nc.vector.tensor_reduce(alpha1[:, :], w1_in, AX_X, ALU.add, apply_absolute_value=True).then_inc(dve_set, 1)
            nc.vector.tensor_reduce(alpha2[:, :], w2_in, AX_X, ALU.add, apply_absolute_value=True).then_inc(dve_set, 1)
            nc.vector.tensor_scalar(last_tap[:, :], taps[:, :, TAPS - 1], 1.0 / SW, None, ALU.mult).then_inc(dve_set, 1)
            dve.wait_ge(dve_set, 2)
            nc.vector.tensor_scalar(alpha1[:, :], alpha1[:, :], 1.0 / D, None, ALU.mult).then_inc(dve_set, 1)
            dve.wait_ge(masks_zero, 11)
            for k in range(KD):
                nc.vector.tensor_scalar(alpha2_wide[k], ones[:, :], alpha2[:, k:k + 1], 1.0 / (FF * SG),
                                        ALU.mult, ALU.mult).then_inc(wide_set, 1)
            dve.wait_ge(*banks.full(None, ("alpha2", 0)))
            nc.vector.tensor_copy(alpha2_row[:, :], bank("alpha2", 0)[:, 0:D]).then_inc(dve_set, 1)
            dve.wait_ge(a_exp, 1)
            nc.vector.tensor_scalar(a_row[:, :], a_row[:, :], -1.0, None, ALU.mult).then_inc(dve_set, 1)
            dve.wait_ge(dve_set, DVE_SETUP)
            dve.wait_ge(low_set, 2 * KD + 2 * KI + 1)
            for s in (ln_stats, ln_moments, ln_eps, xn_made, xh_lo, conv_out, sh_lo, B_out, dt_step, da_seen, mt_out, xdt_out,
                      bw_out, yk_part, yk_out, st_zero, st_scaled, st_out, yT_out, gn_st, gn_mo, gn_step, g_out,
                      mid_out, un_out, hh_hi, hh_lo, y2_scaled, y2_out, y2_norm, uh_lo):
                s.prime(dve)

            def layer_norm(b, which, tile, ready):
                n = LNS.index(which)
                for i in range(NQ):
                    ready(i)
                    nc.vector.bn_stats(stats[:, i, :], tile(i)).then_inc(ln_stats.sem, 1)
                dve.wait_ge(*ln_stats.count(b, (n + 1) * NQ))
                dve.sem_inc(stats_seen, 1)
                for i in range(NQ):
                    nc.vector.bn_aggr(moments[:, i, :], stats[:, i, :]).then_inc(ln_moments.sem, 1)
                dve.wait_ge(*ln_moments.count(b, (n + 1) * NQ))
                dve.wait_ge(*ln_rstd.count(b, n))
                nc.vector.tensor_scalar(var_eps[:, :], moments[:, :, 1], EPS, None, ALU.add).then_inc(ln_eps.sem, 1)
                dve.wait_ge(*ln_rstd.count(b, n + 1))

            def normal(dst, src, i):
                return nc.vector.tensor_scalar(dst, src, moments[:, i, 0:1], rstd[:, i:i + 1], ALU.subtract, ALU.mult)

            def project(b, j):
                layer_norm(b, ("in", j), lambda i: xt[j][:, i, :],
                           lambda i: dve.wait_ge(*x_in[j].count(b, 1)) if i == 0 else None)
                dve.wait_ge(*banks.full(b, ("uT", 1, KD - 1), 1) if j == 0 else banks.full(b, ("xT", 0, KD - 1)))
                for i in range(NQ):
                    normal(xn[:, i, :], xt[j][:, i, :], i).then_inc(xn_made.sem, 1)
                for k in range(KD):
                    dve.wait_ge(*xh_hi.count(b, j * KD + k + 1))
                    nc.vector.tensor_tensor(xh[1][:, k, :], bank("xT", j, k)[:, :], xh[0][:, k, :], ALU.subtract)\
                        .then_inc(xh_lo.sem, 1)
                for c in range(KI):
                    dve.wait_ge(*taps_in.count(b, j * KI + c + 1))
                    dve.wait_ge(*xi_out.count(b, j * KI + c + 1))
                    if j == 1 and c == 0:
                        dve.wait_ge(*halo.count(b, 1))
                    for k in range(TAPS - 1):
                        m = (j * KI + c) * (TAPS - 1) + k
                        if k:
                            dve.wait_ge(*conv_out.count(b, m))
                        nc.vector.scalar_tensor_tensor(out=xs[:, c, :], in0=xi[j][:, c, k:k + BLK],
                                                       scalar=taps[:, c, k:k + 1], in1=xs[:, c, :], op0=ALU.mult,
                                                       op1=ALU.add).then_inc(conv_out.sem, 1)
                for c in range(KI):
                    dve.wait_ge(*sh_hi.count(b, j * KI + c + 1))
                    nc.vector.scalar_tensor_tensor(out=sh[1][:, c, :], in0=xs[:, c, :], scalar=SX, in1=sh[0][:, c, :],
                                                   op0=ALU.mult, op1=ALU.subtract).then_inc(sh_lo.sem, 1)
                s = j * 10
                dve.wait_ge(*banks.full(b, ("dt", j)))
                nc.vector.scalar_tensor_tensor(
                    out=v_dt[:, :, :], in0=bank("dt", j)[:, 0:NQ * HEADS].rearrange("p (q h) -> p q h", q=NQ),
                    scalar=1.0 / (SW * SX), in1=bdt_row[:, None, :].to_broadcast([P, NQ, HEADS]), op0=ALU.mult,
                    op1=ALU.add).then_inc(dt_step.sem, 1)
                dve.wait_ge(*dt_step.count(b, s + 1))
                nc.vector.scalar_tensor_tensor(out=abs_v[:, :, :], in0=v_dt[:, :, :], scalar=-1.0, in1=v_dt[:, :, :],
                                               op0=ALU.mult, op1=ALU.max).then_inc(dt_step.sem, 1)
                dve.wait_ge(*dt_act.count(b, j * 2 + 1))
                nc.vector.tensor_scalar(one_e[:, :, :], exp_v[:, :, :], 1.0, None, ALU.add).then_inc(dt_step.sem, 1)
                dve.wait_ge(*dt_step.count(b, s + 3))
                nc.vector.tensor_scalar(e_back[:, :, :], one_e[:, :, :], 1.0, None, ALU.subtract).then_inc(dt_step.sem, 1)
                dve.wait_ge(*dt_step.count(b, s + 4))
                nc.vector.tensor_tensor(e_rest[:, :, :], exp_v[:, :, :], e_back[:, :, :], ALU.subtract)\
                    .then_inc(dt_step.sem, 1)
                dve.wait_ge(*dt_act.count(b, j * 2 + 2))
                nc.vector.scalar_tensor_tensor(out=dt_raw[:, :, :], in0=v_dt[:, :, :], scalar=0.0, in1=log_u[:, :, :],
                                               op0=ALU.max, op1=ALU.add).then_inc(dt_step.sem, 1)
                dve.wait_ge(*dt_step.count(b, s + 6))
                nc.vector.tensor_tensor(dt_t[:, :, :], dt_raw[:, :, :], e_rest[:, :, :], ALU.add).then_inc(dt_step.sem, 1)
                dve.wait_ge(*dt_step.count(b, s + 7))
                nc.vector.tensor_tensor(da_raw[:, :, :], dt_t[:, :, :], a_row[:, None, :].to_broadcast([P, NQ, HEADS]),
                                        ALU.mult).then_inc(da_seen.sem, 1)
                dve.wait_ge(*da_seen.count(b, j + 1))
                dve.wait_ge(*banks.full(b, ("sums", 1 - j), int(j == 0)))
                nc.vector.tensor_scalar(da[:, :, :], da_raw[:, :, :], DECAY_FLOOR, None, ALU.max).then_inc(dt_step.sem, 1)
                dve.wait_ge(*dt_step.count(b, s + 8))
                dve.wait_ge(*seg_lo.count(b, j * NQ))
                nc.vector.tensor_copy(da_hi[:, :, :], da[:, :, :]).then_inc(dt_step.sem, 1)
                dve.wait_ge(*dt_step.count(b, s + 9))
                nc.vector.tensor_tensor(da_lo[:, :, :], da[:, :, :], da_hi[:, :, :], ALU.subtract).then_inc(dt_step.sem, 1)
                for c in range(KI):
                    dve.wait_ge(*banks.full(b, ("B", j, c)))
                    if c == 0:
                        dve.wait_ge(*banks.full(b, ("S", 1 - j, NQ - 1, HP - 1), int(j == 0)))
                    nc.vector.tensor_scalar(BT[:, c, :], bank("B", j, c)[:, :], 1.0 / (SW * SX), None, ALU.mult)\
                        .then_inc(B_out.sem, 1)

            def per_head(ap):
                return ap[:, :, None].to_broadcast([P, HEADS, HD])

            def heads(ap):
                return ap.rearrange("p (h n) -> p h n", h=HEADS)

            def scan(b, j):
                if j == 0:
                    dve.wait_ge(*banks.full(b, ("YI", NJ - 1, NQ - 1), 1))
                    dve.wait_ge(*st_out.count(b, 0))
                    nc.vector.memset(state[:, :, :], 0.0).then_inc(st_zero.sem, 1)
                for kind, q in scan_steps():
                    n = ch(j, q)
                    r = n % 2
                    m = (n - 2) % NCH
                    if kind == "front":
                        if q == 0:
                            dve.wait_ge(*decays_out.count(b, j + 1))
                        dve.wait_ge(*banks.full(b, ("X", j, q)))
                        dve.wait_ge(*banks.full(b, ("Y", m // NQ, m % NQ), int(n < 2)))
                        nc.vector.tensor_tensor(xdt[r][:, :, :], heads(bank("X", j, q)[:, :]), per_head(dt_t[:, q, :]),
                                                ALU.mult).then_inc(xdt_out.sem, 1)
                        dve.wait_ge(*banks.full(b, ("Bt", j, q)))
                        nc.vector.tensor_tensor(bw[r][:, :, :], heads(bank("Bt", j, q)[:, :]),
                                                per_head(decays[:, 1, q, :]), ALU.mult).then_inc(bw_out.sem, 1)
                        for g in range(HP):
                            dve.wait_ge(*banks.full(b, ("S", j, q, g)))
                            dve.wait_ge(*seg_exp.count(b, n * HP + g + 1))
                            v = mt[r][:, g].rearrange("p c t -> p (c t)")
                            nc.vector.tensor_tensor(v, bank("S", j, q, g)[:, :], v, ALU.mult).then_inc(mt_out.sem, 1)
                    elif kind == "back":
                        dve.wait_ge(*banks.full(b, ("YI", j, q)))
                        dve.wait_ge(*banks.full(b, ("YT", m // NQ, m % NQ), int(n < 2)))
                        nc.vector.tensor_tensor(yk[r][:, :, :], heads(bank("YI", j, q)[:, :]),
                                                per_head(decays[:, 0, q, :]), ALU.mult).then_inc(yk_part.sem, 1)
                        st = state[:, :, :].rearrange("p c (g n) -> p (c g) n", g=HP)
                        if n == 0:
                            dve.wait_ge(*st_zero.count(b, 1))
                        else:
                            dve.wait_ge(*st_out.count(b, n * HP))
                        nc.vector.tensor_tensor(st, st, per_head(decays[:, 2, q, :]), ALU.mult).then_inc(st_scaled.sem, 1)
                        dve.wait_ge(*banks.full(b, ("St", j, q)))
                        dve.wait_ge(*st_scaled.count(b, n + 1))
                        for g in range(HP):
                            rows = slice(g * HD, (g + 1) * HD)
                            v = state[rows, :, g * HD:(g + 1) * HD]
                            nc.vector.tensor_tensor(
                                v, v, bank("St", j, q)[rows, :].rearrange("p (c n) -> p c n", c=KI)[:, :, g * HD:(g + 1) * HD],
                                ALU.add).then_inc(st_out.sem, 1)
                        dve.wait_ge(*banks.full(b, ("Y", j, q)))
                        dve.wait_ge(*yk_part.count(b, n + 1))
                        nc.vector.tensor_tensor(yk[r][:, :, :], yk[r][:, :, :], heads(bank("Y", j, q)[:, :]),
                                                ALU.add).then_inc(yk_out.sem, 1)
                    else:
                        dve.wait_ge(*banks.full(b, ("YT", j, q)))
                        if n == 0:
                            dve.wait_ge(*g_out.count(b, 0))
                            dve.wait_ge(*banks.full(b, ("Wo", NJ - 1, NQ // 2 - 1), 1))
                        for c in range(KI):
                            nc.vector.scalar_tensor_tensor(
                                out=yT[:, c, n * P:(n + 1) * P], in0=xs[:, c, q * P:(q + 1) * P],
                                scalar=skip[:, c:c + 1], in1=bank("YT", j, q)[:, c * P:(c + 1) * P], op0=ALU.mult,
                                op1=ALU.add).then_inc(yT_out.sem, 1)
                for c in range(KI):
                    if c == 0:
                        dve.wait_ge(*yT_out.count(b, (j + 1) * NQ * KI))
                    nc.vector.bn_stats(gn_stats[:, c, j, :], yT[:, c, j * BLK:(j + 1) * BLK]).then_inc(gn_st.sem, 1)

            def head_norm(b):
                for c in range(KI):
                    if c == 0:
                        dve.wait_ge(*gn_st.count(b, NJ * KI))
                        dve.sem_inc(stats_seen, 1)
                    nc.vector.bn_aggr(gn_mom[:, c, :], gn_stats[:, c, :, :].rearrange("p j s -> p (j s)"))\
                        .then_inc(gn_mo.sem, 1)
                dve.wait_ge(*gn_mo.count(b, KI))
                nc.vector.tensor_tensor(gn_sq[:, :], gn_mom[:, :, 0], gn_mom[:, :, 0], ALU.mult).then_inc(gn_step.sem, 1)
                dve.wait_ge(*gn_step.count(b, 1))
                nc.vector.tensor_tensor(gn_mom[:, :, 1], gn_mom[:, :, 1], gn_sq[:, :], ALU.add).then_inc(gn_step.sem, 1)
                dve.wait_ge(*banks.full(b, ("gn",)))
                nc.vector.tensor_copy(gn_head[:, :, :], bank("gn")[:, 0:2 * KI].rearrange("p (c s) -> p c s", s=2))\
                    .then_inc(gn_step.sem, 1)
                dve.wait_ge(*gn_step.count(b, 3))
                nc.vector.tensor_tensor(gn_msq[:, :], gn_head[:, :, 0], gn_head[:, :, 0], ALU.mult)\
                    .then_inc(gn_step.sem, 1)
                dve.wait_ge(*gn_step.count(b, 4))
                nc.vector.scalar_tensor_tensor(out=gn_var[:, :], in0=gn_head[:, :, 1], scalar=EPS, in1=gn_msq[:, :],
                                               op0=ALU.add, op1=ALU.subtract).then_inc(gn_step.sem, 1)
                dve.wait_ge(*gn_rs.count(b, 1))
                nc.vector.tensor_tensor(gn_scale[:, :], gn_rstd[:, :], gnw[:, :], ALU.mult).then_inc(gn_step.sem, 1)
                dve.wait_ge(*gn_step.count(b, 6))
                nc.vector.tensor_tensor(gn_ms[:, :], gn_head[:, :, 0], gn_scale[:, :], ALU.mult).then_inc(gn_step.sem, 1)
                dve.wait_ge(*gn_step.count(b, 7))
                nc.vector.tensor_tensor(gn_shift[:, :], gnb[:, :], gn_ms[:, :], ALU.subtract).then_inc(gn_step.sem, 1)

            def gate(b, j):
                for c in range(KI):
                    dve.wait_ge(*yn_out.count(b, j * KI + c + 1))
                    v = yT[:, c, j * BLK:(j + 1) * BLK]
                    nc.vector.tensor_tensor(v, v, zs[:, c, j * BLK:(j + 1) * BLK], ALU.mult).then_inc(g_out.sem, 1)

            def attention_out(b, j):
                def tile(i):
                    return bank("Wo", j, i // 2)[:, (i % 2) * D:(i % 2 + 1) * D]
                layer_norm(b, ("mid", j), tile, lambda i: dve.wait_ge(*banks.full(b, ("Wo", j, i // 2))))
                dve.wait_ge(*stored[j].count(b, 0))
                for i in range(NQ):
                    normal(u[j][:, i, :], tile(i), i).then_inc(mid_out.sem, 1)
                layer_norm(b, ("ff", j), lambda i: u[j][:, i, :],
                           lambda i: dve.wait_ge(*u_out.count(b, j * NQ + i + 1)))
                dve.wait_ge(*banks.full(b, ("xT", 1, KD - 1) if j == 0 else ("uT", 0, KD - 1)))
                for i in range(NQ):
                    normal(un[:, i, :], u[j][:, i, :], i).then_inc(un_out.sem, 1)

            def hidden(b, j):
                for k in range(KD):
                    dve.wait_ge(*uh_hi.count(b, j * KD + k + 1))
                    nc.vector.tensor_tensor(uh[1][:, k, :], bank("uT", j, k)[:, :], uh[0][:, k, :], ALU.subtract)\
                        .then_inc(uh_lo.sem, 1)

            def hidden_split(b, j):
                for f in range(KF):
                    n = j * KF + f
                    dve.wait_ge(*hf_out.count(b, n + 1))
                    if f == 0:
                        dve.wait_ge(*banks.full(b, ("O", 1 - j, NQ // 2 - 1), int(j == 0)))
                    nc.vector.tensor_scalar(hh[0][:, f, :], hf[f % 2][:, :], SG, None, ALU.mult).then_inc(hh_hi.sem, 1)
                    dve.wait_ge(*hh_hi.count(b, n + 1))
                    nc.vector.scalar_tensor_tensor(out=hh[1][:, f, :], in0=hf[f % 2][:, :], scalar=SG,
                                                   in1=hh[0][:, f, :], op0=ALU.mult, op1=ALU.subtract)\
                        .then_inc(hh_lo.sem, 1)

            def ffn_out(b, j):
                for m in range(NQ // 2):
                    n = j * NQ // 2 + m
                    v = y2[:, 2 * m:2 * m + 2, :]
                    dve.wait_ge(*banks.full(b, ("O", j, m)))
                    dve.wait_ge(*o_out.count(b, (j - 1) * NQ + NQ))
                    nc.vector.tensor_tensor(v, bank("O", j, m)[:, :].rearrange("p (i d) -> p i d", i=2),
                                            alpha2_row[:, None, :].to_broadcast([P, 2, D]), ALU.mult)\
                        .then_inc(y2_scaled.sem, 1)
                    dve.wait_ge(*y2_scaled.count(b, n + 1))
                    nc.vector.tensor_tensor(v, v, b2_row[:, None, :].to_broadcast([P, 2, D]), ALU.add)\
                        .then_inc(y2_out.sem, 1)
                layer_norm(b, ("end", j), lambda i: y2[:, i, :],
                           lambda i: dve.wait_ge(*y2_out.count(b, j * NQ // 2 + i // 2 + 1)))
                for i in range(NQ):
                    normal(y2[:, i, :], y2[:, i, :], i).then_inc(y2_norm.sem, 1)

            with dve.Fori(0, NB) as b:
                for j in range(NJ):
                    project(b, j)
                    scan(b, j)
                head_norm(b)
                for j in range(NJ):
                    gate(b, j)
                attention_out(b, 0)
                hidden(b, 0)
                attention_out(b, 1)
                hidden_split(b, 0)
                hidden(b, 1)
                ffn_out(b, 0)
                hidden_split(b, 1)
                ffn_out(b, 1)

        @block.tensor
        def _(pe):
            pe.wait_ge(masks_made, 9)
            pe.wait_ge(masks_zero, 11)
            pe.wait_ge(loaded, 16 * NLOADS)

            def turn_weights(key, parts, id_=None):
                if banks.place[key][1]:
                    pe.wait_ge(*banks.empty(None, key))
                for n, part in enumerate(parts):
                    rows, w = part.shape[0], psum[banks.index(key)]
                    mm = nc.tensor.transpose(w[:, n * rows:(n + 1) * rows], part, ident[0:rows, 0:rows])
                mm.then_inc(banks.full_sem(key), 1)

            def cols(k):
                return slice(k * P, (k + 1) * P)

            for name, w in (("Wx", Wx_in), ("Wz", Wz_in)):
                for k in range(KD):
                    turn_weights((name, k), [w[:, m, cols(k)] for m in range(KI)])
            for name, w in (("Wb", Wb_in), ("Wc", Wc_in)):
                for k in range(KI):
                    turn_weights((name, k), [w[:, m, cols(k)] for m in range(KI)])
            turn_weights(("Wdt", 0), [Wdt_in[:, cols(k)] for k in range(KI)])
            for k in range(KI // 2):
                turn_weights(("Wout", k), [Wout_in[:, m, cols(2 * k + kk)] for kk in range(2) for m in range(KD)])
            for k in range(KD):
                for h in range(2):
                    turn_weights(("w1", k, h), [w1_in[:, 4 * h + m, cols(k)] for m in range(4)])
            for f in range(KF // 2):
                turn_weights(("w2", f), [w2_in[:, m, cols(2 * f + ff)] for ff in range(2) for m in range(KD)])
            pe.wait_ge(wide_set, KD)
            pe.wait_ge(*banks.empty(None, ("alpha2", 0)))
            for k in range(KD):
                mm = nc.tensor.matmul(bank("alpha2", 0)[:, cols(k)], alpha2_wide[k], ident[:, :], start=True, stop=True)
            mm.then_inc(banks.full_sem(("alpha2", 0)), 1)
            pe.wait_ge(dve_set, DVE_SETUP)
            pe.wait_ge(low_set, 2 * KD + 2 * KI + 1)
            pe.wait_ge(act_set, ACT_SETUP)
            banks.prime(pe)

            def split_product(b, key, w, v, n, m):
                pe.wait_ge(*banks.empty(b, key))
                dst = psum[banks.index(key)]
                terms = [(k, i, h) for k in range(n) for i, h in ((0, 0), (1, 0), (0, 1))]
                for t, (k, i, h) in enumerate(terms):
                    mm = nc.tensor.matmul(dst[:, :], w[i][:, k, cols(m)], v[h][:, k, :], start=(t == 0),
                                          stop=(t == len(terms) - 1))
                mm.then_inc(banks.full_sem(key), 1)

            def turn_tokens(b, name, j, src, made):
                for k in range(KD):
                    pe.wait_ge(*banks.empty(b, (name, j, k)))
                    for i in range(NQ):
                        if k == 0:
                            pe.wait_ge(*made.count(b, j * NQ + i + 1))
                        mm = nc.tensor.transpose(bank(name, j, k)[:, cols(i)], src[:, i, cols(k)], ident[:, :])
                    mm.then_inc(banks.full_sem((name, j, k)), 1)

            def project(b, j):
                turn_tokens(b, "xT", j, xn, xn_made)
                pe.wait_ge(*xh_lo.count(b, (j + 1) * KD))
                for c in range(KI):
                    split_product(b, ("xi", j, c), WxT, xh, KD, c)
                for c in range(KI):
                    split_product(b, ("z", j, c), WzT, xh, KD, c)
                pe.wait_ge(*sh_lo.count(b, (j + 1) * KI))
                pe.wait_ge(*banks.empty(b, ("dt", j)))
                terms = [(k, i, h) for k in range(KI) for i, h in ((0, 0), (1, 0), (0, 1))]
                for q in range(NQ):
                    for t, (k, i, h) in enumerate(terms):
                        mm = nc.tensor.matmul(bank("dt", j)[:, q * HEADS:(q + 1) * HEADS], sh[h][:, k, cols(q)],
                                              WdtT[i][:, k, :], start=(t == 0), stop=(t == len(terms) - 1))
                mm.then_inc(banks.full_sem(("dt", j)), 1)
                for c in range(KI):
                    split_product(b, ("B", j, c), WbT, sh, KI, c)
                for c in range(KI):
                    split_product(b, ("C", j, c), WcT, sh, KI, c)
                pe.wait_ge(*dt_step.count(b, j * 10 + 8))
                pe.wait_ge(*banks.empty(b, ("sums", j)))
                for n, w in enumerate((upto, after, ones)):
                    mm = nc.tensor.matmul(bank("sums", j)[:, n * NQ * HEADS:(n + 1) * NQ * HEADS], w[:, :],
                                          da[:, :, :].rearrange("p q h -> p (q h)"), start=True, stop=True)
                mm.then_inc(banks.full_sem(("sums", j)), 1)

            def scan(b, j):
                for kind, q in scan_steps():
                    n = ch(j, q)
                    r = n % 2
                    if kind == "front":
                        pe.wait_ge(*seg_lo.count(b, n + 1))
                        for g in range(HP):
                            dst = bank("seg", j, q, g)
                            pe.wait_ge(*banks.empty(b, ("seg", j, q, g)))
                            for i in range(2):
                                nc.tensor.matmul(dst[:, :], after_h[:, :],
                                                 seg[i][r][:, g].rearrange("p c t -> p (c t)"), start=(i == 0), stop=False)
                            nc.tensor.matmul(dst[:, :], ident_h[:, :], future_h[:, None, :].to_broadcast([P, KI, P]),
                                             start=False, stop=True).then_inc(banks.full_sem(("seg", j, q, g)), 1)
                        if q == 0:
                            pe.wait_ge(*B_out.count(b, (j + 1) * KI))
                            pe.wait_ge(*C_out.count(b, (j + 1) * KI))
                        for name, src in (("X", xs), ("Bt", BT)):
                            pe.wait_ge(*banks.empty(b, (name, j, q)))
                            for c in range(KI):
                                mm = nc.tensor.transpose(bank(name, j, q)[:, cols(c)], src[:, c, cols(q)], ident[:, :])
                            mm.then_inc(banks.full_sem((name, j, q)), 1)
                        for g in range(HP):
                            rows = slice(g * NS, (g + 1) * NS)
                            pe.wait_ge(*banks.empty(b, ("S", j, q, g)))
                            for c in range(KI):
                                mm = nc.tensor.matmul(bank("S", j, q, g)[:, cols(c)], BT[rows, c, cols(q)],
                                                      CT[rows, c, cols(q)], start=True, stop=True)
                            mm.then_inc(banks.full_sem(("S", j, q, g)), 1)
                    elif kind == "back":
                        pe.wait_ge(*banks.empty(b, ("YI", j, q)))
                        if n == 0:
                            pe.wait_ge(*st_zero.count(b, 1))
                        else:
                            pe.wait_ge(*st_out.count(b, n * HP))
                        for c in range(KI):
                            mm = nc.tensor.matmul(bank("YI", j, q)[:, cols(c)], CT[:, c, cols(q)], state[:, c, :],
                                                  start=True, stop=True)
                        mm.then_inc(banks.full_sem(("YI", j, q)), 1)
                        pe.wait_ge(*bw_out.count(b, n + 1))
                        pe.wait_ge(*banks.empty(b, ("St", j, q)))
                        for c in range(KI):
                            pair = slice(HP * c, HP * c + HP)
                            mm = nc.tensor.matmul(bank("St", j, q)[:, cols(c)],
                                                  bw[r][:, pair, :].rearrange("p h n -> p (h n)"),
                                                  xdt[r][:, pair, :].rearrange("p h n -> p (h n)"), start=True, stop=True)
                        mm.then_inc(banks.full_sem(("St", j, q)), 1)
                        pe.wait_ge(*mt_out.count(b, (n + 1) * HP))
                        pe.wait_ge(*banks.empty(b, ("Y", j, q)))
                        for h in range(HEADS):
                            mm = nc.tensor.matmul(bank("Y", j, q)[:, h * HD:(h + 1) * HD], mt[r][:, h % HP, h // HP, :],
                                                  xdt[r][:, h, :], start=True, stop=True)
                        mm.then_inc(banks.full_sem(("Y", j, q)), 1)
                    else:
                        pe.wait_ge(*yk_out.count(b, n + 1))
                        pe.wait_ge(*banks.empty(b, ("YT", j, q)))
                        for c in range(KI):
                            pair = slice(HP * c, HP * c + HP)
                            mm = nc.tensor.transpose(bank("YT", j, q)[:, cols(c)],
                                                     yk[r][:, pair, :].rearrange("p h n -> p (h n)"), ident[:, :])
                        mm.then_inc(banks.full_sem(("YT", j, q)), 1)

            def attention_out(b, j):
                pe.wait_ge(*g_out.count(b, (j + 1) * KI))
                for m in range(NQ // 2):
                    pe.wait_ge(*banks.empty(b, ("Wo", j, m)))
                    for i in (2 * m, 2 * m + 1):
                        for c in range(KI):
                            mm = nc.tensor.matmul(bank("Wo", j, m)[:, (i % 2) * D:(i % 2 + 1) * D],
                                                  yT[:, c, (j * NQ + i) * P:(j * NQ + i + 1) * P], WoutT[:, c, :],
                                                  start=(c == 0), stop=(c == KI - 1))
                    mm.then_inc(banks.full_sem(("Wo", j, m)), 1)

            def hidden(b, j):
                pe.wait_ge(*uh_lo.count(b, (j + 1) * KD))
                for f in range(KF):
                    pe.wait_ge(*banks.empty(b, ("H", j, f)))
                    for t, (k, i) in enumerate([(k, i) for k in range(KD) for i in range(2)]):
                        mm = nc.tensor.matmul(bank("H", j, f)[:, :], sign1T[:, k, cols(f)], uh[i][:, k, :],
                                              start=(t == 0), stop=(t == 2 * KD - 1))
                    mm.then_inc(banks.full_sem(("H", j, f)), 1)

            def ffn_out(b, j):
                pe.wait_ge(*hh_lo.count(b, (j + 1) * KF))
                for m in range(NQ // 2):
                    pe.wait_ge(*banks.empty(b, ("O", j, m)))
                    for i in (2 * m, 2 * m + 1):
                        for t, (f, p) in enumerate([(f, p) for f in range(KF) for p in range(2)]):
                            mm = nc.tensor.matmul(bank("O", j, m)[:, (i % 2) * D:(i % 2 + 1) * D],
                                                  hh[p][:, f, cols(i)], sign2T[:, f, :], start=(t == 0),
                                                  stop=(t == 2 * KF - 1))
                    mm.then_inc(banks.full_sem(("O", j, m)), 1)

            with pe.Fori(0, NB) as b:
                for j in range(NJ):
                    project(b, j)
                    scan(b, j)
                pe.wait_ge(*gn_step.count(b, 2))
                pe.wait_ge(*banks.empty(b, ("gn",)))
                nc.tensor.matmul(bank("gn")[:, 0:2 * KI], head_mean[:, :], gn_mom[:, :, :].rearrange("p c s -> p (c s)"),
                                 start=True, stop=True).then_inc(banks.full_sem(("gn",)), 1)
                attention_out(b, 0)
                attention_out(b, 1)
                turn_tokens(b, "uT", 0, un, un_out)
                hidden(b, 0)
                turn_tokens(b, "uT", 1, un, un_out)
                ffn_out(b, 0)
                hidden(b, 1)
                ffn_out(b, 1)


_INS = ["L0_attn_input_tensor", "L0_attn_Wx", "L0_attn_Wz", "L0_attn_conv_w", "L0_attn_conv_b", "L0_attn_Wb",
        "L0_attn_Wc", "L0_attn_Wdt", "L0_attn_b_dt", "L0_attn_log_a", "L0_attn_d_param", "L0_attn_gn_w",
        "L0_attn_gn_b", "L0_attn_Wout", "L0_ffn_w1", "L0_ffn_b1", "L0_ffn_w2", "L0_ffn_b2"]


def kernel(**inputs):
    import numpy as _np
    import concourse.bacc as _bacc
    from concourse import mybir as _mybir
    from concourse.bass_utils import run_bass_kernel_spmd as _run

    nc = _bacc.Bacc("TRN2", target_bir_lowering=False, num_devices=1)
    arrays, args = {}, []
    for name in _INS:
        a = _np.ascontiguousarray(inputs[name])
        arrays[f"in_{name}_dram"] = a
        args.append(nc.dram_tensor(f"in_{name}_dram", a.shape, _mybir.dt.from_np(a.dtype), kind="ExternalInput").ap())
    args.append(nc.dram_tensor("out_0_dram", (NB, T, D), F32, kind="ExternalOutput").ap())
    mamba_sandwich_kernel(nc, *args)
    r = _run(nc, [arrays], core_ids=[0])
    return r.results[0]["out_0_dram"]
```

```python
from contextlib import ExitStack

import concourse.bass as bass
from concourse import mybir

F32 = mybir.dt.float32
F16 = mybir.dt.float16
ALU = mybir.AluOpType
ACT = mybir.ActivationFunctionType
AX_X = mybir.AxisListType.X

P = 128
NB, T, D = 8, 1024, 256
INNER, HEADS, HD, NS = 512, 8, 64, 64
TAPS = 4
FF = 1024
EPS = 1e-5

BLK = 512
NJ = T // BLK
NQ = BLK // P
KD = D // P
KI = INNER // P
HP = P // HD
KF = FF // P
HALO = TAPS - 1

SW = 256.0
SX = 256.0
SG = 64.0
MASKED = -30000.0
DECAY_FLOOR = -10000.0


BANKS = 8
OWN_BANKS = 6


class Batch:

    def __init__(self, b, d=0):
        self.b, self.d = b, d

    def ago(self, n):
        return Batch(self.b, self.d - n)

    def number(self):
        return self.b + self.d if self.d else self.b


class Count(tuple):

    def __new__(cls, sem, b, rate, rest):
        self = super().__new__(cls, (sem, b * rate + rest))
        self.rest = rest
        return self


def latest(*counts):
    return [c for c in counts if not any(d[0] is c[0] and d.rest > c.rest for d in counts)]


class Signal:

    def __init__(self, sem, each, step=1):
        self.sem, self.each, self.step = sem, each, step

    def count(self, t, n):
        return Count(self.sem, t.b, self.each * self.step, ((t.d + 1) * self.each + n) * self.step)

    def prime(self, eng):
        eng.sem_inc(self.sem, self.each * self.step)


class Ring:

    def __init__(self, tensors, full_sems, keys, once):
        self.tensors, self.full_sems, self.keys, self.once = tensors, full_sems, keys, once
        self.place, self.each = {}, [0] * len(tensors)
        for n, key in enumerate(keys):
            k = n % len(tensors)
            self.place[key] = k, self.each[k]
            self.each[k] += 1
        self.read = {}

    def bank(self, key):
        return self.tensors[self.place[key][0]]

    def full_sem(self, key):
        return self.full_sems[self.place[key][0]]

    def full(self, t, key):
        k, m = self.place[key]
        if t is None:
            return self.full_sems[k], m + 1
        return Count(self.full_sems[k], t.b, self.each[k], self.once[k] + (t.d + 1) * self.each[k] + m + 1)

    def empty(self, t, key):
        k, m = self.place[key]
        of = [x for x in self.keys if self.place[x] == (k, (m - 1) % self.each[k])][0]
        signal, n = self.read[of]
        if t is None:
            return signal, n
        return signal.count(t.ago(1) if m == 0 else t, n)

    def prime(self, pe):
        for k in range(len(self.tensors)):
            pe.sem_inc(self.full_sems[k], self.each[k])


def turn_steps(first, last):
    def own(*keys):
        return [("own", *k) for k in keys]

    def tail(*keys):
        return [("tail", *k) for k in keys]

    def then(j):
        return [("next", "in_stat", 0)] if j else own(("in_stat", 1)), [("next", "in_norm", 0)] if j else own(("in_norm", 1))

    steps = []
    for j in range(NJ):
        if j == 0:
            steps += tail(("gn_sum",)) + own(("xT", 0)) + tail(("gn_root",))
            steps += own(("xi", 0, 0), ("xi", 0, 1)) + tail(("gn_fold",), ("gate", 0))
            steps += own(("xi", 0, 2), ("xi", 0, 3)) + tail(("gate", 1))
        else:
            steps += own(("xT", 1), *[("xi", 1, c) for c in range(KI)])
        for c in range(KI):
            steps += own(("z", j, c), ("silu", j, c))
        steps += own(*[("xs", j, c) for c in range(KI)])
        if j == 0:
            steps += tail(("Wo", 0), ("mid_stat", 0)) + own(("dt", 0)) + tail(("mid_norm", 0), ("Wo", 1))
            steps += own(("B", 0, 0), ("log", 0), ("B", 0, 1)) + tail(("mid_stat", 1)) + own(("decay", 0), ("B", 0, 2))
            steps += tail(("mid_norm", 1), ("ff_stat", 0)) + own(("B", 0, 3), ("skip", 0), ("seg", 0, 0), ("sums", 0))
            steps += own(("C", 0, 0), ("C", 0, 1)) + tail(("ff_norm", 0)) + own(("seg", 0, 1), ("C", 0, 2), ("C", 0, 3))
            steps += tail(("uT", 0))
        else:
            steps += tail(("ff_stat", 1)) + own(("dt", 1), ("B", 1, 0), ("log", 1)) + tail(("ff_norm", 1))
            steps += own(("B", 1, 1), ("decay", 1), ("B", 1, 2), ("B", 1, 3), ("skip", 1), ("seg", 1, 0), ("sums", 1))
            steps += own(("C", 1, 0), ("C", 1, 1), ("seg", 1, 1), ("C", 1, 2), ("C", 1, 3)) + tail(("uT", 1))
        stat, norm = then(j)
        steps += own(("front", j, 0)) + tail(("H", j)) + own(("front", j, 1), ("seg", j, 2), ("back", j, 0))
        steps += own(("front", j, 2), ("seg", j, 3), ("back", j, 1)) + tail(("O", j)) + own(("turn", j, 0))
        steps += own(("front", j, 3)) + tail(("end_stat", j)) + own(("back", j, 2), ("turn", j, 1)) + stat
        steps += own(("back", j, 3)) + tail(("end_norm", j)) + own(("turn", j, 2)) + norm
        steps += own(("turn", j, 3), ("head_stat", j))
    return [s for s in steps if not (first and s[0] == "tail") and not (last and s[0] == "next")]


def last_tail():
    return [("tail", *k) for k in (
        ("gn_sum",), ("gn_root",), ("gn_fold",), ("gate", 0), ("gate", 1), ("Wo", 0), ("mid_stat", 0),
        ("mid_norm", 0), ("Wo", 1), ("mid_stat", 1), ("ff_stat", 0), ("mid_norm", 1), ("ff_norm", 0), ("uT", 0),
        ("ff_stat", 1), ("H", 0), ("O", 0), ("ff_norm", 1), ("uT", 1), ("end_stat", 0), ("H", 1), ("end_norm", 0),
        ("O", 1), ("end_stat", 1), ("end_norm", 1))]


def mamba_sandwich_kernel(nc, x, Wx, Wz, conv_w, conv_b, Wb, Wc, Wdt, b_dt, log_a, d_param, gn_w, gn_b,
                          Wout, w1, b1, w2, b2, out):
    ctx = ExitStack()
    with ctx:
        def sb(name, shape, dt=F32):
            return ctx.enter_context(nc.sbuf_tensor(name, shape, dt))

        def sem(name):
            return ctx.enter_context(nc.semaphore(name))

        ident = sb("ident", [P, P])
        ident_h = sb("ident_h", [P, P], F16)
        upto = sb("upto", [P, P])
        upto_h = sb("upto_h", [P, P], F16)
        after = sb("after", [P, P])
        after_h = sb("after_h", [P, P], F16)
        ones = sb("ones", [P, P])
        future_h = sb("future_h", [P, P], F16)
        head_mean = sb("head_mean", [P, P])
        power = sb("power", [P, 4])

        WxT = [sb(f"WxT{i}", [P, KD, INNER], F16) for i in range(2)]
        WzT = [sb(f"WzT{i}", [P, KD, INNER], F16) for i in range(2)]
        WbT = [sb(f"WbT{i}", [P, KI, HEADS * NS], F16) for i in range(2)]
        WcT = [sb(f"WcT{i}", [P, KI, HEADS * NS], F16) for i in range(2)]
        WdtT = [sb(f"WdtT{i}", [P, KI, HEADS], F16) for i in range(2)]
        WoutT = sb("WoutT", [P, KI, D])
        sign1T = sb("sign1T", [P, KD, FF], F16)
        sign2T = sb("sign2T", [P, KF, D], F16)
        alpha1 = sb("alpha1", [P, KF])
        alpha2 = sb("alpha2", [P, KD])
        alpha2_row = sb("alpha2_row", [P, D])
        b1_col = sb("b1_col", [P, KF])
        b2_row = sb("b2_row", [P, D])
        taps = sb("taps", [P, KI, TAPS])
        last_tap = sb("last_tap", [P, KI])
        conv_bias = sb("conv_bias", [P, KI])
        gnw = sb("gnw", [P, KI])
        gnb = sb("gnb", [P, KI])
        skip = sb("skip", [P, KI])
        bdt_row = sb("bdt_row", [P, HEADS])
        a_row = sb("a_row", [P, HEADS])

        xt = [sb(f"xt{j}", [P, NQ, D]) for j in range(NJ)]
        xn = sb("xn", [P, NQ, D])
        xh = [sb(f"xh{i}", [P, KD, BLK], F16) for i in range(2)]
        uh = [sb(f"uh{i}", [P, KD, BLK], F16) for i in range(2)]
        xi = sb("xi", [P, KI, HALO + BLK])
        no_halo = sb("no_halo", [P, KI, HALO])
        xs = sb("xs", [P, KI, BLK])
        sh = [sb(f"sh{i}", [P, KI, BLK], F16) for i in range(2)]
        zs = sb("zs", [P, KI, T])
        yT = sb("yT", [P, KI, T])
        BT = sb("BT", [P, KI, BLK])
        CT = sb("CT", [P, KI, BLK])

        def small(name, dt=F32):
            return sb(name, [P, NQ, HEADS], dt)
        v_dt, abs_v, exp_v, one_e, e_back, e_rest, log_u = (small(n) for n in (
            "v_dt", "abs_v", "exp_v", "one_e", "e_back", "e_rest", "log_u"))
        dt_raw = small("dt_raw")
        dt_t = small("dt_t")
        da_raw = small("da_raw")
        da = small("da")
        da_hi, da_lo = small("da_hi", F16), small("da_lo", F16)
        decays = sb("decays", [P, 3, NQ, HEADS])

        seg = [[sb(f"seg{i}{r}", [P, HP, KI, P], F16) for r in range(2)] for i in range(2)]
        mt = [sb(f"mt{r}", [P, HP, KI, P]) for r in range(2)]
        xdt = [sb(f"xdt{r}", [P, HEADS, HD]) for r in range(2)]
        xdw = [sb(f"xdw{r}", [P, HEADS, HD]) for r in range(2)]
        bt = [sb(f"bt{r}", [P, HEADS * NS]) for r in range(2)]
        yk = [sb(f"yk{r}", [P, HEADS, HD]) for r in range(2)]
        state = sb("state", [P, KI, P])

        LNS = ("in", "mid", "ff", "end")
        stats = {w: sb(f"stats_{w}", [P, NQ, 6]) for w in LNS}
        moments = {w: sb(f"moments_{w}", [P, NQ, 2]) for w in LNS}
        var_eps = {w: sb(f"var_eps_{w}", [P, NQ]) for w in LNS}
        rstd = {w: sb(f"rstd_{w}", [P, NQ]) for w in LNS}
        gn_stats = sb("gn_stats", [P, KI, NJ, 6])
        gn_mom = sb("gn_mom", [P, KI, 2])
        gn_sq = sb("gn_sq", [P, KI])
        gn_head = sb("gn_head", [P, KI, 2])
        gn_msq = sb("gn_msq", [P, KI])
        gn_var = sb("gn_var", [P, KI])
        gn_rstd = sb("gn_rstd", [P, KI])
        gn_scale = sb("gn_scale", [P, KI])
        gn_ms = sb("gn_ms", [P, KI])
        gn_shift = sb("gn_shift", [P, KI])

        u = [sb(f"u{j}", [P, NQ, D]) for j in range(NJ)]
        un = sb("un", [P, NQ, D])
        hf = [sb(f"hf{r}", [P, BLK]) for r in range(2)]
        hh = [sb(f"hh{i}", [P, KF, BLK], F16) for i in range(2)]
        y2 = sb("y2", [P, NQ, D])
        mn = [un, y2]

        Wdt_in = state[0:HEADS, :, :].rearrange("p c n -> p (c n)")
        Wb_in, Wc_in = zs[:, :, 0:INNER], zs[:, :, INNER:2 * INNER]
        w1_in = yT[:, 0:2, :].rearrange("p a (b d) -> p (a b) d", d=D)
        w2_in = yT[:, 2:4, :]
        Wx_in = BT[:, :, :].rearrange("p a n -> p (a n)")[:, 0:KI * D].rearrange("p (a d) -> p a d", d=D)
        Wz_in = BT[:, :, :].rearrange("p a n -> p (a n)")[:, KI * D:2 * KI * D].rearrange("p (a d) -> p a d", d=D)
        Wout_in = CT[:, 0:2, :]
        alpha2_wide = [CT[:, 2, k * P:(k + 1) * P] for k in range(KD)]

        before = [("Wx", k) for k in range(KD)] + [("Wz", k) for k in range(KD)]
        before += [("Wb", k) for k in range(KI)] + [("Wc", k) for k in range(KI)] + [("Wdt", 0)]
        before += [("Wout", k) for k in range(KI // 2)]
        before += [("w1", k, m) for k in range(KD) for m in range(2)] + [("w2", f) for f in range(KF // 2)]
        before += [("alpha2", 0)]
        own_keys, tail_keys = [], []
        for who, kind, *at in turn_steps(False, False):
            if kind in ("xi", "z", "B", "C", "dt", "sums"):
                own_keys.append((kind, *at))
            elif kind == "xT":
                own_keys += [("xT", *at, k) for k in range(KD)]
            elif kind == "front":
                own_keys += [("seg", *at, g) for g in range(HP)] + [("X", *at), ("Bt", *at)]
                own_keys += [("S", *at, g) for g in range(HP)]
            elif kind == "back":
                own_keys += [("YI", *at), ("St", *at), ("Y", *at)]
            elif kind == "turn":
                own_keys.append(("YT", *at))
            elif kind == "gn_sum":
                tail_keys.append(("gn",))
            elif kind in ("Wo", "O"):
                tail_keys += [(kind, *at, m) for m in range(NQ // 2)]
            elif kind == "uT":
                tail_keys += [("uT", *at, k) for k in range(KD)]
            elif kind == "H":
                tail_keys += [("H", *at, f) for f in range(KF)]
        full_sems = [sem(f"bank_full{k}") for k in range(BANKS)]
        psum = [ctx.enter_context(nc.psum_tensor(f"bank{k}", [P, 512], F32)) for k in range(BANKS)]
        setup = Ring(psum, full_sems, before, [0] * BANKS)
        own = Ring(psum[:OWN_BANKS], full_sems[:OWN_BANKS], own_keys, setup.each[:OWN_BANKS])
        tail = Ring(psum[OWN_BANKS:], full_sems[OWN_BANKS:], tail_keys, setup.each[OWN_BANKS:])

        masks_zero = sem("masks_zero")
        masks_made = sem("masks_made")
        loaded = sem("loaded")
        w_split = sem("w_split")
        act_set = sem("act_set")
        dve_set = sem("dve_set")
        low_set = sem("low_set")
        wide_set = sem("wide_set")
        a_exp = sem("a_exp")
        stats_seen = sem("stats_seen")
        state_seen = sem("state_seen")
        NCH = NJ * NQ
        x_in = [Signal(sem(f"x_in{j}"), 1, step=16) for j in range(NJ)]
        u_in = [Signal(sem(f"u_in{j}"), 1, step=16) for j in range(NJ)]
        stored = [Signal(sem(f"stored{j}"), 1, step=16) for j in range(NJ)]
        ln_stats = {w: Signal(sem(f"ln_stats_{w}"), NJ * NQ) for w in LNS}
        ln_moments = {w: Signal(sem(f"ln_moments_{w}"), NJ * NQ) for w in LNS}
        ln_eps = {w: Signal(sem(f"ln_eps_{w}"), NJ) for w in LNS}
        ln_rstd = {w: Signal(sem(f"ln_rstd_{w}"), NJ) for w in LNS}
        xn_made = Signal(sem("xn_made"), NJ * NQ)
        xh_hi = Signal(sem("xh_hi"), NJ * KD)
        xh_lo = Signal(sem("xh_lo"), NJ * KD)
        halo = Signal(sem("halo"), NJ)
        xi_out = Signal(sem("xi_out"), NJ * KI)
        tap_out = Signal(sem("tap_out"), NJ * KI)
        conv_out = Signal(sem("conv_out"), NJ * KI * (TAPS - 1))
        xs_out = Signal(sem("xs_out"), NJ * KI)
        zs_out = Signal(sem("zs_out"), NJ * KI)
        sh_hi = Signal(sem("sh_hi"), NJ * KI)
        sh_lo = Signal(sem("sh_lo"), NJ * KI)
        B_out = Signal(sem("B_out"), NJ * KI)
        C_out = Signal(sem("C_out"), NJ * KI)
        DT = 10
        dt_step = Signal(sem("dt_step"), NJ * DT)
        dt_act = Signal(sem("dt_act"), NJ * 2)
        da_seen = Signal(sem("da_seen"), NJ)
        decays_out = Signal(sem("decays_out"), NJ)
        skip_out = Signal(sem("skip_out"), NJ * KI)
        seg_in = Signal(sem("seg_in"), NCH)
        seg_exp = Signal(sem("seg_exp"), NCH * HP)
        mt_out = Signal(sem("mt_out"), NCH * HP)
        xdt_out = Signal(sem("xdt_out"), NCH)
        xdw_out = Signal(sem("xdw_out"), NCH)
        bt_out = Signal(sem("bt_out"), NCH)
        yk_part = Signal(sem("yk_part"), NCH)
        yk_out = Signal(sem("yk_out"), NCH)
        st_zero = Signal(sem("st_zero"), 1)
        st_scaled = Signal(sem("st_scaled"), NCH)
        st_out = Signal(sem("st_out"), NCH * HP)
        yT_out = Signal(sem("yT_out"), NCH)
        gn_st = Signal(sem("gn_st"), NJ * KI)
        gn_mo = Signal(sem("gn_mo"), KI)
        gn_step = Signal(sem("gn_step"), 8)
        gn_rs = Signal(sem("gn_rs"), 1)
        yn_out = Signal(sem("yn_out"), NJ * KI)
        g_out = Signal(sem("g_out"), NJ * KI)
        mid_out = Signal(sem("mid_out"), NJ * NQ)
        u_out = Signal(sem("u_out"), NJ * NQ)
        un_out = Signal(sem("un_out"), NJ * NQ)
        uh_hi = Signal(sem("uh_hi"), NJ * KD)
        uh_lo = Signal(sem("uh_lo"), NJ * KD)
        hf_out = Signal(sem("hf_out"), NJ * KF)
        hh_hi = Signal(sem("hh_hi"), NJ * KF)
        hh_lo = Signal(sem("hh_lo"), NJ * KF)
        y2_scaled = Signal(sem("y2_scaled"), NJ * NQ // 2)
        y2_out = Signal(sem("y2_out"), NJ * NQ // 2)
        y2_norm = Signal(sem("y2_norm"), NJ * NQ)
        o_out = Signal(sem("o_out"), NJ * NQ)

        x_v = x.rearrange("b (j q p) d -> b j p q d", j=NJ, p=P)
        out_v = out.rearrange("b (j q p) d -> b j p q d", j=NJ, p=P)
        NLOADS = 16 + HP
        DVE_SETUP, ACT_SETUP = 6, KI // 2 + 2 * KD + KF // 2

        def ch(j, q):
            return j * NQ + q

        def per_head(ap):
            return ap[:, :, None].to_broadcast([P, HEADS, HD])

        def heads(ap):
            return ap.rearrange("p (h n) -> p h n", h=HEADS)

        def before_block(t, j):
            return (t.ago(1), NJ - 1) if j == 0 else (t, j - 1)

        def two_before(t, n):
            m = (n - 2) % NCH
            return (t.ago(1) if n < 2 else t), m // NQ, m % NQ

        lows = before[:2 * KD + 2 * KI + 1]
        setup.read.update({key: (low_set, n + 1) for n, key in enumerate(lows)})
        setup.read.update({key: (act_set, n + 1) for n, key in enumerate(before[len(lows):-1])})
        tail.read[("gn",)] = gn_step, 3
        for j in range(NJ):
            for k in range(KD):
                own.read[("xT", j, k)] = xh_lo, j * KD + k + 1
                tail.read[("uT", j, k)] = uh_lo, j * KD + k + 1
            for c in range(KI):
                for name, signal in (("xi", tap_out), ("z", zs_out), ("B", B_out), ("C", C_out)):
                    own.read[(name, j, c)] = signal, j * KI + c + 1
            own.read[("dt", j)] = dt_step, j * DT + 1
            own.read[("sums", j)] = decays_out, j + 1
            for q in range(NQ):
                n = ch(j, q)
                for name, signal in (("X", xdt_out), ("Bt", bt_out), ("YI", yk_part), ("Y", yk_out), ("YT", yT_out)):
                    own.read[(name, j, q)] = signal, n + 1
                own.read[("St", j, q)] = st_out, (n + 1) * HP
                for g in range(HP):
                    own.read[("seg", j, q, g)] = seg_exp, n * HP + g + 1
                    own.read[("S", j, q, g)] = mt_out, n * HP + g + 1
            for f in range(KF):
                tail.read[("H", j, f)] = hf_out, j * KF + f + 1
            for m in range(NQ // 2):
                tail.read[("Wo", j, m)] = mid_out, j * NQ + 2 * m + 2
                tail.read[("O", j, m)] = y2_scaled, j * NQ // 2 + m + 1

        def run(steps, b, handlers):
            for who, kind, *at in steps:
                if kind in handlers:
                    handlers[kind](Batch(b, {"own": 0, "tail": -1, "next": 1}[who]), *at)

        def all_batches(eng, handlers):
            run([("own", "in_stat", 0), ("own", "in_norm", 0)] + turn_steps(True, False), 0, handlers)
            with eng.Fori(1, NB - 1) as b:
                run(turn_steps(False, False), b, handlers)
            run(turn_steps(False, True), NB - 1, handlers)
            run(last_tail(), NB, handlers)

        block = ctx.enter_context(nc.Block())

        @block.sync
        def _(sp):
            def load(dst, src):
                sp.dma_start(dst, src).then_inc(loaded, 16)

            with nc.allow_non_contiguous_dma(reason="vectors, once"):
                load(Wx_in, Wx.rearrange("(m p) d -> p m d", p=P))
                load(Wz_in, Wz.rearrange("(m p) d -> p m d", p=P))
                load(Wb_in, Wb.rearrange("(m p) d -> p m d", p=P))
                load(Wc_in, Wc.rearrange("(m p) d -> p m d", p=P))
                load(Wdt_in, Wdt)
                load(Wout_in, Wout.rearrange("(m p) d -> p m d", p=P))
                load(w1_in, w1.rearrange("(m p) d -> p m d", p=P))
                load(w2_in, w2.rearrange("(m p) d -> p m d", p=P))
                load(taps[:, :, :], conv_w.rearrange("(c p) o k -> p c (o k)", p=P))
                load(conv_bias[:, :], conv_b.rearrange("(c p) -> p c", p=P))
                load(gnw[:, :], gn_w.rearrange("(c p) -> p c", p=P))
                load(gnb[:, :], gn_b.rearrange("(c p) -> p c", p=P))
                load(b1_col[:, :], b1.rearrange("(c p) -> p c", p=P))
                load(b2_row[:, :], b2.partition_broadcast(P))
                load(bdt_row[:, :], b_dt.partition_broadcast(P))
                load(a_row[:, :], log_a.partition_broadcast(P))
                for g in range(HP):
                    load(skip[g * HD:(g + 1) * HD, :],
                         d_param.rearrange("(c g) -> g c", g=HP)[g].partition_broadcast(HD))
            for j in range(NJ):
                for signal in (x_in[j], u_in[j], stored[j]):
                    signal.prime(sp)

            def rows(view, t, j):
                return view[bass.ds(t.number(), 1), j].rearrange("a p q d -> p (a q) d")

            def load_x(t, j):
                sp.wait_ge(*xn_made.count(t.ago(1), (j + 1) * NQ))
                sp.dma_start(xt[j][:, :, :], rows(x_v, t, j)).then_inc(x_in[j].sem, 16)

            def load_u(t, j):
                sp.wait_ge(*stored[j].count(t.ago(1), 1))
                sp.dma_start(u[j][:, :, :], rows(x_v, t, j)).then_inc(u_in[j].sem, 16)

            def store(t, j):
                sp.wait_ge(*o_out.count(t, (j + 1) * NQ))
                sp.dma_start(rows(out_v, t, j), u[j][:, :, :]).then_inc(stored[j].sem, 16)

            for j in range(NJ):
                load_x(Batch(0), j)
            for j in range(NJ):
                load_u(Batch(0), j)
            for j in range(NJ):
                load_x(Batch(1), j)
            with sp.Fori(1, NB - 1) as b:
                load_x(Batch(b, 1), 0)
                store(Batch(b, -1), 0)
                load_u(Batch(b), 0)
                load_x(Batch(b, 1), 1)
                store(Batch(b, -1), 1)
                load_u(Batch(b), 1)
            for j in range(NJ):
                store(Batch(NB - 1, -1), j)
                load_u(Batch(NB - 1), j)
            for j in range(NJ):
                store(Batch(NB - 1), j)
            for j in range(NJ):
                sp.wait_ge(*stored[j].count(Batch(NB - 1), 1))

        @block.gpsimd
        def _(pool):
            for n, (t, v) in enumerate(((ident, 0.0), (ident_h, 0.0), (upto, 1.0), (upto_h, 1.0), (after, 1.0),
                                        (after_h, 1.0), (future_h, 0.0), (ones, 1.0), (head_mean, 0.0),
                                        (power, -0.5))):
                pool.memset(t[:, :], v).then_inc(masks_zero, 1)
            pool.memset(no_halo[:, :, :], 0.0).then_inc(masks_zero, 1)
            pool.wait_ge(masks_zero, 11)
            for g in range(HP):
                pool.memset(head_mean[g * HD:(g + 1) * HD, g * HD:(g + 1) * HD], 1.0 / HD).then_inc(masks_made, 1)
                pool.wait_ge(masks_made, g + 1)
            for t in (ident, ident_h):
                pool.affine_select(out=t[:, :], in_=t[:, :], compare_op=ALU.not_equal, fill=1.0, base=0,
                                   pattern=[[-1, P]], channel_multiplier=1).then_inc(masks_made, 1)
            for t in (upto, upto_h):
                pool.affine_select(out=t[:, :], in_=t[:, :], compare_op=ALU.is_ge, fill=0.0, base=0,
                                   pattern=[[1, P]], channel_multiplier=-1).then_inc(masks_made, 1)
            for t in (after, after_h):
                pool.affine_select(out=t[:, :], in_=t[:, :], compare_op=ALU.is_ge, fill=0.0, base=-1,
                                   pattern=[[-1, P]], channel_multiplier=1).then_inc(masks_made, 1)
            pool.affine_select(out=future_h[:, :], in_=future_h[:, :], compare_op=ALU.is_ge, fill=MASKED, base=0,
                               pattern=[[1, P]], channel_multiplier=-1).then_inc(masks_made, 1)
            pool.wait_ge(masks_made, 9)
            for s in (*ln_rstd.values(), gn_rs, u_out, o_out, xdw_out, st_zero, st_scaled):
                s.prime(pool)

            def inverse_root(w):
                def step(t, j):
                    pool.wait_ge(*ln_eps[w].count(t, j + 1))
                    pool.tensor_tensor(rstd[w][:, :], var_eps[w][:, :], power[:, 0:NQ], ALU.pow)\
                        .then_inc(ln_rstd[w].sem, 1)
                return step

            def head_root(t):
                pool.wait_ge(*gn_step.count(t, 5))
                pool.tensor_tensor(gn_rstd[:, :], gn_var[:, :], power[:, 0:KI], ALU.pow).then_inc(gn_rs.sem, 1)

            def add_input(t, j):
                pool.wait_ge(*u_in[j].count(t, 1))
                for i in range(NQ):
                    pool.wait_ge(*mid_out.count(t, j * NQ + i + 1))
                    pool.tensor_tensor(u[j][:, i, :], u[j][:, i, :], mn[j][:, i, :], ALU.add).then_inc(u_out.sem, 1)

            def add_middle(t, j):
                for i in range(NQ):
                    pool.wait_ge(*y2_norm.count(t, j * NQ + i + 1))
                    pool.tensor_tensor(u[j][:, i, :], u[j][:, i, :], y2[:, i, :], ALU.add).then_inc(o_out.sem, 1)

            def front(t, j, q):
                n = ch(j, q)
                if n == 0:
                    pool.wait_ge(*own.full(t.ago(1), ("YI", NJ - 1, NQ - 1)))
                    pool.wait_ge(*st_out.count(t.ago(1), NCH * HP))
                    pool.sem_inc(state_seen, 1)
                    pool.memset(state[:, :, :], 0.0).then_inc(st_zero.sem, 1)
                pool.wait_ge(*xdt_out.count(t, n + 1))
                if q == 0:
                    pool.wait_ge(*decays_out.count(t, j + 1))
                s, sj, sq = two_before(t, n)
                pool.wait_ge(*own.full(s, ("St", sj, sq)))
                pool.tensor_tensor(xdw[n % 2][:, :, :], xdt[n % 2][:, :, :], per_head(decays[:, 1, q, :]), ALU.mult)\
                    .then_inc(xdw_out.sem, 1)

            def back(t, j, q):
                n = ch(j, q)
                pool.wait_ge(*own.full(t, ("YI", j, q)))
                if n == 0:
                    pool.wait_ge(*st_zero.count(t, 1))
                else:
                    pool.wait_ge(*st_out.count(t, n * HP))
                st = state[:, :, :].rearrange("p c (g n) -> p (c g) n", g=HP)
                pool.tensor_tensor(st, st, per_head(decays[:, 2, q, :]), ALU.mult).then_inc(st_scaled.sem, 1)

            all_batches(pool, {
                "in_stat": inverse_root("in"), "mid_stat": inverse_root("mid"), "ff_stat": inverse_root("ff"),
                "end_stat": inverse_root("end"), "gn_root": head_root, "mid_norm": add_input,
                "end_norm": add_middle, "front": front, "back": back})

        @block.scalar
        def _(act):

            def high_half(dst, key):
                act.wait_ge(*setup.full(None, key))
                nc.scalar.activation(dst, setup.bank(key)[:, :], ACT.Copy, scale=SW).then_inc(w_split, 1)

            for k in range(KD):
                high_half(WxT[0][:, k, :], ("Wx", k))
            for k in range(KD):
                high_half(WzT[0][:, k, :], ("Wz", k))
            for k in range(KI):
                high_half(WbT[0][:, k, :], ("Wb", k))
            for k in range(KI):
                high_half(WcT[0][:, k, :], ("Wc", k))
            act.wait_ge(*setup.full(None, ("Wdt", 0)))
            nc.scalar.activation(WdtT[0][:, :, :], setup.bank(("Wdt", 0))[:, 0:KI * HEADS].rearrange("p (k h) -> p k h", k=KI),
                                 ACT.Copy, scale=SW).then_inc(w_split, 1)
            for k in range(KI // 2):
                act.wait_ge(*setup.full(None, ("Wout", k)))
                nc.scalar.activation(WoutT[:, 2 * k:2 * k + 2, :], setup.bank(("Wout", k))[:, :].rearrange("p (k n) -> p k n", k=2),
                                     ACT.Copy).then_inc(act_set, 1)
            for k in range(KD):
                for m in range(2):
                    act.wait_ge(*setup.full(None, ("w1", k, m)))
                    nc.scalar.activation(sign1T[:, k, m * 512:(m + 1) * 512], setup.bank(("w1", k, m))[:, :],
                                         ACT.Sign).then_inc(act_set, 1)
            for f in range(KF // 2):
                act.wait_ge(*setup.full(None, ("w2", f)))
                nc.scalar.activation(sign2T[:, 2 * f:2 * f + 2, :], setup.bank(("w2", f))[:, :].rearrange("p (k n) -> p k n", k=2),
                                     ACT.Sign).then_inc(act_set, 1)
            act.wait_ge(loaded, 16 * NLOADS)
            nc.scalar.activation(a_row[:, :], a_row[:, :], ACT.Exp).then_inc(a_exp, 1)
            act.wait_ge(masks_zero, 11)
            act.wait_ge(dve_set, DVE_SETUP)
            for s in (xh_hi, halo, xi_out, tap_out, xs_out, zs_out, sh_hi, C_out, dt_act, decays_out, skip_out, seg_exp,
                      bt_out, yk_part, yn_out, uh_hi, hf_out):
                s.prime(act)

            def input_high(t, j):
                s, sj = before_block(t, j)
                for k in range(KD):
                    for full in latest(own.full(t, ("xT", j, k)), own.full(s, ("z", sj, KI - 1))):
                        act.wait_ge(*full)
                    nc.scalar.activation(xh[0][:, k, :], own.bank(("xT", j, k))[:, :], ACT.Copy).then_inc(xh_hi.sem, 1)

            def project_x(t, j, c):
                s, sj = before_block(t, j)
                if c == 0:
                    act.wait_ge(*conv_out.count(s, (sj + 1) * KI * (TAPS - 1)))
                    act.wait_ge(*xi_out.count(s, (sj + 1) * KI))
                    nc.scalar.activation(xi[:, :, 0:HALO], xi[:, :, BLK:BLK + HALO] if j else no_halo[:, :, :], ACT.Copy)\
                        .then_inc(halo.sem, 1)
                    act.wait_ge(*halo.count(t, j + 1))
                act.wait_ge(*own.full(t, ("xi", j, c)))
                nc.scalar.activation(xi[:, c, HALO:HALO + BLK], own.bank(("xi", j, c))[:, :], ACT.Copy,
                                     scale=1.0 / SW).then_inc(xi_out.sem, 1)
                if c == 0:
                    act.wait_ge(*own.full(s, ("X", sj, NQ - 1)))
                    act.wait_ge(*sh_lo.count(s, (sj + 1) * KI))
                    act.wait_ge(*skip_out.count(s, (sj + 1) * KI))
                nc.scalar.activation(xs[:, c, :], own.bank(("xi", j, c))[:, :], ACT.Identity, bias=conv_bias[:, c:c + 1],
                                     scale=last_tap[:, c:c + 1]).then_inc(tap_out.sem, 1)

            def gate_silu(t, j, c):
                if c == 0:
                    act.wait_ge(*g_out.count(t.ago(1), (j + 1) * KI))
                act.wait_ge(*own.full(t, ("z", j, c)))
                nc.scalar.activation(zs[:, c, j * BLK:(j + 1) * BLK], own.bank(("z", j, c))[:, :], ACT.Silu,
                                     scale=1.0 / SW).then_inc(zs_out.sem, 1)

            def x_silu(t, j, c):
                act.wait_ge(*conv_out.count(t, (j * KI + c + 1) * (TAPS - 1)))
                nc.scalar.activation(xs[:, c, :], xs[:, c, :], ACT.Silu).then_inc(xs_out.sem, 1)

            def x_high(t, j, c):
                act.wait_ge(*xs_out.count(t, j * KI + c + 1))
                if c == 0:
                    s, sj = before_block(t, j)
                    act.wait_ge(*own.full(s, ("C", sj, KI - 1)))
                nc.scalar.activation(sh[0][:, c, :], xs[:, c, :], ACT.Copy, scale=SX).then_inc(sh_hi.sem, 1)

            def step_exp(t, j):
                act.wait_ge(*dt_step.count(t, j * DT + 2))
                nc.scalar.activation(exp_v[:, :, :], abs_v[:, :, :], ACT.Exp, scale=-1.0).then_inc(dt_act.sem, 1)

            def step_log(t, j):
                act.wait_ge(*dt_step.count(t, j * DT + 3))
                nc.scalar.activation(log_u[:, :, :], one_e[:, :, :], ACT.Ln).then_inc(dt_act.sem, 1)

            def skip_term(t, j):
                act.wait_ge(*xs_out.count(t, (j + 1) * KI))
                act.wait_ge(*tail.full(t.ago(1), ("Wo", j, NQ // 2 - 1)))
                for c in range(KI):
                    nc.scalar.activation(yT[:, c, j * BLK:(j + 1) * BLK], xs[:, c, :], ACT.Copy,
                                         scale=skip[:, c:c + 1]).then_inc(skip_out.sem, 1)

            def project_c(t, j, c):
                s, sj = before_block(t, j)
                for full in latest(own.full(t, ("C", j, c)), own.full(s, ("YI", sj, NQ - 1))):
                    act.wait_ge(*full)
                nc.scalar.activation(CT[:, c, :], own.bank(("C", j, c))[:, :], ACT.Copy, scale=1.0 / (SW * SX))\
                    .then_inc(C_out.sem, 1)

            def decay_exp(t, j):
                act.wait_ge(*own.full(t, ("sums", j)))
                s, sj = before_block(t, j)
                act.wait_ge(*st_scaled.count(s, (sj + 1) * NQ))
                act.wait_ge(*yk_part.count(s, (sj + 1) * NQ))
                nc.scalar.activation(decays[:, :, :, :].rearrange("p a q h -> p (a q h)"),
                                     own.bank(("sums", j))[:, 0:3 * NQ * HEADS], ACT.Exp).then_inc(decays_out.sem, 1)

            def front(t, j, q):
                n = ch(j, q)
                s, sj, sq = two_before(t, n)
                for g in range(HP):
                    for full in latest(own.full(t, ("seg", j, q, g)), own.full(s, ("Y", sj, sq))):
                        act.wait_ge(*full)
                    nc.scalar.activation(mt[n % 2][:, g].rearrange("p c t -> p (c t)"),
                                         own.bank(("seg", j, q, g))[:, :], ACT.Exp).then_inc(seg_exp.sem, 1)
                act.wait_ge(*own.full(t, ("Bt", j, q)))
                nc.scalar.activation(bt[n % 2][:, :], own.bank(("Bt", j, q))[:, :], ACT.Copy).then_inc(bt_out.sem, 1)

            def back(t, j, q):
                n = ch(j, q)
                s, sj, sq = two_before(t, n)
                act.wait_ge(*decays_out.count(t, j + 1))
                for full in latest(own.full(t, ("YI", j, q)), own.full(s, ("YT", sj, sq))):
                    act.wait_ge(*full)
                for h in range(HEADS):
                    last = nc.scalar.activation(yk[n % 2][:, h, :], own.bank(("YI", j, q))[:, h * HD:(h + 1) * HD],
                                                ACT.Copy, scale=decays[:, 0, q, h:h + 1])
                last.then_inc(yk_part.sem, 1)

            def head_normalise(t, j):
                act.wait_ge(*gn_step.count(t, 8))
                for c in range(KI):
                    v = yT[:, c, j * BLK:(j + 1) * BLK]
                    nc.scalar.activation(v, v, ACT.Identity, bias=gn_shift[:, c:c + 1],
                                         scale=gn_scale[:, c:c + 1]).then_inc(yn_out.sem, 1)

            def middle_high(t, j):
                s, sj = before_block(t, j)
                for k in range(KD):
                    for full in latest(tail.full(t, ("uT", j, k)), tail.full(s, ("H", sj, KF - 1))):
                        act.wait_ge(*full)
                    nc.scalar.activation(uh[0][:, k, :], tail.bank(("uT", j, k))[:, :], ACT.Copy).then_inc(uh_hi.sem, 1)

            def hidden(t, j):
                for f in range(KF):
                    n = j * KF + f
                    act.wait_ge(*tail.full(t, ("H", j, f)))
                    act.wait_ge(*hh_lo.count(t, n - 1))
                    nc.scalar.activation(hf[f % 2][:, :], tail.bank(("H", j, f))[:, :], ACT.Gelu,
                                         bias=b1_col[:, f:f + 1], scale=alpha1[:, f:f + 1]).then_inc(hf_out.sem, 1)

            all_batches(act, {
                "xT": input_high, "xi": project_x, "z": gate_silu, "silu": x_silu, "xs": x_high, "dt": step_exp,
                "log": step_log, "skip": skip_term, "C": project_c, "sums": decay_exp, "front": front, "back": back,
                "gate": head_normalise, "uT": middle_high, "H": hidden})

        @block.vector
        def _(dve):
            halves = {"Wx": WxT, "Wz": WzT, "Wb": WbT, "Wc": WcT}
            for n, key in enumerate(lows[:-1]):
                w, k = halves[key[0]], key[1]
                dve.wait_ge(w_split, n + 1)
                nc.vector.scalar_tensor_tensor(out=w[1][:, k, :], in0=setup.bank(key)[:, :], scalar=SW,
                                               in1=w[0][:, k, :], op0=ALU.mult, op1=ALU.subtract)\
                    .then_inc(low_set, 1)
            dve.wait_ge(w_split, len(lows))
            nc.vector.scalar_tensor_tensor(out=WdtT[1][:, :, :], in0=setup.bank(("Wdt", 0))[:, 0:KI * HEADS]
                                           .rearrange("p (k h) -> p k h", k=KI), scalar=SW, in1=WdtT[0][:, :, :],
                                           op0=ALU.mult, op1=ALU.subtract).then_inc(low_set, 1)
            dve.wait_ge(loaded, 16 * NLOADS)
            nc.vector.tensor_reduce(alpha1[:, :], w1_in, AX_X, ALU.add, apply_absolute_value=True).then_inc(dve_set, 1)
            nc.vector.tensor_reduce(alpha2[:, :], w2_in, AX_X, ALU.add, apply_absolute_value=True).then_inc(dve_set, 1)
            nc.vector.tensor_scalar(last_tap[:, :], taps[:, :, TAPS - 1], 1.0 / SW, None, ALU.mult).then_inc(dve_set, 1)
            dve.wait_ge(dve_set, 2)
            nc.vector.tensor_scalar(alpha1[:, :], alpha1[:, :], 1.0 / D, None, ALU.mult).then_inc(dve_set, 1)
            dve.wait_ge(masks_zero, 11)
            for k in range(KD):
                nc.vector.tensor_scalar(alpha2_wide[k], ones[:, :], alpha2[:, k:k + 1], 1.0 / (FF * SG),
                                        ALU.mult, ALU.mult).then_inc(wide_set, 1)
            dve.wait_ge(*setup.full(None, ("alpha2", 0)))
            nc.vector.tensor_copy(alpha2_row[:, :], setup.bank(("alpha2", 0))[:, 0:D]).then_inc(dve_set, 1)
            dve.wait_ge(a_exp, 1)
            nc.vector.tensor_scalar(a_row[:, :], a_row[:, :], -1.0, None, ALU.mult).then_inc(dve_set, 1)
            dve.wait_ge(dve_set, DVE_SETUP)
            dve.wait_ge(low_set, 2 * KD + 2 * KI + 1)
            for s in (*ln_stats.values(), *ln_moments.values(), *ln_eps.values(), xn_made, xh_lo, conv_out, sh_lo, B_out,
                      dt_step, da_seen, seg_in, mt_out, xdt_out, yk_out, st_out, yT_out, gn_st, gn_mo, gn_step, g_out,
                      mid_out, un_out, uh_lo, hh_hi, hh_lo, y2_scaled, y2_out, y2_norm):
                s.prime(dve)

            def statistics(w, t, j, tile, ready):
                for i in range(NQ):
                    ready(i)
                    nc.vector.bn_stats(stats[w][:, i, :], tile(i)).then_inc(ln_stats[w].sem, 1)
                dve.wait_ge(*ln_stats[w].count(t, (j + 1) * NQ))
                dve.sem_inc(stats_seen, 1)
                for i in range(NQ):
                    nc.vector.bn_aggr(moments[w][:, i, :], stats[w][:, i, :]).then_inc(ln_moments[w].sem, 1)
                dve.wait_ge(*ln_moments[w].count(t, (j + 1) * NQ))
                dve.wait_ge(*ln_rstd[w].count(t, j))
                nc.vector.tensor_scalar(var_eps[w][:, :], moments[w][:, :, 1], EPS, None, ALU.add)\
                    .then_inc(ln_eps[w].sem, 1)

            def normal(w, t, j, dst, src, i):
                if i == 0:
                    dve.wait_ge(*ln_rstd[w].count(t, j + 1))
                return nc.vector.tensor_scalar(dst, src, moments[w][:, i, 0:1], rstd[w][:, i:i + 1],
                                               ALU.subtract, ALU.mult)

            def input_stats(t, j):
                statistics("in", t, j, lambda i: xt[j][:, i, :],
                           lambda i: dve.wait_ge(*x_in[j].count(t, 1)) if i == 0 else None)

            def input_norm(t, j):
                s, sj = before_block(t, j)
                dve.wait_ge(*own.full(s, ("xT", sj, KD - 1)))
                for i in range(NQ):
                    normal("in", t, j, xn[:, i, :], xt[j][:, i, :], i).then_inc(xn_made.sem, 1)

            def input_low(t, j):
                for k in range(KD):
                    dve.wait_ge(*xh_hi.count(t, j * KD + k + 1))
                    nc.vector.tensor_tensor(xh[1][:, k, :], own.bank(("xT", j, k))[:, :], xh[0][:, k, :],
                                            ALU.subtract).then_inc(xh_lo.sem, 1)

            def convolve(t, j, c):
                dve.wait_ge(*tap_out.count(t, j * KI + c + 1))
                dve.wait_ge(*xi_out.count(t, j * KI + c + 1))
                for k in range(TAPS - 1):
                    if k:
                        dve.wait_ge(*conv_out.count(t, (j * KI + c) * (TAPS - 1) + k))
                    nc.vector.scalar_tensor_tensor(out=xs[:, c, :], in0=xi[:, c, k:k + BLK], scalar=taps[:, c, k:k + 1],
                                                   in1=xs[:, c, :], op0=ALU.mult, op1=ALU.add).then_inc(conv_out.sem, 1)

            def x_low(t, j, c):
                dve.wait_ge(*sh_hi.count(t, j * KI + c + 1))
                nc.vector.scalar_tensor_tensor(out=sh[1][:, c, :], in0=xs[:, c, :], scalar=SX, in1=sh[0][:, c, :],
                                               op0=ALU.mult, op1=ALU.subtract).then_inc(sh_lo.sem, 1)

            def step_in(t, j):
                dve.wait_ge(*own.full(t, ("dt", j)))
                nc.vector.scalar_tensor_tensor(
                    out=v_dt[:, :, :], in0=own.bank(("dt", j))[:, 0:NQ * HEADS].rearrange("p (q h) -> p q h", q=NQ),
                    scalar=1.0 / (SW * SX), in1=bdt_row[:, None, :].to_broadcast([P, NQ, HEADS]), op0=ALU.mult,
                    op1=ALU.add).then_inc(dt_step.sem, 1)
                dve.wait_ge(*dt_step.count(t, j * DT + 1))
                nc.vector.scalar_tensor_tensor(out=abs_v[:, :, :], in0=v_dt[:, :, :], scalar=-1.0, in1=v_dt[:, :, :],
                                               op0=ALU.mult, op1=ALU.max).then_inc(dt_step.sem, 1)

            def step_mid(t, j):
                s = j * DT
                dve.wait_ge(*dt_act.count(t, j * 2 + 1))
                nc.vector.tensor_scalar(one_e[:, :, :], exp_v[:, :, :], 1.0, None, ALU.add).then_inc(dt_step.sem, 1)
                dve.wait_ge(*dt_step.count(t, s + 3))
                nc.vector.tensor_scalar(e_back[:, :, :], one_e[:, :, :], 1.0, None, ALU.subtract).then_inc(dt_step.sem, 1)
                dve.wait_ge(*dt_step.count(t, s + 4))
                nc.vector.tensor_tensor(e_rest[:, :, :], exp_v[:, :, :], e_back[:, :, :], ALU.subtract)\
                    .then_inc(dt_step.sem, 1)

            def step_out(t, j):
                s = j * DT
                dve.wait_ge(*dt_act.count(t, j * 2 + 2))
                nc.vector.scalar_tensor_tensor(out=dt_raw[:, :, :], in0=v_dt[:, :, :], scalar=0.0, in1=log_u[:, :, :],
                                               op0=ALU.max, op1=ALU.add).then_inc(dt_step.sem, 1)
                dve.wait_ge(*dt_step.count(t, s + 6))
                nc.vector.tensor_tensor(dt_t[:, :, :], dt_raw[:, :, :], e_rest[:, :, :], ALU.add).then_inc(dt_step.sem, 1)
                dve.wait_ge(*dt_step.count(t, s + 7))
                nc.vector.tensor_tensor(da_raw[:, :, :], dt_t[:, :, :], a_row[:, None, :].to_broadcast([P, NQ, HEADS]),
                                        ALU.mult).then_inc(da_seen.sem, 1)
                dve.wait_ge(*da_seen.count(t, j + 1))
                p, pj = before_block(t, j)
                dve.wait_ge(*own.full(p, ("sums", pj)))
                nc.vector.tensor_scalar(da[:, :, :], da_raw[:, :, :], DECAY_FLOOR, None, ALU.max).then_inc(dt_step.sem, 1)
                dve.wait_ge(*dt_step.count(t, s + 8))
                nc.vector.tensor_copy(da_hi[:, :, :], da[:, :, :]).then_inc(dt_step.sem, 1)
                dve.wait_ge(*dt_step.count(t, s + 9))
                nc.vector.tensor_tensor(da_lo[:, :, :], da[:, :, :], da_hi[:, :, :], ALU.subtract).then_inc(dt_step.sem, 1)

            def project_b(t, j, c):
                s, sj = before_block(t, j)
                for full in latest(own.full(t, ("B", j, c)), own.full(s, ("S", sj, NQ - 1, HP - 1))):
                    dve.wait_ge(*full)
                nc.vector.tensor_scalar(BT[:, c, :], own.bank(("B", j, c))[:, :], 1.0 / (SW * SX), None, ALU.mult)\
                    .then_inc(B_out.sem, 1)

            def segments(t, j, q):
                n = ch(j, q)
                if q == 0:
                    dve.wait_ge(*dt_step.count(t, (j + 1) * DT))
                s, sj, sq = two_before(t, n)
                dve.wait_ge(*own.full(s, ("seg", sj, sq, HP - 1)))
                for i, part in enumerate((da_hi, da_lo)):
                    for h in range(HEADS):
                        last = nc.vector.tensor_scalar(seg[i][n % 2][:, h % HP, h // HP, :], upto_h[:, :],
                                                       part[:, q, h:h + 1], None, ALU.mult)
                last.then_inc(seg_in.sem, 1)

            def front(t, j, q):
                n = ch(j, q)
                r = n % 2
                s, sj, sq = two_before(t, n)
                for full in latest(own.full(t, ("X", j, q)), own.full(s, ("Y", sj, sq))):
                    dve.wait_ge(*full)
                dve.wait_ge(*xdw_out.count(s, ch(sj, sq) + 1))
                nc.vector.tensor_tensor(xdt[r][:, :, :], heads(own.bank(("X", j, q))[:, :]), per_head(dt_t[:, q, :]),
                                        ALU.mult).then_inc(xdt_out.sem, 1)
                for g in range(HP):
                    dve.wait_ge(*own.full(t, ("S", j, q, g)))
                    dve.wait_ge(*seg_exp.count(t, n * HP + g + 1))
                    v = mt[r][:, g].rearrange("p c t -> p (c t)")
                    nc.vector.tensor_tensor(v, own.bank(("S", j, q, g))[:, :], v, ALU.mult).then_inc(mt_out.sem, 1)

            def back(t, j, q):
                n = ch(j, q)
                dve.wait_ge(*own.full(t, ("St", j, q)))
                dve.wait_ge(*st_scaled.count(t, n + 1))
                for g in range(HP):
                    rows = slice(g * HD, (g + 1) * HD)
                    v = state[rows, :, g * HD:(g + 1) * HD]
                    nc.vector.tensor_tensor(
                        v, v, own.bank(("St", j, q))[rows, :].rearrange("p (c n) -> p c n", c=KI)[:, :, g * HD:(g + 1) * HD],
                        ALU.add).then_inc(st_out.sem, 1)
                dve.wait_ge(*own.full(t, ("Y", j, q)))
                dve.wait_ge(*yk_part.count(t, n + 1))
                nc.vector.tensor_tensor(yk[n % 2][:, :, :], yk[n % 2][:, :, :], heads(own.bank(("Y", j, q))[:, :]),
                                        ALU.add).then_inc(yk_out.sem, 1)

            def turn(t, j, q):
                n = ch(j, q)
                dve.wait_ge(*own.full(t, ("YT", j, q)))
                dve.wait_ge(*skip_out.count(t, (j + 1) * KI))
                v = yT[:, :, n * P:(n + 1) * P]
                nc.vector.tensor_tensor(v, own.bank(("YT", j, q))[:, :].rearrange("p (c t) -> p c t", c=KI), v,
                                        ALU.add).then_inc(yT_out.sem, 1)

            def head_stats(t, j):
                dve.wait_ge(*yT_out.count(t, (j + 1) * NQ))
                for c in range(KI):
                    nc.vector.bn_stats(gn_stats[:, c, j, :], yT[:, c, j * BLK:(j + 1) * BLK]).then_inc(gn_st.sem, 1)

            def head_moments(t):
                dve.wait_ge(*gn_st.count(t, NJ * KI))
                dve.sem_inc(stats_seen, 1)
                for c in range(KI):
                    nc.vector.bn_aggr(gn_mom[:, c, :], gn_stats[:, c, :, :].rearrange("p j s -> p (j s)"))\
                        .then_inc(gn_mo.sem, 1)
                dve.wait_ge(*gn_mo.count(t, KI))
                nc.vector.tensor_tensor(gn_sq[:, :], gn_mom[:, :, 0], gn_mom[:, :, 0], ALU.mult).then_inc(gn_step.sem, 1)
                dve.wait_ge(*gn_step.count(t, 1))
                nc.vector.tensor_tensor(gn_mom[:, :, 1], gn_mom[:, :, 1], gn_sq[:, :], ALU.add).then_inc(gn_step.sem, 1)

            def head_variance(t):
                dve.wait_ge(*tail.full(t, ("gn",)))
                nc.vector.tensor_copy(gn_head[:, :, :], tail.bank(("gn",))[:, 0:2 * KI].rearrange("p (c s) -> p c s", s=2))\
                    .then_inc(gn_step.sem, 1)
                dve.wait_ge(*gn_step.count(t, 3))
                nc.vector.tensor_tensor(gn_msq[:, :], gn_head[:, :, 0], gn_head[:, :, 0], ALU.mult)\
                    .then_inc(gn_step.sem, 1)
                dve.wait_ge(*gn_step.count(t, 4))
                nc.vector.scalar_tensor_tensor(out=gn_var[:, :], in0=gn_head[:, :, 1], scalar=EPS, in1=gn_msq[:, :],
                                               op0=ALU.add, op1=ALU.subtract).then_inc(gn_step.sem, 1)

            def head_fold(t):
                dve.wait_ge(*gn_rs.count(t, 1))
                nc.vector.tensor_tensor(gn_scale[:, :], gn_rstd[:, :], gnw[:, :], ALU.mult).then_inc(gn_step.sem, 1)
                dve.wait_ge(*gn_step.count(t, 6))
                nc.vector.tensor_tensor(gn_ms[:, :], gn_head[:, :, 0], gn_scale[:, :], ALU.mult).then_inc(gn_step.sem, 1)
                dve.wait_ge(*gn_step.count(t, 7))
                nc.vector.tensor_tensor(gn_shift[:, :], gnb[:, :], gn_ms[:, :], ALU.subtract).then_inc(gn_step.sem, 1)

            def gate(t, j):
                for c in range(KI):
                    dve.wait_ge(*yn_out.count(t, j * KI + c + 1))
                    v = yT[:, c, j * BLK:(j + 1) * BLK]
                    nc.vector.tensor_tensor(v, v, zs[:, c, j * BLK:(j + 1) * BLK], ALU.mult).then_inc(g_out.sem, 1)

            def attention_tile(j, i):
                return tail.bank(("Wo", j, i // 2))[:, (i % 2) * D:(i % 2 + 1) * D]

            def middle_stats(t, j):
                statistics("mid", t, j, lambda i: attention_tile(j, i),
                           lambda i: dve.wait_ge(*tail.full(t, ("Wo", j, i // 2))))

            def middle_norm(t, j):
                if j == 0:
                    dve.wait_ge(*tail.full(t.ago(1), ("uT", NJ - 1, KD - 1)))
                else:
                    dve.wait_ge(*o_out.count(t.ago(1), NJ * NQ))
                for i in range(NQ):
                    normal("mid", t, j, mn[j][:, i, :], attention_tile(j, i), i).then_inc(mid_out.sem, 1)

            def ff_stats(t, j):
                statistics("ff", t, j, lambda i: u[j][:, i, :],
                           lambda i: dve.wait_ge(*u_out.count(t, j * NQ + i + 1)))

            def ff_norm(t, j):
                if j:
                    dve.wait_ge(*tail.full(t, ("uT", j - 1, KD - 1)))
                for i in range(NQ):
                    normal("ff", t, j, un[:, i, :], u[j][:, i, :], i).then_inc(un_out.sem, 1)

            def middle_low(t, j):
                for k in range(KD):
                    dve.wait_ge(*uh_hi.count(t, j * KD + k + 1))
                    nc.vector.tensor_tensor(uh[1][:, k, :], tail.bank(("uT", j, k))[:, :], uh[0][:, k, :],
                                            ALU.subtract).then_inc(uh_lo.sem, 1)

            def hidden_split(t, j):
                for f in range(KF):
                    n = j * KF + f
                    dve.wait_ge(*hf_out.count(t, n + 1))
                    if f == 0:
                        s, sj = before_block(t, j)
                        dve.wait_ge(*tail.full(s, ("O", sj, NQ // 2 - 1)))
                    nc.vector.tensor_scalar(hh[0][:, f, :], hf[f % 2][:, :], SG, None, ALU.mult).then_inc(hh_hi.sem, 1)
                    dve.wait_ge(*hh_hi.count(t, n + 1))
                    nc.vector.scalar_tensor_tensor(out=hh[1][:, f, :], in0=hf[f % 2][:, :], scalar=SG,
                                                   in1=hh[0][:, f, :], op0=ALU.mult, op1=ALU.subtract)\
                        .then_inc(hh_lo.sem, 1)

            def ffn_out(t, j):
                dve.wait_ge(*(o_out.count(t, NQ) if j else u_out.count(t, NJ * NQ)))
                for m in range(NQ // 2):
                    n = j * NQ // 2 + m
                    v = y2[:, 2 * m:2 * m + 2, :]
                    dve.wait_ge(*tail.full(t, ("O", j, m)))
                    nc.vector.tensor_tensor(v, tail.bank(("O", j, m))[:, :].rearrange("p (i d) -> p i d", i=2),
                                            alpha2_row[:, None, :].to_broadcast([P, 2, D]), ALU.mult)\
                        .then_inc(y2_scaled.sem, 1)
                    dve.wait_ge(*y2_scaled.count(t, n + 1))
                    nc.vector.tensor_tensor(v, v, b2_row[:, None, :].to_broadcast([P, 2, D]), ALU.add)\
                        .then_inc(y2_out.sem, 1)

            def end_stats(t, j):
                statistics("end", t, j, lambda i: y2[:, i, :],
                           lambda i: dve.wait_ge(*y2_out.count(t, j * NQ // 2 + i // 2 + 1)))

            def end_norm(t, j):
                for i in range(NQ):
                    normal("end", t, j, y2[:, i, :], y2[:, i, :], i).then_inc(y2_norm.sem, 1)

            all_batches(dve, {
                "in_stat": input_stats, "in_norm": input_norm, "xT": input_low, "xi": convolve, "xs": x_low,
                "dt": step_in, "log": step_mid, "decay": step_out, "B": project_b, "seg": segments, "front": front,
                "back": back, "turn": turn, "head_stat": head_stats, "gn_sum": head_moments, "gn_root": head_variance,
                "gn_fold": head_fold, "gate": gate, "mid_stat": middle_stats, "mid_norm": middle_norm,
                "ff_stat": ff_stats, "ff_norm": ff_norm, "uT": middle_low, "H": hidden_split, "O": ffn_out,
                "end_stat": end_stats, "end_norm": end_norm})

        @block.tensor
        def _(pe):
            pe.wait_ge(masks_made, 9)
            pe.wait_ge(masks_zero, 11)
            pe.wait_ge(loaded, 16 * NLOADS)

            def turn_weights(key, parts, id_=None):
                if setup.place[key][1]:
                    pe.wait_ge(*setup.empty(None, key))
                for n, part in enumerate(parts):
                    rows, w = part.shape[0], setup.bank(key)
                    mm = nc.tensor.transpose(w[:, n * rows:(n + 1) * rows], part, ident[0:rows, 0:rows])
                mm.then_inc(setup.full_sem(key), 1)

            def cols(k):
                return slice(k * P, (k + 1) * P)

            for name, w in (("Wx", Wx_in), ("Wz", Wz_in)):
                for k in range(KD):
                    turn_weights((name, k), [w[:, m, cols(k)] for m in range(KI)])
            for name, w in (("Wb", Wb_in), ("Wc", Wc_in)):
                for k in range(KI):
                    turn_weights((name, k), [w[:, m, cols(k)] for m in range(KI)])
            turn_weights(("Wdt", 0), [Wdt_in[:, cols(k)] for k in range(KI)])
            for k in range(KI // 2):
                turn_weights(("Wout", k), [Wout_in[:, m, cols(2 * k + kk)] for kk in range(2) for m in range(KD)])
            for k in range(KD):
                for h in range(2):
                    turn_weights(("w1", k, h), [w1_in[:, 4 * h + m, cols(k)] for m in range(4)])
            for f in range(KF // 2):
                turn_weights(("w2", f), [w2_in[:, m, cols(2 * f + ff)] for ff in range(2) for m in range(KD)])
            pe.wait_ge(wide_set, KD)
            pe.wait_ge(*setup.empty(None, ("alpha2", 0)))
            for k in range(KD):
                mm = nc.tensor.matmul(setup.bank(("alpha2", 0))[:, cols(k)], alpha2_wide[k], ident[:, :], start=True, stop=True)
            mm.then_inc(setup.full_sem(("alpha2", 0)), 1)
            pe.wait_ge(dve_set, DVE_SETUP)
            pe.wait_ge(low_set, 2 * KD + 2 * KI + 1)
            pe.wait_ge(act_set, ACT_SETUP)
            own.prime(pe)
            tail.prime(pe)

            def split_product(t, key, w, v, n, m):
                pe.wait_ge(*own.empty(t, key))
                terms = [(k, i, h) for k in range(n) for i, h in ((0, 0), (1, 0), (0, 1))]
                for a, (k, i, h) in enumerate(terms):
                    mm = nc.tensor.matmul(own.bank(key)[:, :], w[i][:, k, cols(m)], v[h][:, k, :], start=(a == 0),
                                          stop=(a == len(terms) - 1))
                mm.then_inc(own.full_sem(key), 1)

            def turn_tokens(t, ring, name, j, src, made):
                for k in range(KD):
                    key = (name, j, k)
                    pe.wait_ge(*ring.empty(t, key))
                    for i in range(NQ):
                        if k == 0:
                            pe.wait_ge(*made.count(t, j * NQ + i + 1))
                        mm = nc.tensor.transpose(ring.bank(key)[:, cols(i)], src[:, i, cols(k)], ident[:, :])
                    mm.then_inc(ring.full_sem(key), 1)

            def turn_input(t, j):
                turn_tokens(t, own, "xT", j, xn, xn_made)

            def project_x(t, j, c):
                if c == 0:
                    pe.wait_ge(*xh_lo.count(t, (j + 1) * KD))
                split_product(t, ("xi", j, c), WxT, xh, KD, c)

            def project_z(t, j, c):
                split_product(t, ("z", j, c), WzT, xh, KD, c)

            def step_size(t, j):
                key = ("dt", j)
                for need in latest(own.empty(t, key), sh_lo.count(t, (j + 1) * KI)):
                    pe.wait_ge(*need)
                terms = [(k, i, h) for k in range(KI) for i, h in ((0, 0), (1, 0), (0, 1))]
                for q in range(NQ):
                    for a, (k, i, h) in enumerate(terms):
                        mm = nc.tensor.matmul(own.bank(key)[:, q * HEADS:(q + 1) * HEADS], sh[h][:, k, cols(q)],
                                              WdtT[i][:, k, :], start=(a == 0), stop=(a == len(terms) - 1))
                mm.then_inc(own.full_sem(key), 1)

            def project_b(t, j, c):
                split_product(t, ("B", j, c), WbT, sh, KI, c)

            def project_c(t, j, c):
                split_product(t, ("C", j, c), WcT, sh, KI, c)

            def decay_sums(t, j):
                key = ("sums", j)
                pe.wait_ge(*dt_step.count(t, j * DT + 8))
                pe.wait_ge(*own.empty(t, key))
                for n, w in enumerate((upto, after, ones)):
                    mm = nc.tensor.matmul(own.bank(key)[:, n * NQ * HEADS:(n + 1) * NQ * HEADS], w[:, :],
                                          da[:, :, :].rearrange("p q h -> p (q h)"), start=True, stop=True)
                mm.then_inc(own.full_sem(key), 1)

            def front(t, j, q):
                n = ch(j, q)
                pe.wait_ge(*seg_in.count(t, n + 1))
                for g in range(HP):
                    key = ("seg", j, q, g)
                    pe.wait_ge(*own.empty(t, key))
                    for i in range(2):
                        nc.tensor.matmul(own.bank(key)[:, :], after_h[:, :],
                                         seg[i][n % 2][:, g].rearrange("p c t -> p (c t)"), start=(i == 0), stop=False)
                    nc.tensor.matmul(own.bank(key)[:, :], ident_h[:, :], future_h[:, None, :].to_broadcast([P, KI, P]),
                                     start=False, stop=True).then_inc(own.full_sem(key), 1)
                for name, src in (("X", xs), ("Bt", BT)):
                    key = (name, j, q)
                    for need in latest(own.empty(t, key), B_out.count(t, (j + 1) * KI), C_out.count(t, (j + 1) * KI)):
                        pe.wait_ge(*need)
                    for c in range(KI):
                        mm = nc.tensor.transpose(own.bank(key)[:, cols(c)], src[:, c, cols(q)], ident[:, :])
                    mm.then_inc(own.full_sem(key), 1)
                for g in range(HP):
                    key = ("S", j, q, g)
                    rows = slice(g * NS, (g + 1) * NS)
                    pe.wait_ge(*own.empty(t, key))
                    for c in range(KI):
                        mm = nc.tensor.matmul(own.bank(key)[:, cols(c)], BT[rows, c, cols(q)], CT[rows, c, cols(q)],
                                              start=True, stop=True)
                    mm.then_inc(own.full_sem(key), 1)

            def back(t, j, q):
                n = ch(j, q)
                r = n % 2
                key = ("YI", j, q)
                for need in latest(own.empty(t, key), st_out.count(t, n * HP) if n else st_zero.count(t, 1)):
                    pe.wait_ge(*need)
                for c in range(KI):
                    mm = nc.tensor.matmul(own.bank(key)[:, cols(c)], CT[:, c, cols(q)], state[:, c, :],
                                          start=True, stop=True)
                mm.then_inc(own.full_sem(key), 1)
                key = ("St", j, q)
                for need in latest(own.empty(t, key), bt_out.count(t, n + 1), xdw_out.count(t, n + 1)):
                    pe.wait_ge(*need)
                for c in range(KI):
                    mm = nc.tensor.matmul(own.bank(key)[:, cols(c)], bt[r][:, cols(c)],
                                          xdw[r][:, HP * c:HP * c + HP, :].rearrange("p h n -> p (h n)"),
                                          start=True, stop=True)
                mm.then_inc(own.full_sem(key), 1)
                key = ("Y", j, q)
                for need in latest(own.empty(t, key), mt_out.count(t, (n + 1) * HP)):
                    pe.wait_ge(*need)
                for h in range(HEADS):
                    mm = nc.tensor.matmul(own.bank(key)[:, h * HD:(h + 1) * HD], mt[r][:, h % HP, h // HP, :],
                                          xdt[r][:, h, :], start=True, stop=True)
                mm.then_inc(own.full_sem(key), 1)

            def turn(t, j, q):
                n = ch(j, q)
                key = ("YT", j, q)
                for need in latest(own.empty(t, key), yk_out.count(t, n + 1)):
                    pe.wait_ge(*need)
                for c in range(KI):
                    mm = nc.tensor.transpose(own.bank(key)[:, cols(c)],
                                             yk[n % 2][:, HP * c:HP * c + HP, :].rearrange("p h n -> p (h n)"),
                                             ident[:, :])
                mm.then_inc(own.full_sem(key), 1)

            def head_means(t):
                pe.wait_ge(*gn_step.count(t, 2))
                pe.wait_ge(*tail.empty(t, ("gn",)))
                nc.tensor.matmul(tail.bank(("gn",))[:, 0:2 * KI], head_mean[:, :],
                                 gn_mom[:, :, :].rearrange("p c s -> p (c s)"), start=True, stop=True)\
                    .then_inc(tail.full_sem(("gn",)), 1)

            def attention_out(t, j):
                pe.wait_ge(*g_out.count(t, (j + 1) * KI))
                for m in range(NQ // 2):
                    key = ("Wo", j, m)
                    pe.wait_ge(*tail.empty(t, key))
                    for i in (2 * m, 2 * m + 1):
                        for c in range(KI):
                            mm = nc.tensor.matmul(tail.bank(key)[:, (i % 2) * D:(i % 2 + 1) * D],
                                                  yT[:, c, (j * NQ + i) * P:(j * NQ + i + 1) * P], WoutT[:, c, :],
                                                  start=(c == 0), stop=(c == KI - 1))
                    mm.then_inc(tail.full_sem(key), 1)

            def turn_middle(t, j):
                turn_tokens(t, tail, "uT", j, un, un_out)

            def hidden(t, j):
                pe.wait_ge(*uh_lo.count(t, (j + 1) * KD))
                for f in range(KF):
                    key = ("H", j, f)
                    pe.wait_ge(*tail.empty(t, key))
                    terms = [(k, i) for k in range(KD) for i in range(2)]
                    for a, (k, i) in enumerate(terms):
                        mm = nc.tensor.matmul(tail.bank(key)[:, :], sign1T[:, k, cols(f)], uh[i][:, k, :],
                                              start=(a == 0), stop=(a == len(terms) - 1))
                    mm.then_inc(tail.full_sem(key), 1)

            def ffn_out(t, j):
                pe.wait_ge(*hh_lo.count(t, (j + 1) * KF))
                for m in range(NQ // 2):
                    key = ("O", j, m)
                    pe.wait_ge(*tail.empty(t, key))
                    for i in (2 * m, 2 * m + 1):
                        terms = [(f, p) for f in range(KF) for p in range(2)]
                        for a, (f, p) in enumerate(terms):
                            mm = nc.tensor.matmul(tail.bank(key)[:, (i % 2) * D:(i % 2 + 1) * D], hh[p][:, f, cols(i)],
                                                  sign2T[:, f, :], start=(a == 0), stop=(a == len(terms) - 1))
                    mm.then_inc(tail.full_sem(key), 1)

            all_batches(pe, {
                "xT": turn_input, "xi": project_x, "z": project_z, "dt": step_size, "B": project_b, "C": project_c,
                "sums": decay_sums, "front": front, "back": back, "turn": turn, "gn_sum": head_means,
                "Wo": attention_out, "uT": turn_middle, "H": hidden, "O": ffn_out})


_INS = ["L0_attn_input_tensor", "L0_attn_Wx", "L0_attn_Wz", "L0_attn_conv_w", "L0_attn_conv_b", "L0_attn_Wb",
        "L0_attn_Wc", "L0_attn_Wdt", "L0_attn_b_dt", "L0_attn_log_a", "L0_attn_d_param", "L0_attn_gn_w",
        "L0_attn_gn_b", "L0_attn_Wout", "L0_ffn_w1", "L0_ffn_b1", "L0_ffn_w2", "L0_ffn_b2"]


def kernel(**inputs):
    import numpy as _np
    import concourse.bacc as _bacc
    from concourse import mybir as _mybir
    from concourse.bass_utils import run_bass_kernel_spmd as _run

    nc = _bacc.Bacc("TRN2", target_bir_lowering=False, num_devices=1)
    arrays, args = {}, []
    for name in _INS:
        a = _np.ascontiguousarray(inputs[name])
        arrays[f"in_{name}_dram"] = a
        args.append(nc.dram_tensor(f"in_{name}_dram", a.shape, _mybir.dt.from_np(a.dtype), kind="ExternalInput").ap())
    args.append(nc.dram_tensor("out_0_dram", (NB, T, D), F32, kind="ExternalOutput").ap())
    mamba_sandwich_kernel(nc, *args)
    r = _run(nc, [arrays], core_ids=[0])
    return r.results[0]["out_0_dram"]
```

```python
from contextlib import ExitStack

import concourse.bass as bass
from concourse import mybir

F32 = mybir.dt.float32
F16 = mybir.dt.float16
ALU = mybir.AluOpType
ACT = mybir.ActivationFunctionType
AX_X = mybir.AxisListType.X

P = 128
NB, T, D = 8, 1024, 256
INNER, HEADS, HD, NS = 512, 8, 64, 64
TAPS = 4
FF = 1024
EPS = 1e-5

BLK = 512
NJ = T // BLK
NQ = BLK // P
KD = D // P
KI = INNER // P
HP = P // HD
KF = FF // P
HALO = TAPS - 1

SW = 256.0
SX = 256.0
SG = 64.0
DECAY_FLOOR = -10000.0


BANKS = 8
OWN_BANKS = 5


class Batch:

    def __init__(self, b, d=0):
        self.b, self.d = b, d

    def ago(self, n):
        return Batch(self.b, self.d - n)

    def number(self):
        return self.b + self.d if self.d else self.b


class Count(tuple):

    def __new__(cls, sem, b, rate, rest):
        self = super().__new__(cls, (sem, b * rate + rest))
        self.rest = self[1] if isinstance(b, int) else rest
        return self


def latest(*counts):
    return [c for c in counts if not any(d[0] is c[0] and d.rest > c.rest for d in counts)]


class Signal:

    def __init__(self, sem, each, step=1):
        self.sem, self.each, self.step = sem, each, step

    def count(self, t, n):
        return Count(self.sem, t.b, self.each * self.step, ((t.d + 1) * self.each + n) * self.step)

    def prime(self, eng):
        eng.sem_inc(self.sem, self.each * self.step)


class Ring:

    def __init__(self, tensors, full_sems, keys, once, freed=None):
        self.tensors, self.full_sems, self.keys, self.once, self.freed = tensors, full_sems, keys, once, freed
        self.place, self.each = {}, [0] * len(tensors)
        for n, key in enumerate(keys):
            k = n % len(tensors)
            self.place[key] = k, self.each[k]
            self.each[k] += 1
        self.read = {}

    def bank(self, key):
        return self.tensors[self.place[key][0]]

    def full_sem(self, key):
        return self.full_sems[self.place[key][0]]

    def full(self, t, key):
        k, m = self.place[key]
        if self.freed is not None:
            return Count(self.full_sems[k], 0, 0, self.once[k] + m + 1)
        return Count(self.full_sems[k], t.b, self.each[k], self.once[k] + (t.d + 1) * self.each[k] + m + 1)

    def empty(self, t, key):
        k, m = self.place[key]
        if m == 0 and self.freed is not None:
            return self.freed[k]
        of = self.last_use(k) if m == 0 else [x for x in self.keys if self.place[x] == (k, m - 1)][0]
        signal, n = self.read[of]
        if t is None:
            return signal, n
        return signal.count(t.ago(1) if m == 0 else t, n)

    def last_use(self, k):
        return [x for x in self.keys if self.place[x][0] == k][-1]

    def prime(self, pe):
        for k in range(len(self.tensors)):
            pe.sem_inc(self.full_sems[k], self.each[k])


def turn_steps(first, last):
    def own(*keys):
        return [("own", *k) for k in keys]

    def tail(*keys):
        return [("tail", *k) for k in keys]

    steps = []
    for j in range(NJ):
        if j == 0:
            steps += own(("xi", 0, 0)) + tail(("turn", NJ - 1, NQ - 1)) + own(("xi", 0, 1), ("xi", 0, 2))
            steps += tail(("head_stat", NJ - 1, 1), ("gn_sum",)) + own(("xi", 0, 3), ("silu_table",))
            steps += tail(("gn_mean",), ("gn_root",)) + own(("conv", 0, 0, 0, 2), ("z", 0, 0)) + tail(("gn_fold",))
            steps += own(("conv", 0, 0, 2, 3), ("z", 0, 1)) + tail(("gate", 0, 0)) + own(("z", 0, 2), ("z", 0, 3))
            steps += own(("conv", 0, 1)) + tail(("gate", 0, 1)) + own(*[("z_in", 0, c) for c in range(KI)])
            steps += tail(("Wo", 0, 0)) + own(("silu", 0, 0), ("silu", 0, 1), ("conv", 0, 2), ("conv", 0, 3))
            steps += own(("xs", 0, 0), ("xs", 0, 1), ("silu", 0, 2), ("xs", 0, 2), ("silu", 0, 3), ("xs", 0, 3))
            steps += own(("z_silu",)) + tail(("Wo", 0, 1))
        else:
            steps += own(("xi", 1, 0), ("xi", 1, 1), ("turn", 0, NQ - 1), ("conv", 1, 0), ("head_stat", 0, 1))
            steps += own(("xi", 1, 2), ("conv", 1, 1), ("xi", 1, 3), ("silu_table",), ("z", 1, 0), ("z_in", 1, 0))
            steps += own(("silu", 1, 0), ("conv", 1, 2), ("z", 1, 1), ("z_in", 1, 1), ("silu", 1, 1), ("xs", 1, 0))
            steps += own(("conv", 1, 3), ("z", 1, 2), ("z_in", 1, 2), ("silu", 1, 2), ("xs", 1, 1))
            steps += own(("z", 1, 3), ("z_in", 1, 3), ("silu", 1, 3), ("xs", 1, 2), ("xs", 1, 3))
            steps += tail(("Wo", 1, 0), ("Wo", 1, 1))
        steps += tail(("mid_stat", j)) + own(("B", j, 0), ("dt", j), ("log", j))
        steps += tail(("mid_norm", j)) + own(("B", j, 1), ("decay", j)) + tail(("ff_stat", j), ("gelu_table",))
        steps += own(("B", j, 2), ("seg", j, 0)) + tail(("ff_norm", j)) + own(("B", j, 3), ("seg", j, 1))
        steps += tail(("gate", 1, 0), ("gate", 1, 1)) if j == 0 else []
        steps += own(("C", j, 0)) + tail(("uT", j)) + own(("skip", j), ("C", j, 1)) + tail(("H", j, 0), ("H", j, 1))
        steps += own(("C", j, 2)) + tail(("H", j, 2), ("H", j, 3)) + own(("C", j, 3)) + tail(("H", j, 4), ("H", j, 5))
        steps += own(("sums", j)) + tail(("H", j, 6), ("H", j, 7)) + own(("decays", j))
        who, nj = ("next", 0) if j else ("own", 1)
        both = [[("own", "back" if first else "back+O", j, m)] for m in range(2)]
        steps += own(("front", j, 0), ("seg", j, 2), ("front", j, 1), ("carry", j, 0)) + both[0]
        steps += own(("front", j, 2), ("seg", j, 3), ("carry", j, 1)) + [(who, "in_stat", nj)] + both[1]
        steps += own(("turn", j, 0)) + [(who, "in_norm", nj)] + own(("front", j, 3)) + [(who, "xT", nj, 0)]
        steps += tail(("end_stat", j)) + own(("carry", j, 2), ("back", j, 2), ("turn", j, 1)) + [(who, "xT", nj, 1)]
        steps += tail(("end_root", j), ("end_norm", j)) + own(("carry", j, 3), ("turn", j, 2), ("back", j, 3))
        steps += own(("head_stat", j, 0)) + tail(("end_add", j))
    return [s for s in steps if not (first and s[0] == "tail") and not (last and s[0] == "next")]


def first_norm():
    return [("own", "in_stat", 0), ("own", "in_norm", 0)]


def last_tail():
    def hidden(j, first, end):
        return [("H", j, f) for f in range(first, end)]

    steps = [("turn", NJ - 1, NQ - 1), ("head_stat", NJ - 1, 1), ("gn_sum",), ("gn_mean",), ("gn_root",), ("gn_fold",)]
    steps += [("gate", j, m) for j in range(NJ) for m in range(2)]
    steps += [("Wo", 0, 0), ("Wo", 0, 1), ("mid_stat", 0), ("mid_norm", 0), ("ff_stat", 0), ("ff_norm", 0)]
    steps += [("Wo", 1, 0), ("Wo", 1, 1), ("mid_stat", 1), ("uT", 0), ("mid_norm", 1), *hidden(0, 0, 4)]
    steps += [("ff_stat", 1), *hidden(0, 4, 6), ("ff_norm", 1), *hidden(0, 6, 8), ("uT", 1), ("O", 0, 0), ("O", 0, 1)]
    steps += [*hidden(1, 0, 8), ("end_stat", 0), ("end_root", 0), ("end_norm", 0), ("end_add", 0)]
    steps += [("O", 1, 0), ("O", 1, 1), ("end_stat", 1), ("end_root", 1), ("end_norm", 1), ("end_add", 1)]
    return [("tail", *k) for k in steps]


def mamba_sandwich_kernel(nc, x, Wx, Wz, conv_w, conv_b, Wb, Wc, Wdt, b_dt, log_a, d_param, gn_w, gn_b,
                          Wout, w1, b1, w2, b2, out):
    ctx = ExitStack()
    with ctx:
        def sb(name, shape, dt=F32):
            return ctx.enter_context(nc.sbuf_tensor(name, shape, dt))

        def sem(name):
            return ctx.enter_context(nc.semaphore(name))

        ident = sb("ident", [P, P])
        upto = sb("upto", [P, P])
        upto_h = sb("upto_h", [P, P], F16)
        after = sb("after", [P, P])
        after_h = sb("after_h", [P, P], F16)
        ones = sb("ones", [P, P])
        head_mean = sb("head_mean", [P, P])
        power = sb("power", [P, 4])

        WxT = [sb(f"WxT{i}", [P, KD, INNER], F16) for i in range(2)]
        WzT = [sb(f"WzT{i}", [P, KD, INNER], F16) for i in range(2)]
        WbT = [sb(f"WbT{i}", [P, KI, HEADS * NS], F16) for i in range(2)]
        WcT = [sb(f"WcT{i}", [P, KI, HEADS * NS], F16) for i in range(2)]
        WdtT = [sb(f"WdtT{i}", [P, KI, HEADS], F16) for i in range(2)]
        WoutT = sb("WoutT", [P, KI, D])
        sign1T = sb("sign1T", [P, KD, FF], F16)
        sign2T = sb("sign2T", [P, KF, D], F16)
        alpha1 = sb("alpha1", [P, KF])
        alpha2 = sb("alpha2", [P, KD])
        alpha2_row = sb("alpha2_row", [P, D])
        b1_col = sb("b1_col", [P, KF])
        b2_row = sb("b2_row", [P, D])
        taps = sb("taps", [P, KI, TAPS])
        last_tap = sb("last_tap", [P, KI])
        conv_bias = sb("conv_bias", [P, KI])
        gnw = sb("gnw", [P, KI])
        gnb = sb("gnb", [P, KI])
        skip = sb("skip", [P, KI])
        bdt_row = sb("bdt_row", [P, HEADS])
        a_row = sb("a_row", [P, HEADS])
        table_in = sb("table_in", [P, 1])

        xt = [sb(f"xt{j}", [P, NQ, D]) for j in range(NJ)]
        xn = sb("xn", [P, NQ, D])
        xh = [sb(f"xh{i}", [P, KD, BLK], F16) for i in range(2)]
        xi = sb("xi", [P, KI, HALO + BLK])
        no_halo = sb("no_halo", [P, KI, HALO])
        xs = sb("xs", [P, KI, BLK])
        sh = [sb(f"sh{i}", [P, KI, BLK], F16) for i in range(2)]
        zs = sb("zs", [P, KI, T])
        yT = sb("yT", [P, KI, T])
        BT = sb("BT", [P, KI, BLK])
        CT = sb("CT", [P, KI, BLK])

        def small(name, dt=F32):
            return sb(name, [P, NQ, HEADS], dt)
        v_dt, abs_v, exp_v, one_e, e_back, e_rest, log_u = (small(n) for n in (
            "v_dt", "abs_v", "exp_v", "one_e", "e_back", "e_rest", "log_u"))
        dt_raw = small("dt_raw")
        dt_t = small("dt_t")
        da_raw = small("da_raw")
        da = small("da")
        da_hi, da_lo = small("da_hi", F16), small("da_lo", F16)
        decays = sb("decays", [P, 3, NQ, HEADS])

        seg = [[sb(f"seg{i}{r}", [P, HP, KI, P], F16) for r in range(2)] for i in range(2)]
        mt = [sb(f"mt{r}", [P, HP, KI, P]) for r in range(2)]
        xdt = [sb(f"xdt{r}", [P, HEADS, HD]) for r in range(2)]
        xdw = [sb(f"xdw{r}", [P, HEADS, HD]) for r in range(2)]
        bt = [sb(f"bt{r}", [P, HEADS * NS]) for r in range(2)]
        yk = [sb(f"yk{r}", [P, HEADS, HD]) for r in range(2)]
        state = sb("state", [P, KI, P])

        LNS = ("in", "mid", "ff", "end")
        stats = {w: sb(f"stats_{w}", [P, NQ, 6]) for w in LNS}
        moments = {w: sb(f"moments_{w}", [P, NQ, 2]) for w in LNS}
        var_eps = {w: sb(f"var_eps_{w}", [P, NQ]) for w in LNS}
        rstd = {w: sb(f"rstd_{w}", [P, NQ]) for w in LNS}
        gn_stats = sb("gn_stats", [P, KI, NJ * 2, 6])
        gn_mom = sb("gn_mom", [P, KI, 2])
        gn_sq = sb("gn_sq", [P, KI])
        gn_head = sb("gn_head", [P, KI, 2])
        gn_msq = sb("gn_msq", [P, KI])
        gn_var = sb("gn_var", [P, KI])
        gn_rstd = sb("gn_rstd", [P, KI])
        gn_scale = sb("gn_scale", [P, KI])
        gn_ms = sb("gn_ms", [P, KI])
        gn_shift = sb("gn_shift", [P, KI])

        u = [sb(f"u{j}", [P, NQ, D]) for j in range(NJ)]
        un = sb("un", [P, NQ, D])
        uh = [sb(f"uh{i}", [P, KD, BLK], F16) for i in range(2)]
        hf = [sb(f"hf{r}", [P, BLK]) for r in range(2)]
        hh = [sb(f"hh{i}", [P, KF, BLK], F16) for i in range(2)]
        y2 = sb("y2", [P, NQ, D])

        Wdt_in = state[0:HEADS, :, :].rearrange("p c n -> p (c n)")
        Wb_in, Wc_in = zs[:, :, 0:INNER], zs[:, :, INNER:2 * INNER]
        w1_in = yT[:, 0:2, :].rearrange("p a (b d) -> p (a b) d", d=D)
        w2_in = yT[:, 2:4, :]
        Wx_in = BT[:, :, :].rearrange("p a n -> p (a n)")[:, 0:KI * D].rearrange("p (a d) -> p a d", d=D)
        Wz_in = BT[:, :, :].rearrange("p a n -> p (a n)")[:, KI * D:2 * KI * D].rearrange("p (a d) -> p a d", d=D)
        Wout_in = CT[:, 0:2, :]
        alpha2_wide = [CT[:, 2, k * P:(k + 1) * P] for k in range(KD)]

        before = [("Wx", k) for k in range(KD)] + [("Wz", k) for k in range(KD)]
        before += [("Wb", k) for k in range(KI)] + [("Wc", k) for k in range(KI)] + [("Wdt", 0)]
        before += [("Wout", k) for k in range(KI // 2)]
        before += [("w2", f) for f in range(KF // 2)] + [("w1", k, m) for k in range(KD) for m in range(2)]
        before += [("alpha2", 0)]

        def uses(kind, *at):
            if kind in ("xT", "xi", "z", "B", "C", "dt", "sums", "Wo", "H", "O"):
                return [(kind, *at)]
            if kind == "front":
                heads_of = [[(name, *at, g) for g in range(HP)] for name in ("seg", "S")]
                return [*heads_of[0], ("X", *at), ("Bt", *at), *heads_of[1]]
            if kind == "carry":
                return [("YI", *at), ("St", *at)]
            if kind == "back":
                return [("Y", *at)]
            if kind == "uT":
                return [("uT", *at, k) for k in range(KD)]
            return {"turn": [("YT", *at)], "gn_mean": [("gn",)]}.get(kind, [])

        own_keys, tail_keys, in_keys = [], [], []
        for who, kind, *at in turn_steps(False, False):
            if kind == "back+O":
                own_keys += uses("back", *at)
                who, kind = "tail", "O"
            (tail_keys if who == "tail" else in_keys if kind in ("xT", "sums") else own_keys).extend(uses(kind, *at))
        in_keys.sort(key=lambda key: (key[1], key[0] == "sums", key))
        last_keys = [key for _, kind, *at in last_tail() for key in uses(kind, *at)]
        full_sems = [sem(f"bank_full{k}") for k in range(BANKS)]
        psum = [ctx.enter_context(nc.psum_tensor(f"bank{k}", [P, 512], F32)) for k in range(BANKS)]
        IN = BANKS - 1
        setup = Ring(psum[:IN], full_sems[:IN], before, [0] * IN, freed=[None] * IN)
        rings, k = [], 0
        for keys, n in ((own_keys, OWN_BANKS), (tail_keys, IN - OWN_BANKS), (in_keys, 1)):
            rings.append(Ring(psum[k:k + n], full_sems[k:k + n], keys, (setup.each + [0])[k:k + n]))
            k += n
        ring = {key: r for r in rings for key in r.keys}
        order = [*range(OWN_BANKS), IN, *range(OWN_BANKS, IN)]
        batches = {id(rings[0]): NB, id(rings[1]): NB - 1, id(rings[2]): NB}
        used = [r.once[k] + (batches[id(r)] + 1) * r.each[k] for r in rings for k in range(len(r.tensors))]
        final = Ring([psum[k] for k in order], [full_sems[k] for k in order], last_keys, [used[k] for k in order],
                     freed=[])

        def ring_of(t, key):
            last = isinstance(t.b, int) and t.b + t.d == NB - 1
            return final if last and key in final.place else ring[key]

        def full(t, key):
            return ring_of(t, key).full(t, key)

        def empty(t, key):
            return ring_of(t, key).empty(t, key)

        def bank(t, key):
            return ring_of(t, key).bank(key)

        def full_sem(t, key):
            return ring_of(t, key).full_sem(key)

        masks_zero = sem("masks_zero")
        masks_made = sem("masks_made")
        arrived = {w: sem(f"arrived_{w}") for w in ("Wx", "Wz", "Wb", "Wc", "Wdt", "Wout", "w1", "w2", "vectors")}
        w_split = sem("w_split")
        act_set = sem("act_set")
        dve_set = sem("dve_set")
        low_set = sem("low_set")
        wide_set = sem("wide_set")
        alpha2_read = sem("alpha2_read")
        a_exp = sem("a_exp")
        stats_seen = sem("stats_seen")
        state_seen = sem("state_seen")
        decay_seen = sem("decay_seen")
        NCH = NJ * NQ
        x_in = [Signal(sem(f"x_in{j}"), 1, step=16) for j in range(NJ)]
        u_in = [Signal(sem(f"u_in{j}"), 1, step=16) for j in range(NJ)]
        stored = [Signal(sem(f"stored{j}"), 1, step=16) for j in range(NJ)]
        ln_stats = {w: Signal(sem(f"ln_stats_{w}"), NJ * NQ) for w in LNS}
        ln_moments = {w: Signal(sem(f"ln_moments_{w}"), NJ * NQ) for w in LNS}
        ln_eps = {w: Signal(sem(f"ln_eps_{w}"), NJ) for w in LNS}
        ln_rstd = {w: Signal(sem(f"ln_rstd_{w}"), NJ) for w in LNS}
        xn_made = Signal(sem("xn_made"), NJ * NQ)
        xh_hi = Signal(sem("xh_hi"), NJ * KD)
        xh_lo = Signal(sem("xh_lo"), NJ * KD)
        halo = Signal(sem("halo"), NJ)
        xi_out = Signal(sem("xi_out"), NJ * KI)
        tap_out = Signal(sem("tap_out"), NJ * KI)
        conv_out = Signal(sem("conv_out"), NJ * KI * (TAPS - 1))
        xs_out = Signal(sem("xs_out"), NJ * KI)
        z_read = Signal(sem("z_read"), NJ * KI)
        zs_out = Signal(sem("zs_out"), KI)
        sh_hi = Signal(sem("sh_hi"), NJ * KI)
        sh_lo = Signal(sem("sh_lo"), NJ * KI)
        B_out = Signal(sem("B_out"), NJ * KI)
        C_out = Signal(sem("C_out"), NJ * KI)
        DT = 10
        dt_step = Signal(sem("dt_step"), NJ * DT)
        dt_act = Signal(sem("dt_act"), NJ * 2)
        da_seen = Signal(sem("da_seen"), NJ)
        decays_out = Signal(sem("decays_out"), NJ)
        skip_out = Signal(sem("skip_out"), NJ * KI)
        seg_hi = Signal(sem("seg_hi"), NCH)
        seg_lo = Signal(sem("seg_lo"), NCH)
        seg_exp = Signal(sem("seg_exp"), NCH * HP)
        decay_masked = Signal(sem("decay_masked"), NCH * HP)
        mt_out = Signal(sem("mt_out"), NCH * HP)
        xdt_out = Signal(sem("xdt_out"), NCH)
        xdw_out = Signal(sem("xdw_out"), NCH)
        bt_out = Signal(sem("bt_out"), NCH)
        yk_part = Signal(sem("yk_part"), NCH)
        yk_out = Signal(sem("yk_out"), NCH)
        st_zero = Signal(sem("st_zero"), 1)
        st_scaled = Signal(sem("st_scaled"), NCH)
        st_out = Signal(sem("st_out"), NCH * HP)
        yT_out = Signal(sem("yT_out"), NCH)
        gn_st = Signal(sem("gn_st"), NJ * 2 * KI)
        gn_mo = Signal(sem("gn_mo"), KI)
        gn_step = Signal(sem("gn_step"), 8)
        gn_rs = Signal(sem("gn_rs"), 1)
        yn_out = Signal(sem("yn_out"), NJ * 2 * KI)
        g_out = Signal(sem("g_out"), KI)
        g_late = Signal(sem("g_late"), (2 * NJ - 1) * KI)
        mid_out = Signal(sem("mid_out"), NJ * NQ)
        u_out = Signal(sem("u_out"), NJ * NQ)
        un_out = Signal(sem("un_out"), NJ * NQ)
        uh_hi = Signal(sem("uh_hi"), NJ * KD)
        uh_lo = Signal(sem("uh_lo"), NJ * KD)
        hf_out = Signal(sem("hf_out"), NJ * KF)
        hh_hi = Signal(sem("hh_hi"), NJ * KF)
        hh_lo = Signal(sem("hh_lo"), NJ * KF)
        y2_scaled = Signal(sem("y2_scaled"), NJ * NQ // 2)
        y2_out = Signal(sem("y2_out"), NJ * NQ // 2)
        y2_norm = Signal(sem("y2_norm"), NJ * NQ)
        o_out = Signal(sem("o_out"), NJ * NQ)

        def ffn_buffer(t, j):
            return xn if isinstance(t.b, int) and (t.b + t.d, j) == (NB - 1, NJ - 1) else y2

        x_v = x.rearrange("b (j q p) d -> b j p q d", j=NJ, p=P)
        out_v = out.rearrange("b (j q p) d -> b j p q d", j=NJ, p=P)
        VECTORS = 8 + HP
        DVE_SETUP, ACT_SETUP = 5, KI // 2 + 2 * KD + KF // 2

        def ch(j, q):
            return j * NQ + q

        def per_head(ap):
            return ap[:, :, None].to_broadcast([P, HEADS, HD])

        def heads(ap):
            return ap.rearrange("p (h n) -> p h n", h=HEADS)

        def every_head(mask):
            return mask[:, None, None, :].to_broadcast([P, HP, KI, P])

        def every_token(part, q):
            return part[:, q, :].rearrange("p (c g) -> p g c", g=HP)[:, :, :, None].to_broadcast([P, HP, KI, P])

        def before_block(t, j):
            return (t.ago(1), NJ - 1) if j == 0 else (t, j - 1)

        def two_before(t, n):
            m = (n - 2) % NCH
            return (t.ago(1) if n < 2 else t), m // NQ, m % NQ

        lows = before[:2 * KD + 2 * KI + 1]
        setup.read.update({key: (low_set, n + 1) for n, key in enumerate(lows)})
        setup.read.update({key: (act_set, n + 1) for n, key in enumerate(before[len(lows):-1])})
        read = {("gn",): (gn_step, 3)}
        for j in range(NJ):
            for k in range(KD):
                read[("xT", j, k)] = xh_lo, j * KD + k + 1
                read[("uT", j, k)] = uh_lo, j * KD + k + 1
            for c in range(KI):
                for name, signal in (("xi", tap_out), ("z", z_read), ("B", B_out), ("C", C_out)):
                    read[(name, j, c)] = signal, j * KI + c + 1
            read[("dt", j)] = dt_step, j * DT + 1
            read[("sums", j)] = decays_out, j + 1
            for q in range(NQ):
                n = ch(j, q)
                for name, signal in (("X", xdt_out), ("Bt", bt_out), ("YI", yk_part), ("Y", yk_out), ("YT", yT_out)):
                    read[(name, j, q)] = signal, n + 1
                read[("St", j, q)] = st_out, (n + 1) * HP
                for g in range(HP):
                    read[("seg", j, q, g)] = seg_exp, n * HP + g + 1
                    read[("S", j, q, g)] = mt_out, n * HP + g + 1
            for f in range(KF):
                read[("H", j, f)] = hf_out, j * KF + f + 1
            for m in range(NQ // 2):
                read[("Wo", j, m)] = mid_out, j * NQ + 2 * m + 2
                read[("O", j, m)] = y2_scaled, j * NQ // 2 + m + 1
        for r in (*rings, final):
            r.read = read
        last_uses = [(read[r.last_use(k)], Batch(batches[id(r)], -1)) for r in rings for k in range(len(r.tensors))]
        final.freed = [signal.count(t, n) for (signal, n), t in (last_uses[k] for k in order)]

        def run(steps, b, handlers):
            for who, kind, *at in steps:
                if kind in handlers:
                    handlers[kind](Batch(b, {"own": 0, "tail": -1, "next": 1}[who]), *at)

        def all_batches(eng, handlers):
            run([("own", "xT", 0, k) for k in range(KD)] + turn_steps(True, False), 0, handlers)
            with eng.Fori(1, NB - 1) as b:
                run(turn_steps(False, False), b, handlers)
            run(turn_steps(False, True), NB - 1, handlers)
            run(last_tail(), NB, handlers)

        block = ctx.enter_context(nc.Block())

        @block.sync
        def _(sp):
            def load(name, dst, src):
                sp.dma_start(dst, src).then_inc(arrived[name], 16)

            for j in range(NJ):
                for signal in (x_in[j], u_in[j], stored[j]):
                    signal.prime(sp)

            def rows(view, t, j):
                return view[bass.ds(t.number(), 1), j].rearrange("a p q d -> p (a q) d")

            def load_x(t, j):
                sp.wait_ge(*xn_made.count(t.ago(1), (j + 1) * NQ))
                sp.dma_start(xt[j][:, :, :], rows(x_v, t, j)).then_inc(x_in[j].sem, 16)

            def load_u(t, j):
                sp.wait_ge(*stored[j].count(t.ago(1), 1))
                sp.dma_start(u[j][:, :, :], rows(x_v, t, j)).then_inc(u_in[j].sem, 16)

            def store(t, j):
                sp.wait_ge(*o_out.count(t, (j + 1) * NQ))
                sp.dma_start(rows(out_v, t, j), u[j][:, :, :]).then_inc(stored[j].sem, 16)

            load_x(Batch(0), 0)
            with nc.allow_non_contiguous_dma(reason="vectors, once"):
                load("Wx", Wx_in, Wx.rearrange("(m p) d -> p m d", p=P))
                load("Wz", Wz_in, Wz.rearrange("(m p) d -> p m d", p=P))
                load("Wb", Wb_in, Wb.rearrange("(m p) d -> p m d", p=P))
                load("Wc", Wc_in, Wc.rearrange("(m p) d -> p m d", p=P))
                load("Wdt", Wdt_in, Wdt)
                load("Wout", Wout_in, Wout.rearrange("(m p) d -> p m d", p=P))
                load("w2", w2_in, w2.rearrange("(m p) d -> p m d", p=P))
                load("w1", w1_in, w1.rearrange("(m p) d -> p m d", p=P))
                load("vectors", taps[:, :, :], conv_w.rearrange("(c p) o k -> p c (o k)", p=P))
                load("vectors", conv_bias[:, :], conv_b.rearrange("(c p) -> p c", p=P))
                load("vectors", gnw[:, :], gn_w.rearrange("(c p) -> p c", p=P))
                load("vectors", gnb[:, :], gn_b.rearrange("(c p) -> p c", p=P))
                load("vectors", b1_col[:, :], b1.rearrange("(c p) -> p c", p=P))
                load("vectors", b2_row[:, :], b2.partition_broadcast(P))
                load("vectors", bdt_row[:, :], b_dt.partition_broadcast(P))
                load("vectors", a_row[:, :], log_a.partition_broadcast(P))
                for g in range(HP):
                    load("vectors", skip[g * HD:(g + 1) * HD, :],
                         d_param.rearrange("(c g) -> g c", g=HP)[g].partition_broadcast(HD))
            load_x(Batch(0), 1)
            for j in range(NJ):
                load_u(Batch(0), j)
            for j in range(NJ):
                load_x(Batch(1), j)
            with sp.Fori(1, NB - 1) as b:
                load_x(Batch(b, 1), 0)
                store(Batch(b, -1), 0)
                load_u(Batch(b), 0)
                load_x(Batch(b, 1), 1)
                store(Batch(b, -1), 1)
                load_u(Batch(b), 1)
            for j in range(NJ):
                store(Batch(NB - 1, -1), j)
                load_u(Batch(NB - 1), j)
            for j in range(NJ):
                store(Batch(NB - 1), j)
            for j in range(NJ):
                sp.wait_ge(*stored[j].count(Batch(NB - 1), 1))

        @block.gpsimd
        def _(pool):
            for t, v in ((ident, 0.0), (upto, 1.0), (upto_h, 1.0), (after, 1.0),
                                        (after_h, 1.0), (ones, 1.0), (head_mean, 0.0),
                                        (power, -0.5)):
                pool.memset(t[:, :], v).then_inc(masks_zero, 1)
            pool.memset(no_halo[:, :, :], 0.0).then_inc(masks_zero, 1)
            pool.wait_ge(masks_zero, 9)
            for g in range(HP):
                pool.memset(head_mean[g * HD:(g + 1) * HD, g * HD:(g + 1) * HD], 1.0 / HD).then_inc(masks_made, 1)
                pool.wait_ge(masks_made, g + 1)
            pool.affine_select(out=ident[:, :], in_=ident[:, :], compare_op=ALU.not_equal, fill=1.0, base=0,
                               pattern=[[-1, P]], channel_multiplier=1).then_inc(masks_made, 1)
            for t in (upto, upto_h):
                pool.affine_select(out=t[:, :], in_=t[:, :], compare_op=ALU.is_ge, fill=0.0, base=0,
                                   pattern=[[1, P]], channel_multiplier=-1).then_inc(masks_made, 1)
            for t in (after, after_h):
                pool.affine_select(out=t[:, :], in_=t[:, :], compare_op=ALU.is_ge, fill=0.0, base=-1,
                                   pattern=[[-1, P]], channel_multiplier=1).then_inc(masks_made, 1)
            pool.wait_ge(masks_made, 7)
            for s in (*ln_rstd.values(), gn_rs, u_out, y2_out, o_out, xdw_out, st_zero, st_scaled, seg_lo, g_late,
                      decay_masked):
                s.prime(pool)

            def inverse_root(w):
                def step(t, j):
                    pool.wait_ge(*ln_eps[w].count(t, j + 1))
                    pool.tensor_tensor(rstd[w][:, :], var_eps[w][:, :], power[:, 0:NQ], ALU.pow)\
                        .then_inc(ln_rstd[w].sem, 1)
                return step

            def head_root(t):
                pool.wait_ge(*gn_step.count(t, 5))
                pool.tensor_tensor(gn_rstd[:, :], gn_var[:, :], power[:, 0:KI], ALU.pow).then_inc(gn_rs.sem, 1)

            def add_input(t, j):
                pool.wait_ge(*u_in[j].count(t, 1))
                for i in range(NQ):
                    pool.wait_ge(*mid_out.count(t, j * NQ + i + 1))
                    pool.tensor_tensor(u[j][:, i, :], u[j][:, i, :], un[:, i, :], ALU.add).then_inc(u_out.sem, 1)

            def add_bias(t, j, m):
                n = j * NQ // 2 + m
                pool.wait_ge(*y2_scaled.count(t, n + 1))
                v = ffn_buffer(t, j)[:, 2 * m:2 * m + 2, :]
                pool.tensor_tensor(v, v, b2_row[:, None, :].to_broadcast([P, 2, D]), ALU.add).then_inc(y2_out.sem, 1)

            def add_middle(t, j):
                for i in range(NQ):
                    pool.wait_ge(*y2_norm.count(t, j * NQ + i + 1))
                    pool.tensor_tensor(u[j][:, i, :], u[j][:, i, :], ffn_buffer(t, j)[:, i, :], ALU.add)\
                        .then_inc(o_out.sem, 1)

            def gate(t, j, m):
                n = 2 * j + m
                for c in range(KI if n else 0):
                    at = slice(n * BLK // 2, (n + 1) * BLK // 2)
                    pool.wait_ge(*yn_out.count(t, n * KI + c + 1))
                    pool.tensor_tensor(yT[:, c, at], yT[:, c, at], zs[:, c, at], ALU.mult).then_inc(g_late.sem, 1)

            def segments(t, j, q):
                n = ch(j, q)
                if q == 0:
                    pool.wait_ge(*dt_step.count(t, (j + 1) * DT))
                s, sj, sq = two_before(t, n)
                pool.wait_ge(*full(s, ("seg", sj, sq, HP - 1)))
                pool.tensor_tensor(seg[1][n % 2][:, :, :, :], every_head(upto_h), every_token(da_lo, q), ALU.mult)\
                    .then_inc(seg_lo.sem, 1)

            def front(t, j, q):
                n = ch(j, q)
                if n == 0:
                    pool.wait_ge(*full(t.ago(1), ("YI", NJ - 1, NQ - 1)))
                    pool.wait_ge(*st_out.count(t.ago(1), NCH * HP))
                    pool.sem_inc(state_seen, 1)
                    pool.memset(state[:, :, :], 0.0).then_inc(st_zero.sem, 1)
                for g in range(HP):
                    pool.wait_ge(*seg_exp.count(t, n * HP + g + 1))
                    pool.sem_inc(decay_seen, 1)
                    pool.affine_select(out=mt[n % 2][:, g], in_=mt[n % 2][:, g], compare_op=ALU.is_ge, fill=0.0, base=0,
                                       pattern=[[0, KI], [1, P]], channel_multiplier=-1).then_inc(decay_masked.sem, 1)
                pool.wait_ge(*xdt_out.count(t, n + 1))
                if q == 0:
                    pool.wait_ge(*decays_out.count(t, j + 1))
                s, sj, sq = two_before(t, n)
                pool.wait_ge(*full(s, ("St", sj, sq)))
                pool.tensor_tensor(xdw[n % 2][:, :, :], xdt[n % 2][:, :, :], per_head(decays[:, 1, q, :]), ALU.mult)\
                    .then_inc(xdw_out.sem, 1)

            def carry(t, j, q):
                n = ch(j, q)
                pool.wait_ge(*full(t, ("YI", j, q)))
                if n == 0:
                    pool.wait_ge(*st_zero.count(t, 1))
                else:
                    pool.wait_ge(*st_out.count(t, n * HP))
                st = state[:, :, :].rearrange("p c (g n) -> p (c g) n", g=HP)
                pool.tensor_tensor(st, st, per_head(decays[:, 2, q, :]), ALU.mult).then_inc(st_scaled.sem, 1)

            handlers = {
                "in_stat": inverse_root("in"), "mid_stat": inverse_root("mid"), "ff_stat": inverse_root("ff"),
                "end_root": inverse_root("end"), "gn_root": head_root, "mid_norm": add_input,
                "O": add_bias, "back+O": lambda t, j, m: add_bias(t.ago(1), j, m), "end_add": add_middle,
                "gate": gate, "seg": segments, "front": front, "carry": carry}
            run(first_norm(), 0, handlers)
            pool.wait_ge(arrived["vectors"], 16 * VECTORS)
            all_batches(pool, handlers)

        @block.scalar
        def _(act):
            for s in (xh_hi, halo, xi_out, tap_out, xs_out, z_read, zs_out, sh_hi, C_out, dt_act, decays_out, skip_out,
                      seg_exp, bt_out, yk_part, yn_out, uh_hi, hf_out):
                s.prime(act)

            def high_half(dst, key):
                act.wait_ge(*setup.full(None, key))
                nc.scalar.activation(dst, setup.bank(key)[:, :], ACT.Copy, scale=SW).then_inc(w_split, 1)

            for k in range(KD):
                high_half(WxT[0][:, k, :], ("Wx", k))
            for k in range(KD):
                high_half(WzT[0][:, k, :], ("Wz", k))
            for k in range(KI):
                high_half(WbT[0][:, k, :], ("Wb", k))
            for k in range(KI):
                high_half(WcT[0][:, k, :], ("Wc", k))
            act.wait_ge(*setup.full(None, ("Wdt", 0)))
            nc.scalar.activation(WdtT[0][:, :, :], setup.bank(("Wdt", 0))[:, 0:KI * HEADS].rearrange("p (k h) -> p k h", k=KI),
                                 ACT.Copy, scale=SW).then_inc(w_split, 1)
            for k in range(KI // 2):
                act.wait_ge(*setup.full(None, ("Wout", k)))
                nc.scalar.activation(WoutT[:, 2 * k:2 * k + 2, :], setup.bank(("Wout", k))[:, :].rearrange("p (k n) -> p k n", k=2),
                                     ACT.Copy).then_inc(act_set, 1)
            for f in range(KF // 2):
                act.wait_ge(*setup.full(None, ("w2", f)))
                nc.scalar.activation(sign2T[:, 2 * f:2 * f + 2, :], setup.bank(("w2", f))[:, :].rearrange("p (k n) -> p k n", k=2),
                                     ACT.Sign).then_inc(act_set, 1)
            for k in range(KD):
                for m in range(2):
                    act.wait_ge(*setup.full(None, ("w1", k, m)))
                    nc.scalar.activation(sign1T[:, k, m * 512:(m + 1) * 512], setup.bank(("w1", k, m))[:, :],
                                         ACT.Sign).then_inc(act_set, 1)
            act.wait_ge(arrived["vectors"], 16 * VECTORS)
            nc.scalar.activation(a_row[:, :], a_row[:, :], ACT.Exp).then_inc(a_exp, 1)
            act.wait_ge(masks_zero, 9)
            act.wait_ge(dve_set, DVE_SETUP)

            def table(func):
                return lambda t: nc.scalar.activation(table_in[:, :], ones[:, 0:1], func)

            def input_high(t, j, k):
                s, sj = before_block(t, j)
                act.wait_ge(*full(t, ("xT", j, k)))
                act.wait_ge(*full(s, ("z", sj, KI - 1)))
                nc.scalar.activation(xh[0][:, k, :], bank(t, ("xT", j, k))[:, :], ACT.Copy).then_inc(xh_hi.sem, 1)

            def project_x(t, j, c):
                s, sj = before_block(t, j)
                if c == 0:
                    act.wait_ge(*conv_out.count(s, (sj + 1) * KI * (TAPS - 1)))
                    act.wait_ge(*xi_out.count(s, (sj + 1) * KI))
                    nc.scalar.activation(xi[:, :, 0:HALO], xi[:, :, BLK:BLK + HALO] if j else no_halo[:, :, :], ACT.Copy)\
                        .then_inc(halo.sem, 1)
                    act.wait_ge(*halo.count(t, j + 1))
                act.wait_ge(*full(t, ("xi", j, c)))
                nc.scalar.activation(xi[:, c, HALO:HALO + BLK], bank(t, ("xi", j, c))[:, :], ACT.Copy,
                                     scale=1.0 / SW).then_inc(xi_out.sem, 1)
                if c == 0:
                    act.wait_ge(*full(s, ("X", sj, NQ - 1)))
                    act.wait_ge(*sh_lo.count(s, (sj + 1) * KI))
                    act.wait_ge(*skip_out.count(s, (sj + 1) * KI))
                nc.scalar.activation(xs[:, c, :], bank(t, ("xi", j, c))[:, :], ACT.Identity, bias=conv_bias[:, c:c + 1],
                                     scale=last_tap[:, c:c + 1]).then_inc(tap_out.sem, 1)

            def gate_in(t, j, c):
                if j == 0:
                    s, sj = before_block(t, j)
                    for need in latest(full(t, ("z", j, c)), full(s, ("S", sj, NQ - 1, HP - 1))):
                        act.wait_ge(*need)
                    nc.scalar.activation(BT[:, c, :], bank(t, ("z", j, c))[:, :], ACT.Copy, scale=1.0 / SW)\
                        .then_inc(z_read.sem, 1)
                else:
                    act.wait_ge(*full(t, ("z", j, c)))
                    act.wait_ge(*g_late.count(t.ago(1), 3 * KI))
                    nc.scalar.activation(zs[:, c, j * BLK:(j + 1) * BLK], bank(t, ("z", j, c))[:, :], ACT.Silu,
                                         scale=1.0 / SW).then_inc(z_read.sem, 1)

            def gate_silu(t):
                act.wait_ge(*z_read.count(t, KI))
                act.wait_ge(*g_out.count(t.ago(1), KI))
                act.wait_ge(*g_late.count(t.ago(1), KI))
                for c in range(KI):
                    nc.scalar.activation(zs[:, c, 0:BLK], BT[:, c, :], ACT.Silu).then_inc(zs_out.sem, 1)

            def x_silu(t, j, c):
                act.wait_ge(*conv_out.count(t, (j * KI + c + 1) * (TAPS - 1)))
                nc.scalar.activation(xs[:, c, :], xs[:, c, :], ACT.Silu).then_inc(xs_out.sem, 1)

            def x_high(t, j, c):
                act.wait_ge(*xs_out.count(t, j * KI + c + 1))
                if c == 0:
                    s, sj = before_block(t, j)
                    act.wait_ge(*full(s, ("C", sj, KI - 1)))
                nc.scalar.activation(sh[0][:, c, :], xs[:, c, :], ACT.Copy, scale=SX).then_inc(sh_hi.sem, 1)

            def step_exp(t, j):
                act.wait_ge(*dt_step.count(t, j * DT + 2))
                nc.scalar.activation(exp_v[:, :, :], abs_v[:, :, :], ACT.Exp, scale=-1.0).then_inc(dt_act.sem, 1)

            def step_log(t, j):
                act.wait_ge(*dt_step.count(t, j * DT + 3))
                nc.scalar.activation(log_u[:, :, :], one_e[:, :, :], ACT.Ln).then_inc(dt_act.sem, 1)

            def skip_term(t, j):
                act.wait_ge(*xs_out.count(t, (j + 1) * KI))
                act.wait_ge(*full(t.ago(1), ("Wo", j, NQ // 2 - 1)))
                for c in range(KI):
                    nc.scalar.activation(yT[:, c, j * BLK:(j + 1) * BLK], xs[:, c, :], ACT.Copy,
                                         scale=skip[:, c:c + 1]).then_inc(skip_out.sem, 1)

            def project_c(t, j, c):
                s, sj = before_block(t, j)
                for need in latest(full(t, ("C", j, c)), full(s, ("YI", sj, NQ - 1))):
                    act.wait_ge(*need)
                nc.scalar.activation(CT[:, c, :], bank(t, ("C", j, c))[:, :], ACT.Copy, scale=1.0 / (SW * SX))\
                    .then_inc(C_out.sem, 1)

            def decay_exp(t, j):
                act.wait_ge(*full(t, ("sums", j)))
                s, sj = before_block(t, j)
                act.wait_ge(*st_scaled.count(s, (sj + 1) * NQ))
                act.wait_ge(*yk_part.count(s, (sj + 1) * NQ))
                nc.scalar.activation(decays[:, :, :, :].rearrange("p a q h -> p (a q h)"),
                                     bank(t, ("sums", j))[:, 0:3 * NQ * HEADS], ACT.Exp).then_inc(decays_out.sem, 1)

            def front(t, j, q):
                n = ch(j, q)
                s, sj, sq = two_before(t, n)
                for g in range(HP):
                    for need in latest(full(t, ("seg", j, q, g)), full(s, ("Y", sj, sq))):
                        act.wait_ge(*need)
                    nc.scalar.activation(mt[n % 2][:, g].rearrange("p c t -> p (c t)"),
                                         bank(t, ("seg", j, q, g))[:, :], ACT.Exp).then_inc(seg_exp.sem, 1)
                act.wait_ge(*full(t, ("Bt", j, q)))
                nc.scalar.activation(bt[n % 2][:, :], bank(t, ("Bt", j, q))[:, :], ACT.Copy).then_inc(bt_out.sem, 1)

            def carry(t, j, q):
                n = ch(j, q)
                s, sj, sq = two_before(t, n)
                act.wait_ge(*decays_out.count(t, j + 1))
                for need in latest(full(t, ("YI", j, q)), full(s, ("YT", sj, sq))):
                    act.wait_ge(*need)
                for h in range(HEADS):
                    last = nc.scalar.activation(yk[n % 2][:, h, :], bank(t, ("YI", j, q))[:, h * HD:(h + 1) * HD],
                                                ACT.Copy, scale=decays[:, 0, q, h:h + 1])
                last.then_inc(yk_part.sem, 1)

            def head_normalise(t, j, m):
                act.wait_ge(*gn_step.count(t, 8))
                for c in range(KI):
                    n = 2 * j + m
                    v = yT[:, c, n * BLK // 2:(n + 1) * BLK // 2]
                    nc.scalar.activation(v, v, ACT.Identity, bias=gn_shift[:, c:c + 1],
                                         scale=gn_scale[:, c:c + 1]).then_inc(yn_out.sem, 1)

            def middle_high(t, j):
                s, sj = before_block(t, j)
                for k in range(KD):
                    for need in latest(full(t, ("uT", j, k)), full(s, ("H", sj, KF - 1))):
                        act.wait_ge(*need)
                    nc.scalar.activation(uh[0][:, k, :], bank(t, ("uT", j, k))[:, :], ACT.Copy).then_inc(uh_hi.sem, 1)

            def hidden(t, j, f):
                act.wait_ge(*full(t, ("H", j, f)))
                act.wait_ge(*hh_lo.count(t, j * KF + f - 1))
                nc.scalar.activation(hf[f % 2][:, :], bank(t, ("H", j, f))[:, :], ACT.Gelu,
                                     bias=b1_col[:, f:f + 1], scale=alpha1[:, f:f + 1]).then_inc(hf_out.sem, 1)

            all_batches(act, {
                "silu_table": table(ACT.Silu), "gelu_table": table(ACT.Gelu), "xT": input_high, "xi": project_x,
                "z_in": gate_in, "z_silu": gate_silu, "silu": x_silu, "xs": x_high, "dt": step_exp,
                "log": step_log, "skip": skip_term, "C": project_c, "decays": decay_exp, "front": front, "carry": carry,
                "gate": head_normalise, "uT": middle_high, "H": hidden})

        @block.vector
        def _(dve):
            for s in (*ln_stats.values(), *ln_moments.values(), *ln_eps.values(), xn_made, xh_lo, conv_out, sh_lo, B_out,
                      dt_step, da_seen, seg_hi, mt_out, xdt_out, yk_out, st_out, yT_out, gn_st, gn_mo, gn_step, g_out,
                      mid_out, un_out, uh_lo, hh_hi, hh_lo, y2_scaled, y2_norm):
                s.prime(dve)

            def statistics(w, t, j, tile, ready):
                for i in range(NQ):
                    ready(i)
                    nc.vector.bn_stats(stats[w][:, i, :], tile(i)).then_inc(ln_stats[w].sem, 1)
                dve.wait_ge(*ln_stats[w].count(t, (j + 1) * NQ))
                dve.sem_inc(stats_seen, 1)
                for i in range(NQ):
                    nc.vector.bn_aggr(moments[w][:, i, :], stats[w][:, i, :]).then_inc(ln_moments[w].sem, 1)
                dve.wait_ge(*ln_moments[w].count(t, (j + 1) * NQ))
                dve.wait_ge(*ln_rstd[w].count(t, j))
                nc.vector.tensor_scalar(var_eps[w][:, :], moments[w][:, :, 1], EPS, None, ALU.add)\
                    .then_inc(ln_eps[w].sem, 1)

            def normal(w, t, j, dst, src, i):
                if i == 0:
                    dve.wait_ge(*ln_rstd[w].count(t, j + 1))
                return nc.vector.tensor_scalar(dst, src, moments[w][:, i, 0:1], rstd[w][:, i:i + 1],
                                               ALU.subtract, ALU.mult)

            def input_stats(t, j):
                statistics("in", t, j, lambda i: xt[j][:, i, :],
                           lambda i: dve.wait_ge(*x_in[j].count(t, 1)) if i == 0 else None)

            def input_norm(t, j):
                s, sj = before_block(t, j)
                dve.wait_ge(*full(s, ("xT", sj, KD - 1)))
                for i in range(NQ):
                    normal("in", t, j, xn[:, i, :], xt[j][:, i, :], i).then_inc(xn_made.sem, 1)

            def input_low(t, j, k):
                dve.wait_ge(*xh_hi.count(t, j * KD + k + 1))
                nc.vector.tensor_tensor(xh[1][:, k, :], bank(t, ("xT", j, k))[:, :], xh[0][:, k, :],
                                        ALU.subtract).then_inc(xh_lo.sem, 1)

            def convolve(t, j, c, first=0, end=TAPS - 1):
                if first == 0:
                    dve.wait_ge(*tap_out.count(t, j * KI + c + 1))
                    dve.wait_ge(*xi_out.count(t, j * KI + c + 1))
                for k in range(first, end):
                    if k:
                        dve.wait_ge(*conv_out.count(t, (j * KI + c) * (TAPS - 1) + k))
                    nc.vector.scalar_tensor_tensor(out=xs[:, c, :], in0=xi[:, c, k:k + BLK], scalar=taps[:, c, k:k + 1],
                                                   in1=xs[:, c, :], op0=ALU.mult, op1=ALU.add).then_inc(conv_out.sem, 1)

            def x_low(t, j, c):
                dve.wait_ge(*sh_hi.count(t, j * KI + c + 1))
                nc.vector.scalar_tensor_tensor(out=sh[1][:, c, :], in0=xs[:, c, :], scalar=SX, in1=sh[0][:, c, :],
                                               op0=ALU.mult, op1=ALU.subtract).then_inc(sh_lo.sem, 1)

            def step_in(t, j):
                dve.wait_ge(*full(t, ("dt", j)))
                nc.vector.scalar_tensor_tensor(
                    out=v_dt[:, :, :], in0=bank(t, ("dt", j))[:, 0:NQ * HEADS].rearrange("p (q h) -> p q h", q=NQ),
                    scalar=1.0 / (SW * SX), in1=bdt_row[:, None, :].to_broadcast([P, NQ, HEADS]), op0=ALU.mult,
                    op1=ALU.add).then_inc(dt_step.sem, 1)
                dve.wait_ge(*dt_step.count(t, j * DT + 1))
                nc.vector.scalar_tensor_tensor(out=abs_v[:, :, :], in0=v_dt[:, :, :], scalar=-1.0, in1=v_dt[:, :, :],
                                               op0=ALU.mult, op1=ALU.max).then_inc(dt_step.sem, 1)

            def step_mid(t, j):
                s = j * DT
                dve.wait_ge(*dt_act.count(t, j * 2 + 1))
                nc.vector.tensor_scalar(one_e[:, :, :], exp_v[:, :, :], 1.0, None, ALU.add).then_inc(dt_step.sem, 1)
                dve.wait_ge(*dt_step.count(t, s + 3))
                nc.vector.tensor_scalar(e_back[:, :, :], one_e[:, :, :], 1.0, None, ALU.subtract).then_inc(dt_step.sem, 1)
                dve.wait_ge(*dt_step.count(t, s + 4))
                nc.vector.tensor_tensor(e_rest[:, :, :], exp_v[:, :, :], e_back[:, :, :], ALU.subtract)\
                    .then_inc(dt_step.sem, 1)

            def step_out(t, j):
                s = j * DT
                dve.wait_ge(*dt_act.count(t, j * 2 + 2))
                nc.vector.scalar_tensor_tensor(out=dt_raw[:, :, :], in0=v_dt[:, :, :], scalar=0.0, in1=log_u[:, :, :],
                                               op0=ALU.max, op1=ALU.add).then_inc(dt_step.sem, 1)
                dve.wait_ge(*dt_step.count(t, s + 6))
                nc.vector.tensor_tensor(dt_t[:, :, :], dt_raw[:, :, :], e_rest[:, :, :], ALU.add).then_inc(dt_step.sem, 1)
                dve.wait_ge(*dt_step.count(t, s + 7))
                nc.vector.tensor_tensor(da_raw[:, :, :], dt_t[:, :, :], a_row[:, None, :].to_broadcast([P, NQ, HEADS]),
                                        ALU.mult).then_inc(da_seen.sem, 1)
                dve.wait_ge(*da_seen.count(t, j + 1))
                p, pj = before_block(t, j)
                dve.wait_ge(*full(p, ("sums", pj)))
                nc.vector.tensor_scalar(da[:, :, :], da_raw[:, :, :], DECAY_FLOOR, None, ALU.max).then_inc(dt_step.sem, 1)
                dve.wait_ge(*dt_step.count(t, s + 8))
                nc.vector.tensor_copy(da_hi[:, :, :], da[:, :, :]).then_inc(dt_step.sem, 1)
                dve.wait_ge(*dt_step.count(t, s + 9))
                nc.vector.tensor_tensor(da_lo[:, :, :], da[:, :, :], da_hi[:, :, :], ALU.subtract).then_inc(dt_step.sem, 1)

            def project_b(t, j, c):
                s, sj = before_block(t, j)
                for need in latest(full(t, ("B", j, c)), full(s, ("S", sj, NQ - 1, HP - 1))):
                    dve.wait_ge(*need)
                if j == 0:
                    dve.wait_ge(*zs_out.count(t, KI))
                nc.vector.tensor_scalar(BT[:, c, :], bank(t, ("B", j, c))[:, :], 1.0 / (SW * SX), None, ALU.mult)\
                    .then_inc(B_out.sem, 1)

            def segments(t, j, q):
                n = ch(j, q)
                if q == 0:
                    dve.wait_ge(*dt_step.count(t, (j + 1) * DT))
                s, sj, sq = two_before(t, n)
                dve.wait_ge(*full(s, ("seg", sj, sq, HP - 1)))
                nc.vector.tensor_tensor(seg[0][n % 2][:, :, :, :], every_head(upto_h), every_token(da_hi, q), ALU.mult)\
                    .then_inc(seg_hi.sem, 1)

            def front(t, j, q):
                n = ch(j, q)
                r = n % 2
                s, sj, sq = two_before(t, n)
                for need in latest(full(t, ("X", j, q)), full(s, ("Y", sj, sq))):
                    dve.wait_ge(*need)
                dve.wait_ge(*xdw_out.count(s, ch(sj, sq) + 1))
                nc.vector.tensor_tensor(xdt[r][:, :, :], heads(bank(t, ("X", j, q))[:, :]), per_head(dt_t[:, q, :]),
                                        ALU.mult).then_inc(xdt_out.sem, 1)
                for g in range(HP):
                    dve.wait_ge(*full(t, ("S", j, q, g)))
                    dve.wait_ge(*decay_masked.count(t, n * HP + g + 1))
                    v = mt[r][:, g].rearrange("p c t -> p (c t)")
                    nc.vector.tensor_tensor(v, bank(t, ("S", j, q, g))[:, :], v, ALU.mult).then_inc(mt_out.sem, 1)

            def carry(t, j, q):
                n = ch(j, q)
                dve.wait_ge(*full(t, ("St", j, q)))
                dve.wait_ge(*st_scaled.count(t, n + 1))
                for g in range(HP):
                    rows = slice(g * HD, (g + 1) * HD)
                    v = state[rows, :, g * HD:(g + 1) * HD]
                    nc.vector.tensor_tensor(
                        v, v, bank(t, ("St", j, q))[rows, :].rearrange("p (c n) -> p c n", c=KI)[:, :, g * HD:(g + 1) * HD],
                        ALU.add).then_inc(st_out.sem, 1)

            def back(t, j, q):
                n = ch(j, q)
                dve.wait_ge(*full(t, ("Y", j, q)))
                dve.wait_ge(*yk_part.count(t, n + 1))
                nc.vector.tensor_tensor(yk[n % 2][:, :, :], yk[n % 2][:, :, :], heads(bank(t, ("Y", j, q))[:, :]),
                                        ALU.add).then_inc(yk_out.sem, 1)

            def turn(t, j, q):
                n = ch(j, q)
                dve.wait_ge(*full(t, ("YT", j, q)))
                dve.wait_ge(*skip_out.count(t, (j + 1) * KI))
                v = yT[:, :, n * P:(n + 1) * P]
                nc.vector.tensor_tensor(v, bank(t, ("YT", j, q))[:, :].rearrange("p (c t) -> p c t", c=KI), v,
                                        ALU.add).then_inc(yT_out.sem, 1)

            def head_stats(t, j, half):
                n = 2 * j + half
                dve.wait_ge(*yT_out.count(t, (n + 1) * NQ // 2))
                for c in range(KI):
                    nc.vector.bn_stats(gn_stats[:, c, n, :], yT[:, c, n * BLK // 2:(n + 1) * BLK // 2])\
                        .then_inc(gn_st.sem, 1)

            def head_moments(t):
                dve.wait_ge(*gn_st.count(t, NJ * 2 * KI))
                dve.sem_inc(stats_seen, 1)
                for c in range(KI):
                    nc.vector.bn_aggr(gn_mom[:, c, :], gn_stats[:, c, :, :].rearrange("p j s -> p (j s)"))\
                        .then_inc(gn_mo.sem, 1)
                dve.wait_ge(*gn_mo.count(t, KI))
                nc.vector.tensor_tensor(gn_sq[:, :], gn_mom[:, :, 0], gn_mom[:, :, 0], ALU.mult).then_inc(gn_step.sem, 1)
                dve.wait_ge(*gn_step.count(t, 1))
                nc.vector.tensor_tensor(gn_mom[:, :, 1], gn_mom[:, :, 1], gn_sq[:, :], ALU.add).then_inc(gn_step.sem, 1)

            def head_variance(t):
                dve.wait_ge(*full(t, ("gn",)))
                nc.vector.tensor_copy(gn_head[:, :, :], bank(t, ("gn",))[:, 0:2 * KI].rearrange("p (c s) -> p c s", s=2))\
                    .then_inc(gn_step.sem, 1)
                dve.wait_ge(*gn_step.count(t, 3))
                nc.vector.tensor_tensor(gn_msq[:, :], gn_head[:, :, 0], gn_head[:, :, 0], ALU.mult)\
                    .then_inc(gn_step.sem, 1)
                dve.wait_ge(*gn_step.count(t, 4))
                nc.vector.scalar_tensor_tensor(out=gn_var[:, :], in0=gn_head[:, :, 1], scalar=EPS, in1=gn_msq[:, :],
                                               op0=ALU.add, op1=ALU.subtract).then_inc(gn_step.sem, 1)

            def head_fold(t):
                dve.wait_ge(*gn_rs.count(t, 1))
                nc.vector.tensor_tensor(gn_scale[:, :], gn_rstd[:, :], gnw[:, :], ALU.mult).then_inc(gn_step.sem, 1)
                dve.wait_ge(*gn_step.count(t, 6))
                nc.vector.tensor_tensor(gn_ms[:, :], gn_head[:, :, 0], gn_scale[:, :], ALU.mult).then_inc(gn_step.sem, 1)
                dve.wait_ge(*gn_step.count(t, 7))
                nc.vector.tensor_tensor(gn_shift[:, :], gnb[:, :], gn_ms[:, :], ALU.subtract).then_inc(gn_step.sem, 1)

            def gate(t, j, m):
                for c in range(0 if j or m else KI):
                    at = slice(0, BLK // 2)
                    dve.wait_ge(*yn_out.count(t, c + 1))
                    nc.vector.tensor_tensor(yT[:, c, at], yT[:, c, at], zs[:, c, at], ALU.mult).then_inc(g_out.sem, 1)

            def attention_tile(t, j, i):
                return bank(t, ("Wo", j, i // 2))[:, (i % 2) * D:(i % 2 + 1) * D]

            def middle_stats(t, j):
                statistics("mid", t, j, lambda i: attention_tile(t, j, i),
                           lambda i: dve.wait_ge(*full(t, ("Wo", j, i // 2))))

            def middle_norm(t, j):
                s, sj = before_block(t, j)
                dve.wait_ge(*full(s, ("uT", sj, KD - 1)))
                for i in range(NQ):
                    normal("mid", t, j, un[:, i, :], attention_tile(t, j, i), i).then_inc(mid_out.sem, 1)

            def ff_stats(t, j):
                statistics("ff", t, j, lambda i: u[j][:, i, :],
                           lambda i: dve.wait_ge(*u_out.count(t, j * NQ + i + 1)))

            def ff_norm(t, j):
                for i in range(NQ):
                    normal("ff", t, j, un[:, i, :], u[j][:, i, :], i).then_inc(un_out.sem, 1)

            def middle_low(t, j):
                for k in range(KD):
                    dve.wait_ge(*uh_hi.count(t, j * KD + k + 1))
                    nc.vector.tensor_tensor(uh[1][:, k, :], bank(t, ("uT", j, k))[:, :], uh[0][:, k, :],
                                            ALU.subtract).then_inc(uh_lo.sem, 1)

            def hidden_split(t, j, f):
                n = j * KF + f
                dve.wait_ge(*hf_out.count(t, n + 1))
                if f == 0:
                    s, sj = before_block(t, j)
                    dve.wait_ge(*full(s, ("O", sj, NQ // 2 - 1)))
                nc.vector.tensor_scalar(hh[0][:, f, :], hf[f % 2][:, :], SG, None, ALU.mult).then_inc(hh_hi.sem, 1)
                dve.wait_ge(*hh_hi.count(t, n + 1))
                nc.vector.scalar_tensor_tensor(out=hh[1][:, f, :], in0=hf[f % 2][:, :], scalar=SG, in1=hh[0][:, f, :],
                                               op0=ALU.mult, op1=ALU.subtract).then_inc(hh_lo.sem, 1)

            def ffn_out(t, j, m):
                if m == 0 and ffn_buffer(t, j) is y2:
                    s, sj = before_block(t, j)
                    dve.wait_ge(*o_out.count(s, (sj + 1) * NQ))
                dve.wait_ge(*full(t, ("O", j, m)))
                v = bank(t, ("O", j, m))[:, :].rearrange("p (i d) -> p i d", i=2)
                nc.vector.tensor_tensor(ffn_buffer(t, j)[:, 2 * m:2 * m + 2, :], v,
                                        alpha2_row[:, None, :].to_broadcast([P, 2, D]), ALU.mult)\
                    .then_inc(y2_scaled.sem, 1)

            def end_stats(t, j):
                statistics("end", t, j, lambda i: ffn_buffer(t, j)[:, i, :],
                           lambda i: dve.wait_ge(*y2_out.count(t, j * NQ // 2 + i // 2 + 1)))

            def end_norm(t, j):
                for i in range(NQ):
                    v = ffn_buffer(t, j)[:, i, :]
                    normal("end", t, j, v, v, i).then_inc(y2_norm.sem, 1)

            def back_and_ffn(t, j, m):
                back(t, j, m)
                ffn_out(t.ago(1), j, m)

            handlers = {
                "back+O": back_and_ffn, "in_stat": input_stats, "in_norm": input_norm, "xT": input_low,
                "conv": convolve, "xs": x_low,
                "dt": step_in, "log": step_mid, "decay": step_out, "B": project_b, "seg": segments, "front": front,
                "carry": carry, "back": back, "turn": turn, "head_stat": head_stats, "gn_sum": head_moments, "gn_root": head_variance,
                "gn_fold": head_fold, "gate": gate, "mid_stat": middle_stats, "mid_norm": middle_norm,
                "ff_stat": ff_stats, "ff_norm": ff_norm, "uT": middle_low, "H": hidden_split, "O": ffn_out,
                "end_stat": end_stats, "end_norm": end_norm}
            run(first_norm(), 0, handlers)

            halves = {"Wx": WxT, "Wz": WzT, "Wb": WbT, "Wc": WcT}
            for n, key in enumerate(lows[:-1]):
                w, k = halves[key[0]], key[1]
                dve.wait_ge(w_split, n + 1)
                nc.vector.scalar_tensor_tensor(out=w[1][:, k, :], in0=setup.bank(key)[:, :], scalar=SW,
                                               in1=w[0][:, k, :], op0=ALU.mult, op1=ALU.subtract)\
                    .then_inc(low_set, 1)
            dve.wait_ge(w_split, len(lows))
            nc.vector.scalar_tensor_tensor(out=WdtT[1][:, :, :], in0=setup.bank(("Wdt", 0))[:, 0:KI * HEADS]
                                           .rearrange("p (k h) -> p k h", k=KI), scalar=SW, in1=WdtT[0][:, :, :],
                                           op0=ALU.mult, op1=ALU.subtract).then_inc(low_set, 1)
            dve.wait_ge(arrived["w2"], 16)
            nc.vector.tensor_reduce(alpha2[:, :], w2_in, AX_X, ALU.add, apply_absolute_value=True).then_inc(dve_set, 1)
            dve.wait_ge(dve_set, 1)
            dve.wait_ge(masks_zero, 9)
            for k in range(KD):
                nc.vector.tensor_scalar(alpha2_wide[k], ones[:, :], alpha2[:, k:k + 1], 1.0 / (FF * SG),
                                        ALU.mult, ALU.mult).then_inc(wide_set, 1)
            dve.wait_ge(arrived["vectors"], 16 * VECTORS)
            nc.vector.tensor_scalar(last_tap[:, :], taps[:, :, TAPS - 1], 1.0 / SW, None, ALU.mult).then_inc(dve_set, 1)
            dve.wait_ge(*setup.full(None, ("alpha2", 0)))
            nc.vector.tensor_copy(alpha2_row[:, :], setup.bank(("alpha2", 0))[:, 0:D]).then_inc(alpha2_read, 1)
            dve.wait_ge(a_exp, 1)
            nc.vector.tensor_scalar(a_row[:, :], a_row[:, :], -1.0, None, ALU.mult).then_inc(dve_set, 1)
            dve.wait_ge(arrived["w1"], 16)
            nc.vector.tensor_reduce(alpha1[:, :], w1_in, AX_X, ALU.add, apply_absolute_value=True).then_inc(dve_set, 1)
            dve.wait_ge(dve_set, 4)
            nc.vector.tensor_scalar(alpha1[:, :], alpha1[:, :], 1.0 / D, None, ALU.mult).then_inc(dve_set, 1)
            dve.wait_ge(dve_set, DVE_SETUP)
            dve.wait_ge(alpha2_read, 1)
            dve.wait_ge(low_set, 2 * KD + 2 * KI + 1)
            all_batches(dve, handlers)

        @block.tensor
        def _(pe):
            pe.wait_ge(masks_made, 7)
            pe.wait_ge(masks_zero, 9)
            rings[2].prime(pe)

            def turn_weights(key, parts, id_=None):
                if setup.place[key][1]:
                    pe.wait_ge(*setup.empty(None, key))
                for n, part in enumerate(parts):
                    rows, w = part.shape[0], setup.bank(key)
                    mm = nc.tensor.transpose(w[:, n * rows:(n + 1) * rows], part, ident[0:rows, 0:rows])
                mm.then_inc(setup.full_sem(key), 1)

            def cols(k):
                return slice(k * P, (k + 1) * P)

            for name, w in (("Wx", Wx_in), ("Wz", Wz_in)):
                pe.wait_ge(arrived[name], 16)
                for k in range(KD):
                    turn_weights((name, k), [w[:, m, cols(k)] for m in range(KI)])
            for name, w in (("Wb", Wb_in), ("Wc", Wc_in)):
                pe.wait_ge(arrived[name], 16)
                for k in range(KI):
                    turn_weights((name, k), [w[:, m, cols(k)] for m in range(KI)])
            pe.wait_ge(arrived["Wdt"], 16)
            turn_weights(("Wdt", 0), [Wdt_in[:, cols(k)] for k in range(KI)])
            pe.wait_ge(arrived["Wout"], 16)
            for k in range(KI // 2):
                turn_weights(("Wout", k), [Wout_in[:, m, cols(2 * k + kk)] for kk in range(2) for m in range(KD)])
            pe.wait_ge(arrived["w2"], 16)
            for f in range(KF // 2):
                turn_weights(("w2", f), [w2_in[:, m, cols(2 * f + ff)] for ff in range(2) for m in range(KD)])
            pe.wait_ge(arrived["w1"], 16)
            for k in range(KD):
                for h in range(2):
                    turn_weights(("w1", k, h), [w1_in[:, 4 * h + m, cols(k)] for m in range(4)])
            pe.wait_ge(wide_set, KD)
            pe.wait_ge(*setup.empty(None, ("alpha2", 0)))
            for k in range(KD):
                mm = nc.tensor.matmul(setup.bank(("alpha2", 0))[:, cols(k)], alpha2_wide[k], ident[:, :],
                                      start=True, stop=True)
            mm.then_inc(setup.full_sem(("alpha2", 0)), 1)
            pe.wait_ge(alpha2_read, 1)
            pe.wait_ge(low_set, 2 * KD + 2 * KI + 1)
            pe.wait_ge(act_set, ACT_SETUP)
            for r in rings[:2]:
                r.prime(pe)

            def split_product(t, key, w, v, n, m, ready=None):
                pe.wait_ge(*empty(t, key))
                terms = [(k, i, h) for k in range(n) for i, h in ((0, 0), (1, 0), (0, 1))]
                for a, (k, i, h) in enumerate(terms):
                    if ready and i == h == 0:
                        pe.wait_ge(*ready(k))
                    mm = nc.tensor.matmul(bank(t, key)[:, :], w[i][:, k, cols(m)], v[h][:, k, :], start=(a == 0),
                                          stop=(a == len(terms) - 1))
                mm.then_inc(full_sem(t, key), 1)

            def turn_tokens(t, name, j, k, src, made):
                key = (name, j, k)
                pe.wait_ge(*empty(t, key))
                for i in range(NQ):
                    if k == 0:
                        pe.wait_ge(*made.count(t, j * NQ + i + 1))
                    mm = nc.tensor.transpose(bank(t, key)[:, cols(i)], src[:, i, cols(k)], ident[:, :])
                mm.then_inc(full_sem(t, key), 1)

            def turn_input(t, j, k):
                turn_tokens(t, "xT", j, k, xn, xn_made)

            def project_x(t, j, c):
                if c == 0:
                    pe.wait_ge(*xh_lo.count(t, (j + 1) * KD))
                split_product(t, ("xi", j, c), WxT, xh, KD, c)

            def project_z(t, j, c):
                split_product(t, ("z", j, c), WzT, xh, KD, c)

            def step_size(t, j):
                key = ("dt", j)
                for need in latest(empty(t, key), sh_lo.count(t, (j + 1) * KI)):
                    pe.wait_ge(*need)
                terms = [(k, i, h) for k in range(KI) for i, h in ((0, 0), (1, 0), (0, 1))]
                for q in range(NQ):
                    for a, (k, i, h) in enumerate(terms):
                        mm = nc.tensor.matmul(bank(t, key)[:, q * HEADS:(q + 1) * HEADS], sh[h][:, k, cols(q)],
                                              WdtT[i][:, k, :], start=(a == 0), stop=(a == len(terms) - 1))
                mm.then_inc(full_sem(t, key), 1)

            def project_b(t, j, c):
                first = (lambda k: sh_lo.count(t, j * KI + k + 1)) if c == 0 else None
                split_product(t, ("B", j, c), WbT, sh, KI, c, first)

            def project_c(t, j, c):
                split_product(t, ("C", j, c), WcT, sh, KI, c)

            def decay_sums(t, j):
                key = ("sums", j)
                pe.wait_ge(*dt_step.count(t, j * DT + 8))
                pe.wait_ge(*empty(t, key))
                for n, w in enumerate((upto, after, ones)):
                    mm = nc.tensor.matmul(bank(t, key)[:, n * NQ * HEADS:(n + 1) * NQ * HEADS], w[:, :],
                                          da[:, :, :].rearrange("p q h -> p (q h)"), start=True, stop=True)
                mm.then_inc(full_sem(t, key), 1)

            def front(t, j, q):
                n = ch(j, q)
                pe.wait_ge(*seg_hi.count(t, n + 1))
                pe.wait_ge(*seg_lo.count(t, n + 1))
                for g in range(HP):
                    key = ("seg", j, q, g)
                    pe.wait_ge(*empty(t, key))
                    for i in range(2):
                        mm = nc.tensor.matmul(bank(t, key)[:, :], after_h[:, :],
                                              seg[i][n % 2][:, g].rearrange("p c t -> p (c t)"),
                                              start=(i == 0), stop=(i == 1))
                    mm.then_inc(full_sem(t, key), 1)
                for name, src in (("X", xs), ("Bt", BT)):
                    key = (name, j, q)
                    for need in latest(empty(t, key), B_out.count(t, (j + 1) * KI), C_out.count(t, (j + 1) * KI)):
                        pe.wait_ge(*need)
                    for c in range(KI):
                        mm = nc.tensor.transpose(bank(t, key)[:, cols(c)], src[:, c, cols(q)], ident[:, :])
                    mm.then_inc(full_sem(t, key), 1)
                for g in range(HP):
                    key = ("S", j, q, g)
                    rows = slice(g * NS, (g + 1) * NS)
                    pe.wait_ge(*empty(t, key))
                    for c in range(KI):
                        mm = nc.tensor.matmul(bank(t, key)[:, cols(c)], BT[rows, c, cols(q)], CT[rows, c, cols(q)],
                                              start=True, stop=True)
                    mm.then_inc(full_sem(t, key), 1)

            def carry(t, j, q):
                n = ch(j, q)
                r = n % 2
                key = ("YI", j, q)
                for need in latest(empty(t, key), st_out.count(t, n * HP) if n else st_zero.count(t, 1)):
                    pe.wait_ge(*need)
                for c in range(KI):
                    mm = nc.tensor.matmul(bank(t, key)[:, cols(c)], CT[:, c, cols(q)], state[:, c, :],
                                          start=True, stop=True)
                mm.then_inc(full_sem(t, key), 1)
                key = ("St", j, q)
                for need in latest(empty(t, key), bt_out.count(t, n + 1), xdw_out.count(t, n + 1)):
                    pe.wait_ge(*need)
                for c in range(KI):
                    mm = nc.tensor.matmul(bank(t, key)[:, cols(c)], bt[r][:, cols(c)],
                                          xdw[r][:, HP * c:HP * c + HP, :].rearrange("p h n -> p (h n)"),
                                          start=True, stop=True)
                mm.then_inc(full_sem(t, key), 1)

            def back_products(t, j, q):
                n = ch(j, q)
                r = n % 2
                key = ("Y", j, q)
                for need in latest(empty(t, key), mt_out.count(t, (n + 1) * HP)):
                    pe.wait_ge(*need)
                for h in range(HEADS):
                    mm = nc.tensor.matmul(bank(t, key)[:, h * HD:(h + 1) * HD], mt[r][:, h % HP, h // HP, :],
                                          xdt[r][:, h, :], start=True, stop=True)
                    if h == HEADS - 1:
                        mm.then_inc(full_sem(t, key), 1)
                    yield

            def back(t, j, q):
                for _ in back_products(t, j, q):
                    pass

            def turn(t, j, q):
                n = ch(j, q)
                key = ("YT", j, q)
                for need in latest(empty(t, key), yk_out.count(t, n + 1)):
                    pe.wait_ge(*need)
                for c in range(KI):
                    mm = nc.tensor.transpose(bank(t, key)[:, cols(c)],
                                             yk[n % 2][:, HP * c:HP * c + HP, :].rearrange("p h n -> p (h n)"),
                                             ident[:, :])
                mm.then_inc(full_sem(t, key), 1)

            def head_means(t):
                pe.wait_ge(*gn_step.count(t, 2))
                pe.wait_ge(*empty(t, ("gn",)))
                nc.tensor.matmul(bank(t, ("gn",))[:, 0:2 * KI], head_mean[:, :],
                                 gn_mom[:, :, :].rearrange("p c s -> p (c s)"), start=True, stop=True)\
                    .then_inc(full_sem(t, ("gn",)), 1)

            def attention_out(t, j, m):
                key = ("Wo", j, m)
                gated = 2 * j + m
                pe.wait_ge(*(g_late.count(t, gated * KI) if gated else g_out.count(t, KI)))
                pe.wait_ge(*empty(t, key))
                for i in (2 * m, 2 * m + 1):
                    for c in range(KI):
                        mm = nc.tensor.matmul(bank(t, key)[:, (i % 2) * D:(i % 2 + 1) * D],
                                              yT[:, c, (j * NQ + i) * P:(j * NQ + i + 1) * P], WoutT[:, c, :],
                                              start=(c == 0), stop=(c == KI - 1))
                mm.then_inc(full_sem(t, key), 1)

            def turn_middle(t, j):
                for k in range(KD):
                    turn_tokens(t, "uT", j, k, un, un_out)

            def hidden(t, j, f):
                key = ("H", j, f)
                for need in latest(empty(t, key), uh_lo.count(t, (j + 1) * KD)):
                    pe.wait_ge(*need)
                terms = [(k, i) for k in range(KD) for i in range(2)]
                for a, (k, i) in enumerate(terms):
                    mm = nc.tensor.matmul(bank(t, key)[:, :], sign1T[:, k, cols(f)], uh[i][:, k, :],
                                          start=(a == 0), stop=(a == len(terms) - 1))
                mm.then_inc(full_sem(t, key), 1)

            def ffn_products(t, j, m):
                key = ("O", j, m)
                pe.wait_ge(*empty(t, key))
                for i in (2 * m, 2 * m + 1):
                    terms = [(f, p) for f in range(KF) for p in range(2)]
                    for a, (f, p) in enumerate(terms):
                        if i == p == 0:
                            pe.wait_ge(*hh_lo.count(t, j * KF + f + 1))
                        mm = nc.tensor.matmul(bank(t, key)[:, (i % 2) * D:(i % 2 + 1) * D], hh[p][:, f, cols(i)],
                                              sign2T[:, f, :], start=(a == 0), stop=(a == len(terms) - 1))
                        if (i, a) == (2 * m + 1, len(terms) - 1):
                            mm.then_inc(full_sem(t, key), 1)
                        yield

            def ffn_out(t, j, m):
                for _ in ffn_products(t, j, m):
                    pass

            def back_and_ffn(t, j, m):
                others = ffn_products(t.ago(1), j, m)
                for _ in back_products(t, j, m):
                    next(others)
                    next(others)
                for _ in others:
                    pass

            all_batches(pe, {
                "xT": turn_input, "xi": project_x, "z": project_z, "dt": step_size, "B": project_b, "C": project_c,
                "sums": decay_sums, "front": front, "carry": carry, "back": back, "turn": turn, "gn_mean": head_means,
                "Wo": attention_out, "uT": turn_middle, "H": hidden, "O": ffn_out,
                "back+O": back_and_ffn})


_INS = ["L0_attn_input_tensor", "L0_attn_Wx", "L0_attn_Wz", "L0_attn_conv_w", "L0_attn_conv_b", "L0_attn_Wb",
        "L0_attn_Wc", "L0_attn_Wdt", "L0_attn_b_dt", "L0_attn_log_a", "L0_attn_d_param", "L0_attn_gn_w",
        "L0_attn_gn_b", "L0_attn_Wout", "L0_ffn_w1", "L0_ffn_b1", "L0_ffn_w2", "L0_ffn_b2"]


def kernel(**inputs):
    import numpy as _np
    import concourse.bacc as _bacc
    from concourse import mybir as _mybir
    from concourse.bass_utils import run_bass_kernel_spmd as _run

    nc = _bacc.Bacc("TRN2", target_bir_lowering=False, num_devices=1)
    arrays, args = {}, []
    for name in _INS:
        a = _np.ascontiguousarray(inputs[name])
        arrays[f"in_{name}_dram"] = a
        args.append(nc.dram_tensor(f"in_{name}_dram", a.shape, _mybir.dt.from_np(a.dtype), kind="ExternalInput").ap())
    args.append(nc.dram_tensor("out_0_dram", (NB, T, D), F32, kind="ExternalOutput").ap())
    mamba_sandwich_kernel(nc, *args)
    r = _run(nc, [arrays], core_ids=[0])
    return r.results[0]["out_0_dram"]
```
